# Optimizing a Trainium2 kernel written in Bass

```python
import numpy as np
import jax
import jax.numpy as jnp

def _softmax(x, axis=-1):
    return jax.nn.softmax(x, axis=axis)

def _gelu(x):
    return jax.nn.gelu(x, approximate=True)

def _silu(x):
    return jax.nn.silu(x)

def _sigmoid(x):
    return jax.nn.sigmoid(x)

def _layernorm(x, axis=-1, eps=1e-05):
    m = jnp.mean(x, axis=axis, keepdims=True)
    v = jnp.var(x, axis=axis, keepdims=True)
    return (x - m) / jnp.sqrt(v + eps)

def _scatter_add(tgt, idx, src, axis=0):
    return tgt.at[idx].add(src)

def _segment_sum(src, seg, n):
    return jax.ops.segment_sum(src, seg, n)
kernel_name = 'mk_sandwich_d2_jaxref_r8_4a8329'

def setup_inputs(seed: int=0):
    np.random.seed(seed)
    _w = jnp.asarray

    def _L0_attn_setup():
        import jax, jax.numpy as jnp
        import numpy as np
        D_MODEL = 128
        N_HEADS = 16
        HEAD_DIM = D_MODEL // N_HEADS
        WINDOW = 128
        LOCAL_BLOCK = 32
        LATENT_TOKENS = 64
        LATENT_D = 32
        LATENT_HEADS = 4
        LATENT_HD = LATENT_D // LATENT_HEADS
        NEG = -1000000000.0

        def _local_attention(q, k, v):
            B, H, S, hd = q.shape
            bs = min(S, max(WINDOW, LOCAL_BLOCK))
            nb = S // bs
            w = WINDOW
            L = bs + w - 1
            k_pad = jnp.pad(k, ((0, 0), (0, 0), (w - 1, 0), (0, 0)))
            v_pad = jnp.pad(v, ((0, 0), (0, 0), (w - 1, 0), (0, 0)))
            starts = jnp.arange(nb) * bs
            idx = starts[:, None] + jnp.arange(L)[None, :]
            kb = k_pad[:, :, idx]
            vb = v_pad[:, :, idx]
            qb = q.reshape(B, H, nb, bs, hd)
            q_pos = starts[:, None] + jnp.arange(bs)[None, :]
            k_gpos = starts[:, None] + jnp.arange(L)[None, :] - (w - 1)
            dist = q_pos[:, :, None] - k_gpos[:, None, :]
            allowed = (dist > 0) & (dist <= w) & (k_gpos[:, None, :] >= 0)
            scale = 1.0 / np.sqrt(hd)
            scores = jnp.einsum('bhnqd,bhnkd->bhnqk', qb, kb) * scale
            scores = jnp.where(allowed, scores, NEG)
            attn = jax.nn.softmax(scores, axis=-1)
            attn = jnp.where(allowed.any(-1)[None, None, :, :, None], attn, 0.0)
            out = jnp.einsum('bhnqk,bhnkd->bhnqd', attn, vb)
            return out.reshape(B, H, S, hd)
        key = jax.random.key(seed)
        ks = jax.random.split(key, 14)
        B, S = (2, 512)
        s = 0.02
        f32 = jnp.float32
        return {'x': jax.random.normal(ks[0], (B, S, D_MODEL), f32), 'qkv_w': jax.random.normal(ks[1], (D_MODEL, 3 * D_MODEL), f32) * s, 'qkv_b': jnp.zeros((3 * D_MODEL,), f32), 'rq_w': jax.random.normal(ks[2], (D_MODEL, LATENT_D), f32) * s, 'rq_b': jnp.zeros((LATENT_D,), f32), 'rkv_w': jax.random.normal(ks[3], (D_MODEL, 2 * LATENT_D), f32) * s, 'rkv_b': jnp.zeros((2 * LATENT_D,), f32), 'rout_w': jax.random.normal(ks[4], (LATENT_D, D_MODEL), f32) * s, 'rout_b': jnp.zeros((D_MODEL,), f32), 'out_w': jax.random.normal(ks[5], (D_MODEL, D_MODEL), f32) * s, 'out_b': jnp.zeros((D_MODEL,), f32), 'gl_w': jax.random.normal(ks[6], (HEAD_DIM, 1), f32) * s, 'gr_w': jax.random.normal(ks[7], (HEAD_DIM, 1), f32) * s}
    _L0_attn_in = _L0_attn_setup()

    def _L0_ffn_setup():
        import jax, jax.numpy as jnp
        import numpy as np
        EPS = 1e-05

        def _quantize(W):
            gamma = jnp.mean(jnp.abs(W))
            return jnp.clip(jnp.round(W / (gamma + EPS)), -1.0, 1.0)
        key = jax.random.key(seed)
        k_x, k_w1, k_b1, k_w2, k_b2 = jax.random.split(key, 5)
        n_embd = 128
        d_ff = 4 * n_embd
        B, S = (4, 512)
        bound1 = 1.0 / np.sqrt(n_embd)
        bound2 = 1.0 / np.sqrt(d_ff)
        x = jax.random.normal(k_x, (B, S, n_embd), dtype=jnp.float32)
        W1 = jax.random.uniform(k_w1, (d_ff, n_embd), jnp.float32, -bound1, bound1)
        b1 = jax.random.uniform(k_b1, (d_ff,), jnp.float32, -bound1, bound1)
        W2 = jax.random.uniform(k_w2, (n_embd, d_ff), jnp.float32, -bound2, bound2)
        b2 = jax.random.uniform(k_b2, (n_embd,), jnp.float32, -bound2, bound2)
        return {'x': x, 'W1': W1, 'b1': b1, 'W2': W2, 'b2': b2}
    _L0_ffn_in = _L0_ffn_setup()

    def _L1_attn_setup():
        import jax, jax.numpy as jnp
        import numpy as np
        N_HEADS = 16
        HEAD_DIM = 64
        ROPE_THETA = 10000.0
        EPS = 1e-06

        def _rmsnorm(x, w):
            rms = jnp.sqrt(jnp.mean(jnp.square(x), axis=-1, keepdims=True) + EPS)
            return x / rms * w

        def _rope(x, cos, sin):
            x1, x2 = jnp.split(x, 2, axis=-1)
            return jnp.concatenate([x1 * cos - x2 * sin, x1 * sin + x2 * cos], axis=-1)
        key = jax.random.key(seed)
        ks = jax.random.split(key, 3)
        B, T, C = (2, 256, 128)
        x = jax.random.normal(ks[0], (B, T, C), dtype=jnp.float32)
        wqkv = jax.random.normal(ks[1], (3 * N_HEADS * HEAD_DIM, C), dtype=jnp.float32) * C ** (-0.5)
        wo = jax.random.normal(ks[2], (C, N_HEADS * HEAD_DIM), dtype=jnp.float32) * (N_HEADS * HEAD_DIM) ** (-0.5)
        q_norm_w = jnp.ones((HEAD_DIM,), dtype=jnp.float32)
        k_norm_w = jnp.ones((HEAD_DIM,), dtype=jnp.float32)
        return {'x': x, 'wqkv': wqkv, 'wo': wo, 'q_norm_w': q_norm_w, 'k_norm_w': k_norm_w}
    _L1_attn_in = _L1_attn_setup()

    def _L1_ffn_setup():
        import jax, jax.numpy as jnp
        import numpy as np
        H = 128
        F = 512
        E = 8
        TOP_K = 2
        B, S = (1, 256)
        key = jax.random.key(seed)
        k0, k1, k2, k3 = jax.random.split(key, 4)
        hidden_states = jax.random.normal(k0, (B, S, H), dtype=jnp.float32)
        gate_w = jax.random.normal(k1, (E, H), dtype=jnp.float32) * 0.02
        gate_up_w = jax.random.normal(k2, (E, 2 * F, H), dtype=jnp.float32) * 0.02
        down_w = jax.random.normal(k3, (E, H, F), dtype=jnp.float32) * 0.02
        return {'hidden_states': hidden_states, 'gate_w': gate_w, 'gate_up_w': gate_up_w, 'down_w': down_w}
    _L1_ffn_in = _L1_ffn_setup()
    _d = {'L0_attn_x': _L0_attn_in['x'], 'L0_attn_qkv_w': _L0_attn_in['qkv_w'], 'L0_attn_qkv_b': _L0_attn_in['qkv_b'], 'L0_attn_rq_w': _L0_attn_in['rq_w'], 'L0_attn_rq_b': _L0_attn_in['rq_b'], 'L0_attn_rkv_w': _L0_attn_in['rkv_w'], 'L0_attn_rkv_b': _L0_attn_in['rkv_b'], 'L0_attn_rout_w': _L0_attn_in['rout_w'], 'L0_attn_rout_b': _L0_attn_in['rout_b'], 'L0_attn_out_w': _L0_attn_in['out_w'], 'L0_attn_out_b': _L0_attn_in['out_b'], 'L0_attn_gl_w': _L0_attn_in['gl_w'], 'L0_attn_gr_w': _L0_attn_in['gr_w'], 'L0_ffn_W1': _L0_ffn_in['W1'], 'L0_ffn_b1': _L0_ffn_in['b1'], 'L0_ffn_W2': _L0_ffn_in['W2'], 'L0_ffn_b2': _L0_ffn_in['b2'], 'L1_attn_wqkv': _L1_attn_in['wqkv'], 'L1_attn_wo': _L1_attn_in['wo'], 'L1_attn_q_norm_w': _L1_attn_in['q_norm_w'], 'L1_attn_k_norm_w': _L1_attn_in['k_norm_w'], 'L1_ffn_gate_w': _L1_ffn_in['gate_w'], 'L1_ffn_gate_up_w': _L1_ffn_in['gate_up_w'], 'L1_ffn_down_w': _L1_ffn_in['down_w']}
    _x0 = _d['L0_attn_x']
    _d['L0_attn_x'] = jax.random.normal(jax.random.fold_in(jax.random.key(seed), 1), (8, 512, 128), dtype=_x0.dtype)
    del _x0
    return _d

def reference(L0_attn_x, L0_attn_qkv_w, L0_attn_qkv_b, L0_attn_rq_w, L0_attn_rq_b, L0_attn_rkv_w, L0_attn_rkv_b, L0_attn_rout_w, L0_attn_rout_b, L0_attn_out_w, L0_attn_out_b, L0_attn_gl_w, L0_attn_gr_w, L0_ffn_W1, L0_ffn_b1, L0_ffn_W2, L0_ffn_b2, L1_attn_wqkv, L1_attn_wo, L1_attn_q_norm_w, L1_attn_k_norm_w, L1_ffn_gate_w, L1_ffn_gate_up_w, L1_ffn_down_w):

    def _L0_attn_ref(x, qkv_w, qkv_b, rq_w, rq_b, rkv_w, rkv_b, rout_w, rout_b, out_w, out_b, gl_w, gr_w):
        import jax, jax.numpy as jnp
        import numpy as np
        D_MODEL = 128
        N_HEADS = 16
        HEAD_DIM = D_MODEL // N_HEADS
        WINDOW = 128
        LOCAL_BLOCK = 32
        LATENT_TOKENS = 64
        LATENT_D = 32
        LATENT_HEADS = 4
        LATENT_HD = LATENT_D // LATENT_HEADS
        NEG = -1000000000.0

        def _local_attention(q, k, v):
            B, H, S, hd = q.shape
            bs = min(S, max(WINDOW, LOCAL_BLOCK))
            nb = S // bs
            w = WINDOW
            L = bs + w - 1
            k_pad = jnp.pad(k, ((0, 0), (0, 0), (w - 1, 0), (0, 0)))
            v_pad = jnp.pad(v, ((0, 0), (0, 0), (w - 1, 0), (0, 0)))
            starts = jnp.arange(nb) * bs
            idx = starts[:, None] + jnp.arange(L)[None, :]
            kb = k_pad[:, :, idx]
            vb = v_pad[:, :, idx]
            qb = q.reshape(B, H, nb, bs, hd)
            q_pos = starts[:, None] + jnp.arange(bs)[None, :]
            k_gpos = starts[:, None] + jnp.arange(L)[None, :] - (w - 1)
            dist = q_pos[:, :, None] - k_gpos[:, None, :]
            allowed = (dist > 0) & (dist <= w) & (k_gpos[:, None, :] >= 0)
            scale = 1.0 / np.sqrt(hd)
            scores = jnp.einsum('bhnqd,bhnkd->bhnqk', qb, kb) * scale
            scores = jnp.where(allowed, scores, NEG)
            attn = jax.nn.softmax(scores, axis=-1)
            attn = jnp.where(allowed.any(-1)[None, None, :, :, None], attn, 0.0)
            out = jnp.einsum('bhnqk,bhnkd->bhnqd', attn, vb)
            return out.reshape(B, H, S, hd)
        B, S, D = x.shape
        qkv = x @ qkv_w + qkv_b
        q, k, v = jnp.split(qkv, 3, axis=-1)

        def heads(t):
            return t.reshape(B, S, N_HEADS, HEAD_DIM).transpose(0, 2, 1, 3)
        local = _local_attention(heads(q), heads(k), heads(v))
        chunk = -(-S // min(LATENT_TOKENS, S))
        nlat = S // chunk
        pooled = x.reshape(B, nlat, chunk, D).mean(axis=2)
        chunk_ids = jnp.arange(S) // chunk
        rq = (x @ rq_w + rq_b).reshape(B, S, LATENT_HEADS, LATENT_HD).transpose(0, 2, 1, 3)
        rkv = pooled @ rkv_w + rkv_b
        rk, rv = jnp.split(rkv, 2, axis=-1)
        rk = rk.reshape(B, nlat, LATENT_HEADS, LATENT_HD).transpose(0, 2, 1, 3)
        rv = rv.reshape(B, nlat, LATENT_HEADS, LATENT_HD).transpose(0, 2, 1, 3)
        lscale = 1.0 / np.sqrt(LATENT_HD)
        lscores = jnp.einsum('bhsd,bhld->bhsl', rq, rk) * lscale
        lat_allowed = jnp.arange(nlat)[None, :] < chunk_ids[:, None]
        lscores = jnp.where(lat_allowed[None, None], lscores, NEG)
        lattn = jax.nn.softmax(lscores, axis=-1)
        lattn = jnp.where(lat_allowed.any(-1)[None, None, :, None], lattn, 0.0)
        lat_out = jnp.einsum('bhsl,bhld->bhsd', lattn, rv)
        lat_out = lat_out.transpose(0, 2, 1, 3).reshape(B, S, LATENT_D)
        remote = lat_out @ rout_w + rout_b
        remote_h = remote.reshape(B, S, N_HEADS, HEAD_DIM).transpose(0, 2, 1, 3)
        gate = jax.nn.sigmoid(local @ gl_w + remote_h @ gr_w)
        mixed = gate * local + (1.0 - gate) * remote_h
        mixed = mixed.transpose(0, 2, 1, 3).reshape(B, S, D)
        return mixed @ out_w + out_b

    def _L0_ffn_ref(x, W1, b1, W2, b2):
        import jax, jax.numpy as jnp
        import numpy as np
        EPS = 1e-05

        def _quantize(W):
            gamma = jnp.mean(jnp.abs(W))
            return jnp.clip(jnp.round(W / (gamma + EPS)), -1.0, 1.0)
        Wq1 = _quantize(W1)
        Wq2 = _quantize(W2)
        h = jax.nn.relu(jnp.einsum('bsd,fd->bsf', x, Wq1) + b1)
        out = jnp.einsum('bsf,df->bsd', h, Wq2) + b2
        return out

    def _L1_attn_ref(x, wqkv, wo, q_norm_w, k_norm_w):
        import jax, jax.numpy as jnp
        import numpy as np
        N_HEADS = 16
        HEAD_DIM = 64
        ROPE_THETA = 10000.0
        EPS = 1e-06

        def _rmsnorm(x, w):
            rms = jnp.sqrt(jnp.mean(jnp.square(x), axis=-1, keepdims=True) + EPS)
            return x / rms * w

        def _rope(x, cos, sin):
            x1, x2 = jnp.split(x, 2, axis=-1)
            return jnp.concatenate([x1 * cos - x2 * sin, x1 * sin + x2 * cos], axis=-1)
        B, T, C = x.shape
        H, D = (N_HEADS, HEAD_DIM)
        qkv = jnp.einsum('btc,oc->bto', x, wqkv)
        q, k, v = jnp.split(qkv, 3, axis=-1)

        def to_heads(t):
            return t.reshape(B, T, H, D).transpose(0, 2, 1, 3)
        q, k, v = (to_heads(q), to_heads(k), to_heads(v))
        q = _rmsnorm(q, q_norm_w)
        k = _rmsnorm(k, k_norm_w)
        inv_freq = 1.0 / ROPE_THETA ** (jnp.arange(0, D, 2, dtype=jnp.float32) / D)
        freqs = jnp.arange(T, dtype=jnp.float32)[:, None] * inv_freq
        cos, sin = (jnp.cos(freqs), jnp.sin(freqs))
        q = _rope(q, cos, sin)
        k = _rope(k, cos, sin)
        scale = D ** (-0.5)
        attn = jnp.einsum('bhtd,bhsd->bhts', q, k) * scale
        causal = jnp.tril(jnp.ones((T, T), dtype=bool))
        attn = jnp.where(causal, attn, -jnp.inf)
        attn = jax.nn.softmax(attn.astype(jnp.float32), axis=-1).astype(q.dtype)
        out = jnp.einsum('bhts,bhsd->bhtd', attn, v)
        out = out.transpose(0, 2, 1, 3).reshape(B, T, H * D)
        return jnp.einsum('bte,ce->btc', out, wo)

    def _L1_ffn_ref(hidden_states, gate_w, gate_up_w, down_w):
        import jax, jax.numpy as jnp
        import numpy as np
        H = 128
        F = 512
        E = 8
        TOP_K = 2
        B, S = (1, 256)
        b, s, h = hidden_states.shape
        x = hidden_states.reshape(-1, h)
        router_logits = x @ gate_w.T
        probs = jax.nn.softmax(router_logits.astype(jnp.float32), axis=-1)
        topw, sel = jax.lax.top_k(probs, TOP_K)
        topw = topw / jnp.sum(topw, axis=-1, keepdims=True)
        topw = topw.astype(x.dtype)
        combine = jnp.sum(jax.nn.one_hot(sel, E, dtype=x.dtype) * topw[..., None], axis=1)
        gu = jnp.einsum('th,efh->etf', x, gate_up_w)
        gate, up = (gu[..., :F], gu[..., F:])
        hact = up * jax.nn.gelu(gate, approximate=False)
        expert_out = jnp.einsum('etf,ehf->eth', hact, down_w)
        out = jnp.einsum('eth,te->th', expert_out, combine)
        return out.reshape(b, s, h)
    x = L0_attn_x
    x = x + _layernorm(_L0_attn_ref(_layernorm(x, axis=-1), L0_attn_qkv_w, L0_attn_qkv_b, L0_attn_rq_w, L0_attn_rq_b, L0_attn_rkv_w, L0_attn_rkv_b, L0_attn_rout_w, L0_attn_rout_b, L0_attn_out_w, L0_attn_out_b, L0_attn_gl_w, L0_attn_gr_w), axis=-1)
    x = x + _layernorm(_L0_ffn_ref(_layernorm(x, axis=-1), L0_ffn_W1, L0_ffn_b1, L0_ffn_W2, L0_ffn_b2), axis=-1)
    x = x + _layernorm(_L1_attn_ref(_layernorm(x, axis=-1), L1_attn_wqkv, L1_attn_wo, L1_attn_q_norm_w, L1_attn_k_norm_w), axis=-1)
    x = x + _layernorm(_L1_ffn_ref(_layernorm(x, axis=-1), L1_ffn_gate_w, L1_ffn_gate_up_w, L1_ffn_down_w), axis=-1)
    return x

_drawn_inputs = setup_inputs


def setup_inputs(seed=0):
    import zlib

    import numpy as np

    out = dict(_drawn_inputs(seed))
    spreads = {'L0_attn_qkv_b': (0.0, 0.1),
     'L0_attn_rq_b': (0.0, 2.0),
     'L0_attn_rkv_b': (0.0, 0.1),
     'L0_attn_rout_b': (0.0, 0.1),
     'L0_attn_out_b': (0.0, 0.1),
     'L1_attn_q_norm_w': (1.0, 0.2),
     'L1_attn_k_norm_w': (1.0, 0.2)}
    factors = {'L0_attn_rq_w': 23.228,
     'L0_attn_rkv_w': 3.164,
     'L0_attn_gl_w': 7.77,
     'L0_attn_gr_w': 17.383,
     'L0_ffn_b2': 43.372}
    for name, (base, spread) in spreads.items():
        noise = np.random.default_rng([zlib.crc32(name.encode()), seed]).standard_normal(out[name].shape)
        drawn = base * np.exp(spread * noise) if base else spread * noise
        out[name] = jnp.asarray(drawn.astype(out[name].dtype))
    for name, factor in factors.items():
        out[name] = (out[name] * factor).astype(out[name].dtype)
    return out
```

```python
from contextlib import ExitStack

import numpy as np

import concourse.bass as bass
from concourse import mybir

F32 = mybir.dt.float32
BF16 = mybir.dt.bfloat16
ALU = mybir.AluOpType
ACT = mybir.ActivationFunctionType
X = mybir.AxisListType.X

P = 128
NSEQ, S, D = 8, 512, 128
T = S // P
H = 16
HD0, HD1 = D // H, 64
G0 = 4
NLAT, LH, LHD, LD = 64, 4, 8, 32
CHUNK = S // NLAT
FF = 512
NE, FE = 8, 512
FC = FF // P
NEG = -1.0e9
NEG1 = -1.0e30
CLAMP = 1.0e8
LN_EPS, RMS_EPS, Q_EPS = 1e-5, 1e-6, 1e-5
SCALE0 = float(1.0 / np.sqrt(HD0))
SCALEL = float(1.0 / np.sqrt(LHD))
SCALE1 = float(HD1 ** -0.5)
W0 = (256, 256, 256, 128)
OFF0 = (0, 256, 512, 768)
OFF1 = (0, 512, 1024, 896)
VEC_STEPS = 81


class Sig:

    def __init__(self, ctx, nc, name, per_turn):
        self.sem = ctx.enter_context(nc.semaphore(name))
        self.n = per_turn

    def at(self, b, k):
        return b * self.n + k


def build(nc, ins, out):
    ctx = ExitStack()
    with ctx:
        def sb(name, shape, dt=F32):
            return ctx.enter_context(nc.sbuf_tensor(name, shape, dt))

        def sig(name, n):
            return Sig(ctx, nc, name, n)

        loaded = {}
        order = ["ident_f", "wqrep", "wkrep", "bqk", "wv", "bv", "rq_w", "rq_b", "rkv_w", "rk_b", "rv_b",
                 "small", "lmask", "rout_w", "rout_b", "out_w", "out_b", "glr",
                 "w1", "b1", "w2", "b2", "cs", "qkn", "wqkv1", "wo1", "gate_w", "tri", "gu", "down", "masks", "sel"]
        for name in order[:-2]:
            loaded[name] = sb("c_" + name, list(ins[name].shape))
        c = loaded
        ident_f = c["ident_f"][:, :]
        ident_b_t = sb("ident_b", [P, P], BF16)
        masks_b = sb("masks_b", [P, 768], BF16)
        sel_b = sb("sel_b", [H, H, P], BF16)
        ident_b = ident_b_t[:, :]
        hmask = c["small"][:, 0:4]
        lhmask = c["small"][0:LD, 4:8]
        bdmask = c["small"][:, 8:8 + 2 * LD].rearrange("p (c d) -> p c d", c=2)
        mhalf = c["small"][:, 72:88]
        onesf = sb("onesf", [P, P])
        mask_rows, mask_cols = masks_b[:, 0:256], masks_b[:, 256:512]
        cmask_rows, cmask_cols = masks_b[:, 512:640], masks_b[:, 640:768]

        x_in = sb("x_in", [P, T, D])
        x = sb("x", [P, T, D])
        x_out = sb("x_out", [P, T, D])
        xn = sb("xn", [P, T, D])
        xnT = sb("xnT", [P, S])
        y = sb("y", [P, T, D])
        bst = sb("bst", [P, T, 6])
        mv = sb("mv", [P, T, 2])
        ve = sb("ve", [P, T])
        rstd = sb("rstd", [P, T])

        region = sb("region", [P, 12 * 1024])
        region2 = sb("region2", [P, 7 * 1024])
        rb = region[:, :].bitcast(BF16)
        c["masks"], c["sel"] = region[:, 1024:1792], region[0:H, 2048:4096]
        km = rb[:, 0:H * S].rearrange("p (h s) -> p h s", h=H)
        pT0 = region[:, 4096:4096 + 3 * 896].rearrange("p (r s) -> p r s", r=3)
        lp = region[:, 7168:7168 + 1024].rearrange("p (t h l) -> p t h l", t=T, h=LH)
        lpT = region[:, 8192:8192 + 1024].rearrange("p (c s) -> p c s", c=2)
        qs = region[:, 9216:9216 + 1024].bitcast(BF16).rearrange("p (g s) -> p g s", g=H // G0)
        ks = region[:, 10240:10240 + 1024].bitcast(BF16).rearrange("p (g s) -> p g s", g=H // G0)
        mixT = region[:, 11264:11264 + 512]
        remote = region2[:, 0:512].rearrange("p (t d) -> p t d", t=T)
        local = region2[:, 512:1024].rearrange("p (t d) -> p t d", t=T)
        gtmp = region2[:, 1024:1536].rearrange("p (t d) -> p t d", t=T)
        rqT = region2[0:LD, 1536:2048]
        latT = region2[0:LD, 2048:2560]
        rkM = region2[0:LD, 2560:2816].rearrange("p (h l) -> p h l", h=LH)
        pooled2 = region2[:, 2816:2944].rearrange("p (r l) -> p r l", r=2)
        psumf = region2[:, 2944:3008]
        rvb = region2[:, 3008:3040]
        rvM = region2[:, 3072:3136].rearrange("p (c d) -> p c d", c=2)
        mx0 = sb("mx0", [P, T, H])
        nm = sb("nm", [P, T, H])
        nmT = sb("nmT", [H, S], BF16)
        lmx = sb("lmx", [P, T, LH])
        lsum = sb("lsum", [P, T, LH])
        v0 = sb("v0", [P, T, H, HD0 + 1])
        rden = sb("rden", [P, T, H])
        gz = sb("gz", [P, T, H])
        gz2 = sb("gz2", [P, T, H])
        h0T = region[:, 0:4 * S].rearrange("p (f s) -> p f s", f=FC)
        qst = rb[:, 0:8192].rearrange("p (h s) -> p h s", h=H)
        kst = rb[:, 8192:16384].rearrange("p (h s) -> p h s", h=H)
        kst2 = rb[:, 16384:24576].rearrange("p (h s) -> p h s", h=H)
        rot1 = region2[:, 0:2048].rearrange("p (r h d) -> p r h d", r=2, h=H)
        rot2 = region2[:, 2048:4096].rearrange("p (r h d) -> p r h d", r=2, h=H)
        sq = region2[:, 4096:5120].rearrange("p (h d) -> p h d", h=H)
        hilo = region2[:, 5120:7168].bitcast(BF16).rearrange("p (r h k d) -> p r h k d", r=2, h=H, k=2)
        ao = region2[:, 0:4096].rearrange("p (t n) -> p t n", t=T)
        aoT = region[:, 0:4096].rearrange("p (r k s) -> p r k s", r=4, k=8)
        p1 = region2[:, 4096:6656].rearrange("p (r s) -> p r s", r=2)
        v1 = sb("v1", [P, T, H, HD1 + 1])
        ve1 = sb("ve1", [P, 2, H])
        rinv = sb("rinv", [P, 2, H])
        r1 = sb("r1", [P, 2, T])
        csq = sb("csq", [P, 2, 2, T, HD1])
        hT = region[:, 0:4096].rearrange("p (r f s) -> p r f s", r=2, f=FC)
        gact = region[:, 4096:4096 + 1536].rearrange("p (r s) -> p r s", r=3)
        acc = y
        pr = sb("pr", [P, T, NE])
        comb = sb("comb", [P, T, NE])
        cmp1 = region[:, 5632:5888].rearrange("p (t a e) -> p t a e", t=T, a=NE)
        cmp2 = region[:, 5888:6144].rearrange("p (t a e) -> p t a e", t=T, a=NE)
        r4 = sb("r4", [P, T])
        thr = sb("thr", [P, 4])
        gam = sb("gam", [P, 2])
        qtmp = region[:, 0:512]
        qtmp2 = region[:, 512:1024]

        ps = ctx.enter_context(nc.psum_tensor("ps", [P, 8, 512], F32))

        def bank(i, n=1):
            return ps[:, i, :] if n == 1 else ps[:, i:i + n, :].rearrange("p b n -> p (b n)")

        wload = {k: sig("w_" + k, 16) for k in ("qkv", "lat", "gate", "mlp", "attn1", "exp")}
        group_of = {}
        for k in order:
            group_of[k] = ("qkv" if k in ("ident_f", "wqrep", "wkrep", "bqk", "wv", "bv") else
                           "lat" if k in ("rq_w", "rq_b", "rkv_w", "rk_b", "rv_b", "small", "lmask", "rout_w",
                                          "rout_b") else
                           "gate" if k in ("out_w", "out_b", "glr", "masks", "sel") else
                           "mlp" if k in ("w1", "b1", "w2", "b2") else
                           "attn1" if k in ("cs", "qkn", "wqkv1", "wo1") else "exp")
        gcount = {g: 16 * sum(1 for k in order if group_of[k] == g) for g in wload}

        set_ones = sig("set_ones", 0)
        abs_sums = sig("abs_sums", 0)
        gam_ready = sig("gam_ready", 0)
        quant_done = sig("quant_done", 0)
        setup_step = sig("setup_step", 0)

        x_loaded = sig("x_loaded", 16)
        x_taken = sig("x_taken", 1)
        x_final = sig("x_final", 1)
        x_out_free = sig("x_out_free", 16)
        vec = sig("vec_step", VEC_STEPS)
        var_ready = sig("var_ready", 16)
        rstd_ready = sig("rstd_ready", 16)
        xn_ready = sig("xn_ready", 4)
        xnT_ps = sig("xnT_ps", 4)
        xnT_ready = sig("xnT_ready", 4)

        q0_ps = sig("q0_ps", 8)
        q0_hi = sig("q0_hi", 8)
        q0_lo = sig("q0_lo", 8)
        km_ready = sig("km_ready", H)
        va_ps = sig("va_ps", 1)
        va_ready = sig("va_ready", 1)
        rq_ps = sig("rq_ps", 1)
        rq_ready = sig("rq_ready", 1)
        pool_ready = sig("pool_ready", 1)
        rkv_ps = sig("rkv_ps", 1)
        rkv_ready = sig("rkv_ready", 1)
        ls_ps = sig("ls_ps", 1)
        ls_free = sig("ls_free", 1)
        ls_ready = sig("ls_ready", 1)
        lexp = sig("lexp", 1)
        lp_ready = sig("lp_ready", 1)
        lpT_ps = sig("lpT_ps", 1)
        lpT_ready = sig("lpT_ready", 1)
        lat_ps = sig("lat_ps", 1)
        lat_ready = sig("lat_ready", 1)
        rem_ps = sig("rem_ps", 1)
        rem_ready = sig("rem_ready", 1)
        sr0 = sig("sr0", 16)
        mx0_done = sig("mx0_done", 16)
        nm_ready = sig("nm_ready", 2)
        nmT_ps = sig("nmT_ps", 2)
        nmT_ready = sig("nmT_ready", 2)
        sc0 = sig("sc0", H)
        e0 = sig("e0", H)
        pv0 = sig("pv0", H)
        local_done = sig("local_done", 1)
        gz_ready = sig("gz_ready", 1)
        gexp = sig("gexp", 1)
        mix_ready = sig("mix_ready", 1)
        mixT_ps = sig("mixT_ps", 1)
        mixT_ready = sig("mixT_ready", 1)
        y_ps = sig("y_ps", 3)
        y_read = sig("y_read", 3)
        h_ps = sig("h_ps", FC)
        h_ready = sig("h_ready", FC)

        pj = sig("pj", 12)
        b_sq = sig("b_sq", 8)
        b_rot = sig("b_rot", 8)
        b_v = sig("b_v", 4)
        b_sum = sig("b_sum", 8)
        b_qn = sig("b_qn", 8)
        b_hi = sig("b_hi", 8)
        b_lo = sig("b_lo", 8)
        b_tr = sig("b_tr", 8)
        b_ev = sig("b_ev", 8)
        k_swapped = sig("k_swapped", 32)
        sr1 = sig("sr1", H)
        mx1_done = sig("mx1_done", H)
        sc1 = sig("sc1", H)
        e1 = sig("e1", H)
        pv1 = sig("pv1", H)
        ao_done = sig("ao_done", H)
        aoT_ps = sig("aoT_ps", T)
        aoT_ready = sig("aoT_ready", T)

        lg_ps = sig("lg_ps", 1)
        lg_max = sig("lg_max", 1)
        lg_exp = sig("lg_exp", 1)
        gu_ps = sig("gu_ps", NE * FC)
        gelu_done = sig("gelu_done", NE * FC)
        hact = sig("hact", NE * FC)
        dn_ps = sig("dn_ps", NE)
        dn_read = sig("dn_read", NE)

        block = ctx.enter_context(nc.Block())
        x_dram = ins["x"].rearrange("(b t p) d -> b p t d", t=T, p=P)
        out_dram = out.rearrange("(b t p) d -> b p t d", t=T, p=P)

        @block.sync
        def _(sp):
            sp.dma_start(x_in[:, :, :], x_dram[0]).then_inc(x_loaded.sem, 16)
            for name in order:
                dst = c[name]
                full = tuple(slice(None) for _ in dst.shape)
                sp.dma_start(dst[full], ins[name]).then_inc(wload[group_of[name]].sem, 16)
            with sp.Fori(0, NSEQ) as b:
                sp.wait_ge(b_ev.sem, b_ev.at(b, 8))
                sp.dma_start(kst2[64:128, :, :], kst[0:64, :, :]).then_inc(k_swapped.sem, 16)
                sp.dma_start(kst2[0:64, :, :], kst[64:128, :, :]).then_inc(k_swapped.sem, 16)
                sp.wait_ge(x_taken.sem, x_taken.at(b, 1))
                sp.dma_start(x_in[:, :, :], x_dram[(b + 1) % NSEQ]).then_inc(x_loaded.sem, 16)
                sp.wait_ge(x_final.sem, x_final.at(b, 1))
                sp.dma_start(out_dram[b], x_out[:, :, :]).then_inc(x_out_free.sem, 16)
            sp.wait_ge(x_loaded.sem, 16 * (NSEQ + 1))
            sp.wait_ge(x_out_free.sem, 16 * NSEQ + 1)

        @block.gpsimd
        def _(pool):
            with pool.Fori(0, NSEQ) as b:
                done = [0]

                def power(dst, src):
                    done[0] += 1
                    pool.wait_ge(var_ready.sem, var_ready.at(b, done[0]))
                    pool.tensor_tensor(dst, src, mhalf[:, 0:src.shape[1]], ALU.pow).then_inc(rstd_ready.sem, 1)

                for n in range(5):
                    power(rstd[:, :], ve[:, :])
                for i in range(8):
                    pool.wait_ge(b_rot.sem, b_rot.at(b, i + 1))
                    pool.tensor_tensor(rot1[:, i % 2], rot1[:, i % 2], rot2[:, i % 2], ALU.add)\
                        .then_inc(b_sum.sem, 1)
                    power(rinv[:, i % 2, :], ve1[:, i % 2, :])
                for n in range(3):
                    power(rstd[:, :], ve[:, :])

        @block.scalar
        def _(act):
            act.wait_ge(wload["mlp"].sem, gcount["mlp"])
            act.activation(qtmp, c["w1"][:, :], ACT.Abs, accum_out=gam[:, 0:1]).then_inc(abs_sums.sem, 1)
            act.activation(qtmp2, c["w2"][:, :], ACT.Abs, accum_out=gam[:, 1:2]).then_inc(abs_sums.sem, 1)
            with act.Fori(0, NSEQ) as b:
                def copy_xnT(n):
                    act.wait_ge(xnT_ps.sem, xnT_ps.at(b, n + 1))
                    act.copy(xnT[:, :], bank(0)).then_inc(xnT_ready.sem, 1)

                copy_xnT(0)
                for g in range(H // G0):
                    for kk, dst in enumerate((qs, ks)):
                        i = 2 * g + kk
                        act.wait_ge(q0_ps.sem, q0_ps.at(b, i + 1))
                        act.activation(dst[:, g, :], bank(i), ACT.Identity, bias=c["bqk"][:, i:i + 1])\
                            .then_inc(q0_hi.sem, 1)
                act.wait_ge(rq_ps.sem, rq_ps.at(b, 1))
                act.activation(rqT, ps[0:LD, 1, :], ACT.Identity, bias=c["rq_b"][:, 0:1])\
                    .then_inc(rq_ready.sem, 1)
                act.wait_ge(ls_ready.sem, ls_ready.at(b, 1))
                act.activation(lp, lp, ACT.Exp, scale=SCALEL).then_inc(lexp.sem, 1)
                act.wait_ge(lpT_ps.sem, lpT_ps.at(b, 1))
                act.copy(lpT.rearrange("p c s -> p (c s)"), bank(4, 2)).then_inc(lpT_ready.sem, 1)
                act.wait_ge(lat_ps.sem, lat_ps.at(b, 1))
                act.copy(latT, ps[0:LD, 6, :]).then_inc(lat_ready.sem, 1)
                act.wait_ge(nmT_ps.sem, nmT_ps.at(b, 1))
                act.copy(nmT[:, :], ps[0:H, 6, :]).then_inc(nmT_ready.sem, 1)
                for h in range(H):
                    act.wait_ge(sc0.sem, sc0.at(b, h + 1))
                    if h >= 3:
                        act.wait_ge(pv0.sem, pv0.at(b, h - 2))
                    act.activation(pT0[:, h % 3, :], bank(2 * (h % 3), 2)[:, 0:896], ACT.Exp, scale=SCALE0)\
                        .then_inc(e0.sem, 1)
                act.wait_ge(gz_ready.sem, gz_ready.at(b, 1))
                act.activation(gz2[:, :, :], gz[:, :, :], ACT.Exp, scale=-1.0).then_inc(gexp.sem, 1)
                act.wait_ge(mixT_ps.sem, mixT_ps.at(b, 1))
                act.copy(mixT, bank(0)).then_inc(mixT_ready.sem, 1)

                copy_xnT(1)
                for f in range(FC):
                    act.wait_ge(h_ps.sem, h_ps.at(b, f + 1))
                    act.activation(h0T[:, f, :], bank(1 + f), ACT.Relu, bias=c["b1"][:, f:f + 1])\
                        .then_inc(h_ready.sem, 1)

                copy_xnT(2)

                def hi(i):
                    act.wait_ge(b_qn.sem, b_qn.at(b, i + 1))
                    act.copy(hilo[:, i % 2, :, 0, :], rot1[:, i % 2]).then_inc(b_hi.sem, 1)

                def evac(i):
                    act.wait_ge(b_tr.sem, b_tr.at(b, i + 1))
                    dst = (qst, kst)[i % 2]
                    t = i // 2
                    act.copy(dst[:, :, t * P:(t + 1) * P],
                             bank(6, 2).bitcast(BF16).rearrange("p (h s) -> p h s", h=H)).then_inc(b_ev.sem, 1)

                for i in range(8):
                    t = i // 2
                    u = 3 * t + i % 2
                    act.wait_ge(pj.sem, pj.at(b, u + 1))
                    if i >= 1:
                        act.wait_ge(var_ready.sem, var_ready.at(b, 5 + i))
                    act.activation(sq.rearrange("p h d -> p (h d)"), bank(2 * (u % 3), 2), ACT.Square)\
                        .then_inc(b_sq.sem, 1)
                    if i % 2:
                        act.wait_ge(pj.sem, pj.at(b, 3 * t + 3))
                        act.copy(v1[:, t, :, 0:HD1],
                                 bank(4, 2).rearrange("p (h d) -> p h d", h=H)).then_inc(b_v.sem, 1)
                    if i >= 1:
                        hi(i - 1)
                    if i >= 2:
                        evac(i - 2)
                hi(7)
                evac(6)
                evac(7)
                act.wait_ge(nmT_ps.sem, nmT_ps.at(b, 2))
                act.copy(nmT[:, :], ps[0:H, 6, :]).then_inc(nmT_ready.sem, 1)
                for h in range(H):
                    act.wait_ge(sc1.sem, sc1.at(b, h + 1))
                    if h >= 2:
                        act.wait_ge(pv1.sem, pv1.at(b, h - 1))
                    act.activation(p1[:, h % 2, :], bank(3 * (h % 2), 3)[:, 0:1280], ACT.Exp, scale=SCALE1)\
                        .then_inc(e1.sem, 1)
                for t in range(T):
                    act.wait_ge(aoT_ps.sem, aoT_ps.at(b, t + 1))
                    act.copy(aoT[:, t].rearrange("p k s -> p (k s)"), bank(2 * (t % 2), 2))\
                        .then_inc(aoT_ready.sem, 1)

                copy_xnT(3)
                act.wait_ge(lg_max.sem, lg_max.at(b, 1))
                act.activation(pr[:, :, :], pr[:, :, :], ACT.Exp).then_inc(lg_exp.sem, 1)
                for n in range(NE * FC):
                    act.wait_ge(gu_ps.sem, gu_ps.at(b, n + 1))
                    if n >= 3:
                        act.wait_ge(hact.sem, hact.at(b, n - 2))
                    act.activation(gact[:, n % 3, :], bank(2 * (n % 3)), ACT.Gelu).then_inc(gelu_done.sem, 1)

        @block.tensor
        def _(pe):
            pe.wait_ge(abs_sums.sem, 2)
            pe.wait_ge(set_ones.sem, 1)
            pe.matmul(ps[:, 7, 0:2], onesf[:, :], gam[:, :], start=True, stop=True).then_inc(gam_ready.sem, 1)
            for g in wload:
                pe.wait_ge(wload[g].sem, gcount[g])
            pe.wait_ge(quant_done.sem, 2)
            with pe.Fori(0, NSEQ) as b:
                def mm(o, l, r, start=True, stop=True):
                    return pe.matmul(o, l, r, start=start, stop=stop, skip_group_check=True)

                def turn_rows(n):
                    pe.wait_ge(xn_ready.sem, xn_ready.at(b, n + 1))
                    for t in range(T):
                        last = pe.transpose(ps[:, 0, t * P:(t + 1) * P], xn[:, t, :], ident_f)
                    last.then_inc(xnT_ps.sem, 1)
                    pe.wait_ge(xnT_ready.sem, xnT_ready.at(b, n + 1))

                turn_rows(0)
                for g in range(H // G0):
                    for kk, w in enumerate(("wqrep", "wkrep")):
                        mm(bank(2 * g + kk), c[w][:, g * P:(g + 1) * P], xnT[:, :]).then_inc(q0_ps.sem, 1)
                pe.wait_ge(q0_lo.sem, q0_lo.at(b, 1))
                for t in range(T):
                    last = mm(ps[:, 0, t * P:(t + 1) * P], xnT[:, t * P:(t + 1) * P], c["wv"][:, :])
                last.then_inc(va_ps.sem, 1)
                pe.wait_ge(q0_lo.sem, q0_lo.at(b, 2))
                mm(ps[0:LD, 1, :], c["rq_w"][:, :], xnT[:, :]).then_inc(rq_ps.sem, 1)
                pe.wait_ge(q0_lo.sem, q0_lo.at(b, 3))
                pe.wait_ge(pool_ready.sem, pool_ready.at(b, 1))
                mm(ps[0:LD, 2, 0:NLAT], c["rkv_w"][:, 0:LD], pooled2[:, 0, :])
                mm(ps[:, 2, NLAT:NLAT + LD], pooled2.rearrange("p r l -> p (r l)"), c["rkv_w"][:, LD:2 * LD])\
                    .then_inc(rkv_ps.sem, 1)
                pe.wait_ge(rq_ready.sem, rq_ready.at(b, 1))
                pe.wait_ge(rkv_ready.sem, rkv_ready.at(b, 1))
                pe.wait_ge(q0_lo.sem, q0_lo.at(b, 8))
                for t in range(T):
                    last = mm(bank(6, 2)[:, t * 256:(t + 1) * 256], rqT[:, t * P:(t + 1) * P],
                              rkM.rearrange("p h l -> p (h l)"))
                last.then_inc(ls_ps.sem, 1)

                pe.wait_ge(va_ready.sem, va_ready.at(b, 1))

                def rows0(i):
                    g, qb = divmod(i, T)
                    s = i % 3
                    if i >= 3:
                        pe.wait_ge(mx0_done.sem, mx0_done.at(b, i - 2))
                    if i % T == 0:
                        pe.wait_ge(km_ready.sem, km_ready.at(b, G0 * (g + 1)))
                    w, k0 = (P, 0) if qb == 0 else (2 * P, (qb - 1) * P)
                    for half in range(1 if qb == 0 else 2):
                        nh = 512 // w
                        o = ps[:, 2 * s + half, :]
                        mm(o.rearrange("p (h n) -> p h n", h=nh), ident_b,
                           mask_rows[:, 256 - w:256].unsqueeze(1).to_broadcast([P, nh, w]), stop=False)
                        for hh in range(nh):
                            h = G0 * g + nh * half + hh
                            last = mm(o[:, hh * w:(hh + 1) * w], qs[:, g, qb * P:(qb + 1) * P],
                                      km[:, h, k0:k0 + w], start=False)
                    last.then_inc(sr0.sem, 1)

                for i in range(6):
                    rows0(i)
                pe.wait_ge(mx0_done.sem, mx0_done.at(b, 6))
                pe.wait_ge(lp_ready.sem, lp_ready.at(b, 1))
                for cc in range(2):
                    for t in range(T):
                        last = pe.transpose(ps[:, 4 + cc, t * P:(t + 1) * P],
                                            lp[:, t, 2 * cc:2 * cc + 2, :].rearrange("p h l -> p (h l)"), ident_f)
                last.then_inc(lpT_ps.sem, 1)
                pe.wait_ge(lpT_ready.sem, lpT_ready.at(b, 1))
                for cc in range(2):
                    last = mm(ps[0:LD, 6, :], rvM[:, cc, :], lpT[:, cc, :], start=cc == 0, stop=cc == 1)
                last.then_inc(lat_ps.sem, 1)
                pe.wait_ge(lat_ready.sem, lat_ready.at(b, 1))
                for t in range(T):
                    last = mm(ps[:, 7, t * P:(t + 1) * P], latT[:, t * P:(t + 1) * P], c["rout_w"][:, :])
                last.then_inc(rem_ps.sem, 1)
                for i in range(6, 16):
                    rows0(i)

                def turn_max(n):
                    pe.wait_ge(nm_ready.sem, nm_ready.at(b, n + 1))
                    for t in range(T):
                        last = pe.transpose(ps[0:H, 6, t * P:(t + 1) * P], nm[:, t, :], ident_f)
                    last.then_inc(nmT_ps.sem, 1)
                    pe.wait_ge(nmT_ready.sem, nmT_ready.at(b, n + 1))

                turn_max(0)
                pe.wait_ge(rem_ready.sem, rem_ready.at(b, 1))

                def cols0(h):
                    g, s = h // G0, 2 * (h % 3)
                    if h >= 3:
                        pe.wait_ge(e0.sem, e0.at(b, h - 2))
                    o = ps[:, s, :]
                    mm(o.rearrange("p (j n) -> p j n", j=2), ident_b,
                       mask_cols.unsqueeze(1).to_broadcast([P, 2, 256]), stop=False)
                    o = ps[:, s + 1, :]
                    mm(o[:, 0:256], ident_b, mask_cols, stop=False)
                    mm(o[:, 256:384], ident_b, mask_cols[:, 0:P], start=False, stop=False)
                    for j in range(T):
                        o = ps[:, s + j // 2, (j % 2) * 256:(j % 2) * 256 + W0[j]]
                        q = slice(j * P, j * P + W0[j])
                        mm(o, sel_b[:, h, :], nmT[:, q], start=False, stop=False)
                        last = mm(o, km[:, h, j * P:(j + 1) * P], qs[:, g, q], start=False)
                    last.then_inc(sc0.sem, 1)

                def values0(h):
                    pe.wait_ge(e0.sem, e0.at(b, h + 1))
                    for qb in range(T):
                        o = ps[:, 6 + qb // 2, (qb % 2) * 144 + 9 * h:(qb % 2) * 144 + 9 * h + 9]
                        if qb:
                            a = OFF0[qb - 1] + P
                            mm(o, pT0[:, h % 3, a:a + P], v0[:, qb - 1, h, :], stop=False)
                        a = OFF0[qb]
                        last = mm(o, pT0[:, h % 3, a:a + P], v0[:, qb, h, :], start=qb == 0)
                    last.then_inc(pv0.sem, 1)

                for h in range(H):
                    cols0(h)
                    if h >= 1:
                        values0(h - 1)
                values0(H - 1)
                pe.wait_ge(mix_ready.sem, mix_ready.at(b, 1))
                for t in range(T):
                    last = pe.transpose(ps[:, 0, t * P:(t + 1) * P], xn[:, t, :], ident_f)
                last.then_inc(mixT_ps.sem, 1)
                pe.wait_ge(mixT_ready.sem, mixT_ready.at(b, 1))
                for t in range(T):
                    last = mm(ps[:, 1, t * P:(t + 1) * P], mixT[:, t * P:(t + 1) * P], c["out_w"][:, :])
                last.then_inc(y_ps.sem, 1)

                turn_rows(1)
                for f in range(FC):
                    mm(bank(1 + f), c["w1"][:, f * P:(f + 1) * P], xnT[:, :]).then_inc(h_ps.sem, 1)
                pe.wait_ge(h_ready.sem, h_ready.at(b, FC))
                for t in range(T):
                    for f in range(FC):
                        last = mm(ps[:, 5, t * P:(t + 1) * P], h0T[:, f, t * P:(t + 1) * P],
                                  c["w2"][:, f * P:(f + 1) * P], start=f == 0, stop=f == FC - 1)
                last.then_inc(y_ps.sem, 1)

                turn_rows(2)

                def turn_parts(i):
                    pe.wait_ge(b_lo.sem, b_lo.at(b, i + 1))
                    if i >= 1:
                        pe.wait_ge(b_ev.sem, b_ev.at(b, i))
                    dst = bank(6, 2).bitcast(BF16)
                    for h in range(H):
                        last = pe.transpose(dst[:, h * P:(h + 1) * P],
                                            hilo[:, i % 2, h].rearrange("p k d -> p (k d)"), ident_b)
                    last.then_inc(b_tr.sem, 1)

                for u in range(12):
                    t, kind = divmod(u, 3)
                    i = 2 * t + kind
                    if u >= 3:
                        if kind == 2:
                            pe.wait_ge(b_v.sem, b_v.at(b, t))
                        else:
                            pe.wait_ge(b_sq.sem, b_sq.at(b, i - 1))
                            pe.wait_ge(b_rot.sem, b_rot.at(b, i - 1))
                    for n in range(2):
                        col = kind * 1024 + n * 512
                        last = mm(bank(2 * (u % 3) + n), xnT[:, t * P:(t + 1) * P], c["wqkv1"][:, col:col + 512])
                    last.then_inc(pj.sem, 1)
                    if kind < 2 and i >= 2:
                        turn_parts(i - 2)
                turn_parts(6)
                turn_parts(7)
                pe.wait_ge(b_ev.sem, b_ev.at(b, 8))
                pe.wait_ge(b_rot.sem, b_rot.at(b, 8))
                pe.wait_ge(b_v.sem, b_v.at(b, 4))

                def rows1(h):
                    s = 3 * (h % 2)
                    if h >= 2:
                        pe.wait_ge(mx1_done.sem, mx1_done.at(b, h - 1))
                    for qb in (3, 2, 1, 0):
                        w = (qb + 1) * P
                        o = ps[:, s + (0, 1, 2, 2)[3 - qb], (256 if qb == 0 else 0):(256 if qb == 0 else 0) + w]
                        mm(o, qst[0:64, h, qb * P:(qb + 1) * P], kst[0:64, h, 0:w], stop=False)
                        last = mm(o[:, w - P:w], ident_b, cmask_rows, start=False)
                    last.then_inc(sr1.sem, 1)

                for h in range(H):
                    rows1(h)
                turn_max(1)
                pe.wait_ge(k_swapped.sem, k_swapped.at(b, 32))

                def cols1(h):
                    s = 3 * (h % 2)
                    if h >= 2:
                        pe.wait_ge(e1.sem, e1.at(b, h - 1))
                    for j in range(T):
                        w = S - j * P
                        o = bank(s, 3)[:, OFF1[j]:OFF1[j] + w]
                        k = slice(j * P, (j + 1) * P)
                        q = slice(j * P, S)
                        mm(o, kst[:, h, k], qst[:, h, q], stop=False)
                        mm(o, kst2[:, h, k], qst[:, h, q], start=False, stop=False)
                        mm(o, sel_b[:, h, :], nmT[:, q], start=False, stop=False)
                        last = mm(o[:, 0:P], ident_b, cmask_cols, start=False)
                    last.then_inc(sc1.sem, 1)

                def values1(h):
                    pe.wait_ge(e1.sem, e1.at(b, h + 1))
                    if h >= 2:
                        pe.wait_ge(ao_done.sem, ao_done.at(b, h - 1))
                    for qb in range(T):
                        o = ps[:, 6 + h % 2, 65 * qb:65 * qb + 65]
                        for j in range(qb + 1):
                            a = OFF1[j] + (qb - j) * P
                            last = mm(o, p1[:, h % 2, a:a + P], v1[:, j, h, :], start=j == 0, stop=j == qb)
                    last.then_inc(pv1.sem, 1)

                for h in range(H):
                    cols1(h)
                    if h >= 1:
                        values1(h - 1)
                values1(H - 1)
                pe.wait_ge(ao_done.sem, ao_done.at(b, H))
                for t in range(T + 1):
                    if t < T:
                        if t >= 2:
                            pe.wait_ge(aoT_ready.sem, aoT_ready.at(b, t - 1))
                        for k in range(8):
                            last = pe.transpose(bank(2 * (t % 2), 2)[:, k * P:(k + 1) * P],
                                                ao[:, t, k * P:(k + 1) * P], ident_f)
                        last.then_inc(aoT_ps.sem, 1)
                    if t >= 1:
                        pe.wait_ge(aoT_ready.sem, aoT_ready.at(b, t))
                        for k in range(8):
                            last = mm(ps[:, 4, (t - 1) * P:t * P], aoT[:, t - 1, k, :],
                                      c["wo1"][:, k * P:(k + 1) * P], start=k == 0, stop=k == 7)
                last.then_inc(y_ps.sem, 1)

                turn_rows(3)
                for t in range(T):
                    last = mm(ps[:, 7, t * NE:(t + 1) * NE], xnT[:, t * P:(t + 1) * P], c["gate_w"][:, :])
                last.then_inc(lg_ps.sem, 1)

                def down(e):
                    pe.wait_ge(hact.sem, hact.at(b, FC * (e + 1)))
                    if e >= 2:
                        pe.wait_ge(dn_read.sem, dn_read.at(b, e - 1))
                    if e == 1:
                        pe.wait_ge(lg_max.sem, lg_max.at(b, 1))
                    for t in range(T):
                        for f in range(FC):
                            last = mm(ps[:, 6 + e % 2, t * P:(t + 1) * P], hT[:, e % 2, f, t * P:(t + 1) * P],
                                      c["down"][:, e, f, :], start=f == 0, stop=f == FC - 1)
                    last.then_inc(dn_ps.sem, 1)

                for e in range(NE):
                    for f in range(FC):
                        n = e * FC + f
                        if n >= 3:
                            pe.wait_ge(hact.sem, hact.at(b, n - 2))
                        mm(bank(2 * (n % 3)), c["gu"][:, e, f * P:(f + 1) * P], xnT[:, :])
                        mm(bank(2 * (n % 3) + 1), c["gu"][:, e, FE + f * P:FE + (f + 1) * P], xnT[:, :])\
                            .then_inc(gu_ps.sem, 1)
                    if e >= 1:
                        down(e - 1)
                down(NE - 1)

        @block.vector
        def _(dve):
            n = [0]

            def s_step(i):
                n[0] += 1
                i.then_inc(setup_step.sem, 1)
                dve.wait_ge(setup_step.sem, n[0])

            dve.memset(x_out[:, 0, 0:1], 0.0).then_inc(x_out_free.sem, 1)
            dve.memset(v0[:, :, :, HD0:HD0 + 1], 1.0)
            dve.memset(v1[:, :, :, HD1:HD1 + 1], 1.0)
            dve.memset(onesf[:, :], 1.0).then_inc(set_ones.sem, 1)
            dve.wait_ge(gam_ready.sem, 1)
            s_step(dve.tensor_scalar(thr[:, 2:4], ps[:, 7, 0:2], 1.0 / (D * FF), Q_EPS, ALU.mult, ALU.add))
            s_step(dve.tensor_scalar(thr[:, 0:2], thr[:, 2:4], 0.5, None, ALU.mult))
            s_step(dve.tensor_scalar(thr[:, 2:4], thr[:, 0:2], -1.0, None, ALU.mult))
            for k, w in enumerate(("w1", "w2")):
                s_step(dve.tensor_scalar(qtmp, c[w][:, :], thr[:, 2 + k:3 + k], None, ALU.is_lt))
                s_step(dve.scalar_tensor_tensor(out=c[w][:, :], in0=c[w][:, :], scalar=thr[:, k:k + 1],
                                                in1=qtmp, op0=ALU.is_gt, op1=ALU.subtract))
            dve.wait_ge(wload["attn1"].sem, gcount["attn1"])
            half = HD1 // 2
            for k in range(2):
                w = c["qkn"][:, k, :]
                for t in range(T):
                    dve.tensor_tensor(csq[:, k, 0, t, :], c["cs"][:, 0, t, :], w, ALU.mult)
                    dve.tensor_tensor(csq[:, k, 1, t, 0:half], c["cs"][:, 1, t, 0:half], w[:, half:HD1], ALU.mult)
                    last = dve.tensor_tensor(csq[:, k, 1, t, half:HD1], c["cs"][:, 1, t, half:HD1],
                                             w[:, 0:half], ALU.mult)
            last.then_inc(quant_done.sem, 1)
            for g in ("qkv", "lat", "gate", "exp"):
                dve.wait_ge(wload[g].sem, gcount[g])
            dve.tensor_copy(ident_b_t[:, :], ident_f)
            dve.tensor_copy(masks_b[:, :], c["masks"])
            dve.tensor_copy(sel_b[:, :, :].rearrange("r h p -> r (h p)"), c["sel"]).then_inc(quant_done.sem, 1)
            dve.wait_ge(quant_done.sem, 2)

            with dve.Fori(0, NSEQ) as b:
                step_no, norm_no = [0], [0]

                def step(i):
                    step_no[0] += 1
                    i.then_inc(vec.sem, 1)
                    dve.wait_ge(vec.sem, vec.at(b, step_no[0]))

                def stats(src):
                    for t in range(T):
                        last = dve.bn_stats(bst[:, t, :], src[:, t, :])
                    step(last)
                    dve.memset(ve[:, :], 0.0)
                    for t in range(T):
                        last = dve.bn_aggr(mv[:, t, :], bst[:, t, :])
                    step(last)
                    dve.tensor_scalar(ve[:, :], mv[:, :, 1], LN_EPS, None, ALU.add).then_inc(var_ready.sem, 1)
                    norm_no[0] += 1
                    dve.wait_ge(rstd_ready.sem, rstd_ready.at(b, norm_no[0]))

                def norm_in():
                    stats(x)
                    for t in range(T):
                        last = dve.tensor_scalar(xn[:, t, :], x[:, t, :], mv[:, t, 0:1], rstd[:, t:t + 1],
                                                 ALU.subtract, ALU.mult)
                    last.then_inc(xn_ready.sem, 1)

                def norm_out(dst):
                    stats(y)
                    for t in range(T):
                        last = dve.tensor_scalar(xn[:, t, :], y[:, t, :], mv[:, t, 0:1], rstd[:, t:t + 1],
                                                 ALU.subtract, ALU.mult)
                    step(last)
                    return dve.tensor_tensor(dst[:, :, :], x[:, :, :], xn[:, :, :], ALU.add)

                def rows(bk):
                    return bank(bk).rearrange("p (t d) -> p t d", t=T)

                def over_tiles(w):
                    return w.unsqueeze(1).to_broadcast([P, T, D])

                dve.wait_ge(x_loaded.sem, x_loaded.at(b, 16))
                dve.tensor_copy(x[:, :, :], x_in[:, :, :]).then_inc(x_taken.sem, 1)
                dve.wait_ge(x_taken.sem, x_taken.at(b, 1))

                norm_in()
                dve.wait_ge(xnT_ready.sem, xnT_ready.at(b, 1))
                step(dve.tensor_reduce(psumf, xnT[:, :].rearrange("p (l c) -> p l c", c=CHUNK), X, ALU.add))
                dve.tensor_scalar(pooled2[:, 0, :], psumf, 1.0 / CHUNK, None, ALU.mult)
                dve.tensor_scalar(pooled2[:, 1, :], psumf, 1.0 / CHUNK, None, ALU.mult).then_inc(pool_ready.sem, 1)
                for g in range(H // G0):
                    for kk, dst in enumerate((qs, ks)):
                        i = 2 * g + kk
                        dve.wait_ge(q0_hi.sem, q0_hi.at(b, i + 1))
                        for r0, r1_ in (((64, 128),) if kk == 0 else ((32, 64), (64, 96))):
                            last = dve.scalar_tensor_tensor(
                                out=dst[r0:r1_, g, :], in0=ps[r0:r1_, i, :], scalar=c["bqk"][r0:r1_, i:i + 1],
                                in1=dst[r0:r1_, g, :], op0=ALU.add, op1=ALU.subtract)
                        last.then_inc(q0_lo.sem, 1)
                    dve.wait_ge(q0_lo.sem, q0_lo.at(b, 2 * g + 2))
                    for hh in range(G0):
                        dve.tensor_scalar(km[:, G0 * g + hh, :], ks[:, g, :], hmask[:, hh:hh + 1], None, ALU.mult)\
                            .then_inc(km_ready.sem, 1)
                dve.wait_ge(rkv_ps.sem, rkv_ps.at(b, 1))
                for hh in range(LH):
                    dve.tensor_scalar(rkM[:, hh, :], ps[0:LD, 2, 0:NLAT], c["rk_b"][:, 0:1], lhmask[:, hh:hh + 1],
                                      ALU.add, ALU.mult)
                step(dve.tensor_tensor(rvb, ps[:, 2, NLAT:NLAT + LD], c["rv_b"][:, :], ALU.add))
                dve.tensor_tensor(rvM, rvb.unsqueeze(1).to_broadcast([P, 2, LD]), bdmask, ALU.mult)\
                    .then_inc(rkv_ready.sem, 1)
                dve.wait_ge(va_ps.sem, va_ps.at(b, 1))
                for t in range(T):
                    last = dve.tensor_tensor(v0[:, t, :, 0:HD0],
                                             ps[:, 0, t * P:(t + 1) * P].rearrange("p (h d) -> p h d", h=H),
                                             c["bv"][:, :].rearrange("p (h d) -> p h d", h=H), ALU.add)
                last.then_inc(va_ready.sem, 1)
                dve.wait_ge(ls_ps.sem, ls_ps.at(b, 1))
                lsc = bank(6, 2).rearrange("p (t h l) -> p t h l", t=T, h=LH)
                for t in range(T):
                    last = dve.tensor_tensor(lp[:, t], lsc[:, t],
                                             c["lmask"][:, t, :].unsqueeze(1).to_broadcast([P, LH, NLAT]), ALU.add)
                step(last)
                step(dve.tensor_reduce(lmx[:, :, :], lp, X, ALU.max))
                step(dve.tensor_scalar(lmx[:, :, :], lmx[:, :, :], -CLAMP, None, ALU.max))
                lpf = lp.rearrange("p t h l -> p (t h) l")

                def lat_bc(a):
                    return a[:, :, :].rearrange("p t h -> p (t h)").unsqueeze(2).to_broadcast([P, T * LH, NLAT])

                dve.tensor_tensor(lpf, lpf, lat_bc(lmx), ALU.subtract).then_inc(ls_ready.sem, 1)

                def max0(i):
                    g, qb = divmod(i, T)
                    s = 2 * (i % 3)
                    dve.wait_ge(sr0.sem, sr0.at(b, i + 1))
                    w = P if qb == 0 else 2 * P
                    src = bank(s, 2)[:, 0:G0 * w].rearrange("p (h n) -> p h n", h=G0)
                    dve.tensor_reduce(mx0[:, qb, G0 * g:G0 * g + G0], src, X, ALU.max).then_inc(mx0_done.sem, 1)

                for i in range(3):
                    max0(i)
                dve.wait_ge(lexp.sem, lexp.at(b, 1))
                step(dve.tensor_reduce(lsum[:, :, :], lp, X, ALU.add))
                step(dve.tensor_scalar(lsum[:, :, :], lsum[:, :, :], 1e-30, None, ALU.max))
                step(dve.reciprocal(lsum[:, :, :], lsum[:, :, :]))
                dve.tensor_tensor(lpf, lpf, lat_bc(lsum), ALU.mult).then_inc(lp_ready.sem, 1)
                for i in range(3, 6):
                    max0(i)
                dve.wait_ge(rem_ps.sem, rem_ps.at(b, 1))
                dve.tensor_tensor(remote, rows(7), over_tiles(c["rout_b"][:, :]), ALU.add)\
                    .then_inc(rem_ready.sem, 1)
                for i in range(6, 16):
                    max0(i)
                dve.wait_ge(mx0_done.sem, mx0_done.at(b, 16))
                dve.tensor_scalar(nm[:, :, :], mx0[:, :, :], -1.0, CLAMP, ALU.mult, ALU.min)\
                    .then_inc(nm_ready.sem, 1)

                def heads(a):
                    return a.rearrange("p t (h d) -> p (t h) d", h=H)

                def head_bc(a):
                    return a.rearrange("p t h -> p (t h)").unsqueeze(2).to_broadcast([P, T * H, HD0])

                dve.wait_ge(rem_ready.sem, rem_ready.at(b, 1))
                step(dve.tensor_tensor(heads(gtmp), heads(remote),
                                       c["glr"][:, 1, :].unsqueeze(1).to_broadcast([P, T * H, HD0]), ALU.mult))
                step(dve.tensor_reduce(gz2[:, :, :].rearrange("p t h -> p (t h)"), heads(gtmp), X, ALU.add))
                dve.wait_ge(pv0.sem, pv0.at(b, H))
                acc0 = [ps[:, 6 + k, 0:288].rearrange("p (t h d) -> p t h d", t=2, h=H) for k in range(2)]
                for k in range(2):
                    last = dve.tensor_scalar(rden[:, 2 * k:2 * k + 2, :], acc0[k][:, :, :, HD0], 1e-30, None, ALU.max)
                step(last)
                step(dve.reciprocal(rden[:, :, :], rden[:, :, :]))
                for t in range(T):
                    last = dve.tensor_tensor(local[:, t, :].rearrange("p (h d) -> p h d", h=H),
                                             acc0[t // 2][:, t % 2, :, 0:HD0],
                                             rden[:, t, :].unsqueeze(2).to_broadcast([P, H, HD0]), ALU.mult)
                step(last)
                step(dve.tensor_tensor(heads(gtmp), heads(local),
                                       c["glr"][:, 0, :].unsqueeze(1).to_broadcast([P, T * H, HD0]), ALU.mult))
                step(dve.tensor_reduce(gz[:, :, :].rearrange("p t h -> p (t h)"), heads(gtmp), X, ALU.add))
                dve.tensor_tensor(gz[:, :, :], gz[:, :, :], gz2[:, :, :], ALU.add).then_inc(gz_ready.sem, 1)
                step(dve.tensor_tensor(local, local, remote, ALU.subtract))
                dve.wait_ge(gexp.sem, gexp.at(b, 1))
                step(dve.tensor_scalar(gz2[:, :, :], gz2[:, :, :], 1.0, None, ALU.add))
                step(dve.reciprocal(gz2[:, :, :], gz2[:, :, :]))
                step(dve.tensor_tensor(heads(local), heads(local), head_bc(gz2[:, :, :]), ALU.mult))
                dve.tensor_tensor(xn[:, :, :], local, remote, ALU.add).then_inc(mix_ready.sem, 1)

                def finish(n, bk, bias, dst):
                    dve.wait_ge(y_ps.sem, y_ps.at(b, n + 1))
                    if bias is None:
                        i = dve.tensor_copy(y[:, :, :], rows(bk))
                    else:
                        i = dve.tensor_tensor(y[:, :, :], rows(bk), over_tiles(bias), ALU.add)
                    step(i)
                    step(norm_out(dst))

                finish(0, 1, c["out_b"][:, :], x)
                norm_in()
                finish(1, 5, c["b2"][:, :], x)
                norm_in()

                def rotate(i):
                    t, kk = divmod(i, 2)
                    u = 3 * t + kk
                    if i >= 2:
                        dve.wait_ge(b_lo.sem, b_lo.at(b, i - 1))
                    dve.wait_ge(b_sq.sem, b_sq.at(b, i + 1))
                    src = bank(2 * (u % 3), 2).rearrange("p (h d) -> p h d", h=H)

                    def tab(k, lo, hi_):
                        return csq[:, kk, k, t, lo:hi_].unsqueeze(1).to_broadcast([P, H, hi_ - lo])

                    dve.tensor_tensor(rot1[:, i % 2], src, tab(0, 0, HD1), ALU.mult)
                    dve.tensor_tensor(rot2[:, i % 2, :, 0:half], src[:, :, half:HD1], tab(1, 0, half), ALU.mult)
                    dve.tensor_tensor(rot2[:, i % 2, :, half:HD1], src[:, :, 0:half], tab(1, half, HD1), ALU.mult)\
                        .then_inc(b_rot.sem, 1)
                    step(dve.tensor_reduce(ve1[:, i % 2, :], sq, X, ALU.add))
                    dve.tensor_scalar(ve1[:, i % 2, :], ve1[:, i % 2, :], 1.0 / HD1, RMS_EPS, ALU.mult, ALU.add)\
                        .then_inc(var_ready.sem, 1)

                def split(i):
                    dve.wait_ge(b_sum.sem, b_sum.at(b, i + 1))
                    dve.wait_ge(rstd_ready.sem, rstd_ready.at(b, 5 + i + 1))
                    dve.tensor_tensor(rot1[:, i % 2], rot1[:, i % 2],
                                      rinv[:, i % 2, :].unsqueeze(2).to_broadcast([P, H, HD1]), ALU.mult)\
                        .then_inc(b_qn.sem, 1)
                    dve.wait_ge(b_hi.sem, b_hi.at(b, i + 1))
                    dve.tensor_tensor(hilo[:, i % 2, :, 1, :], rot1[:, i % 2], hilo[:, i % 2, :, 0, :], ALU.subtract)\
                        .then_inc(b_lo.sem, 1)

                for i in range(8):
                    rotate(i)
                    if i >= 1:
                        split(i - 1)
                split(7)
                norm_no[0] += 8
                for h in range(H):
                    s = 3 * (h % 2)
                    dve.wait_ge(sr1.sem, sr1.at(b, h + 1))
                    for qb in (3, 2, 1, 0):
                        w = (qb + 1) * P
                        a = 256 if qb == 0 else 0
                        last = dve.tensor_reduce(mx0[:, qb, h:h + 1], ps[:, s + (0, 1, 2, 2)[3 - qb], a:a + w],
                                                 X, ALU.max)
                    last.then_inc(mx1_done.sem, 1)
                dve.wait_ge(mx1_done.sem, mx1_done.at(b, H))
                dve.tensor_scalar(nm[:, :, :], mx0[:, :, :], -1.0, None, ALU.mult).then_inc(nm_ready.sem, 1)
                for h in range(H):
                    dve.wait_ge(pv1.sem, pv1.at(b, h + 1))
                    src = ps[:, 6 + h % 2, 0:260].rearrange("p (t d) -> p t d", t=T)
                    step(dve.reciprocal(r1[:, h % 2, :], src[:, :, HD1]))
                    dve.tensor_tensor(ao[:, :, h * HD1:(h + 1) * HD1], src[:, :, 0:HD1],
                                      r1[:, h % 2, :].unsqueeze(2).to_broadcast([P, T, HD1]), ALU.mult)\
                        .then_inc(ao_done.sem, 1)
                finish(2, 4, None, x)

                norm_in()
                dve.wait_ge(lg_ps.sem, lg_ps.at(b, 1))
                lg = ps[:, 7, 0:T * NE].rearrange("p (t e) -> p t e", t=T)

                def tok_bc(a):
                    return a.unsqueeze(2).to_broadcast([P, T, NE])

                step(dve.tensor_reduce(r4[:, :], lg, X, ALU.max))
                dve.tensor_tensor(pr[:, :, :], lg, tok_bc(r4[:, :]), ALU.subtract).then_inc(lg_max.sem, 1)
                dve.wait_ge(lg_exp.sem, lg_exp.at(b, 1))
                step(dve.tensor_reduce(r4[:, :], pr[:, :, :], X, ALU.add))
                step(dve.reciprocal(r4[:, :], r4[:, :]))
                step(dve.tensor_tensor(pr[:, :, :], pr[:, :, :], tok_bc(r4[:, :]), ALU.mult))
                for t in range(T):
                    other = pr[:, t, :].unsqueeze(1).to_broadcast([P, NE, NE])
                    mine = pr[:, t, :].unsqueeze(2).to_broadcast([P, NE, NE])
                    dve.tensor_tensor(cmp1[:, t], other, mine, ALU.is_gt)
                    last = dve.tensor_tensor(cmp2[:, t], other, mine, ALU.is_equal)
                step(last)
                tri = c["tri"][:, :].unsqueeze(1).to_broadcast([P, T, NE * NE])
                step(dve.tensor_tensor(cmp2[:, :, :, :].rearrange("p t a e -> p t (a e)"),
                                       cmp2[:, :, :, :].rearrange("p t a e -> p t (a e)"), tri, ALU.mult))
                step(dve.tensor_tensor(cmp1[:, :, :, :], cmp1[:, :, :, :], cmp2[:, :, :, :], ALU.add))
                step(dve.tensor_reduce(comb[:, :, :], cmp1[:, :, :, :], X, ALU.add))
                step(dve.scalar_tensor_tensor(out=comb[:, :, :], in0=comb[:, :, :], scalar=2.0, in1=pr[:, :, :],
                                              op0=ALU.is_lt, op1=ALU.mult))
                step(dve.tensor_reduce(r4[:, :], comb[:, :, :], X, ALU.add))
                step(dve.reciprocal(r4[:, :], r4[:, :]))
                step(dve.tensor_tensor(comb[:, :, :], comb[:, :, :], tok_bc(r4[:, :]), ALU.mult))

                def combine(e):
                    dve.wait_ge(dn_ps.sem, dn_ps.at(b, e + 1))
                    if e:
                        dve.wait_ge(dn_read.sem, dn_read.at(b, e))
                    for t in range(T):
                        o = ps[:, 6 + e % 2, t * P:(t + 1) * P]
                        if e == 0:
                            last = dve.tensor_scalar(acc[:, t, :], o, comb[:, t, e:e + 1], None, ALU.mult)
                        else:
                            last = dve.scalar_tensor_tensor(out=acc[:, t, :], in0=o, scalar=comb[:, t, e:e + 1],
                                                            in1=acc[:, t, :], op0=ALU.mult, op1=ALU.add)
                    last.then_inc(dn_read.sem, 1)

                for e in range(NE):
                    for f in range(FC):
                        k = e * FC + f
                        dve.wait_ge(gelu_done.sem, gelu_done.at(b, k + 1))
                        if e >= 2 and f == 0:
                            dve.wait_ge(dn_ps.sem, dn_ps.at(b, e - 1))
                        dve.tensor_tensor(hT[:, e % 2, f, :], gact[:, k % 3, :], bank(2 * (k % 3) + 1), ALU.mult)\
                            .then_inc(hact.sem, 1)
                    if e >= 1:
                        combine(e - 1)
                combine(NE - 1)
                dve.wait_ge(dn_read.sem, dn_read.at(b, NE))
                dve.wait_ge(x_out_free.sem, x_out_free.at(b, 1))
                norm_out(x_out).then_inc(x_final.sem, 1)
                dve.wait_ge(x_final.sem, x_final.at(b, 1))
                assert step_no[0] == VEC_STEPS, step_no[0]


_CONST = {}


def constants():
    i = np.arange(P)
    small = np.zeros((P, 88), np.float32)
    small[:, 0:4] = (i[:, None] % 32) // 8 == np.arange(4)
    small[:LD, 4:8] = i[:LD, None] // 8 == np.arange(4)
    col = np.arange(2 * LD)
    small[:, 8:72] = (col[None, :] % LD) // LHD == 2 * (col[None, :] // LD) + i[:, None] // 64
    small[:, 72:] = -0.5
    a, k = i[:, None], i[None, :]
    masks = np.zeros((P, 768), np.float32)
    masks[:, 0:128] = np.where(k >= a, 0, NEG)
    masks[:, 128:256] = np.where(k < a, 0, NEG)
    masks[:, 256:384] = np.where(k > a, 0, NEG)
    masks[:, 384:512] = np.where(k <= a, 0, NEG)
    masks[:, 512:640] = np.where(k <= a, 0, NEG1)
    masks[:, 640:768] = np.where(k >= a, 0, NEG1)
    sel = np.zeros((H, H, P), np.float32)
    sel[np.arange(H), np.arange(H), :] = 1
    tok = (np.arange(T)[None, :] * P + i[:, None])
    lmask = np.where(np.arange(NLAT)[None, None, :] < (tok // CHUNK)[:, :, None], 0, NEG).astype(np.float32)
    inv = (1.0 / np.float32(10000.0) ** (np.arange(0, HD1, 2, dtype=np.float32) / np.float32(HD1))).astype(np.float32)
    fr = (np.arange(S, dtype=np.float32)[:, None] * inv).astype(np.float32)
    cos, sin = np.cos(fr), np.sin(fr)
    cs = np.stack([np.concatenate([cos, cos], 1), np.concatenate([-sin, sin], 1)])
    cs = cs.reshape(2, T, P, HD1).transpose(2, 0, 1, 3)
    e = np.arange(NE)
    tri = np.broadcast_to((e[None, :] < e[:, None]).reshape(1, -1), (P, NE * NE))
    return {"ident_f": np.eye(P, dtype=np.float32), "small": small,
            "masks": masks, "sel": sel.reshape(H, H * P), "lmask": lmask, "cs": cs.astype(np.float32),
            "tri": tri.astype(np.float32)}


def kernel(**inputs):
    import concourse.bacc as bacc
    from concourse.bass_utils import run_bass_kernel_spmd as run

    w = {k: np.asarray(v) for k, v in inputs.items()}

    def rows(v):
        return np.broadcast_to(v.reshape(1, -1), (P, v.size))

    def slots(m):
        return np.concatenate([np.tile(m[..., 32 * g:32 * g + 32], 4) for g in range(4)], -1)

    qkv, qb = w["L0_attn_qkv_w"], w["L0_attn_qkv_b"]
    bq, bk = slots(qb[0:D]).reshape(4, P), slots(qb[D:2 * D]).reshape(4, P)
    a = dict(constants())
    a.update({
        "x": w["L0_attn_x"].reshape(NSEQ * S, D),
        "wqrep": slots(qkv[:, 0:D]), "wkrep": slots(qkv[:, D:2 * D]), "wv": qkv[:, 2 * D:],
        "bqk": np.stack([bq, bk], 1).reshape(8, P).T, "bv": rows(qb[2 * D:]),
        "rq_w": w["L0_attn_rq_w"], "rq_b": w["L0_attn_rq_b"].reshape(LD, 1),
        "rkv_w": w["L0_attn_rkv_w"], "rk_b": w["L0_attn_rkv_b"][:LD].reshape(LD, 1),
        "rv_b": rows(w["L0_attn_rkv_b"][LD:]),
        "rout_w": w["L0_attn_rout_w"], "rout_b": rows(w["L0_attn_rout_b"]),
        "out_w": w["L0_attn_out_w"], "out_b": rows(w["L0_attn_out_b"]),
        "glr": np.broadcast_to(np.stack([w["L0_attn_gl_w"].ravel(), w["L0_attn_gr_w"].ravel()])[None],
                               (P, 2, HD0)),
        "w1": w["L0_ffn_W1"].T, "b1": w["L0_ffn_b1"].reshape(FC, P).T,
        "w2": w["L0_ffn_W2"].T.reshape(FC, P, D).transpose(1, 0, 2).reshape(P, FC * D),
        "b2": rows(w["L0_ffn_b2"]),
        "qkn": np.broadcast_to(np.stack([w["L1_attn_q_norm_w"], w["L1_attn_k_norm_w"]])[None], (P, 2, HD1)),
        "wqkv1": w["L1_attn_wqkv"].T,
        "wo1": w["L1_attn_wo"].T.reshape(8, P, D).transpose(1, 0, 2).reshape(P, 8 * D),
        "gate_w": w["L1_ffn_gate_w"].T,
        "gu": w["L1_ffn_gate_up_w"].transpose(2, 0, 1),
        "down": w["L1_ffn_down_w"].transpose(2, 0, 1).reshape(FC, P, NE, D).transpose(1, 2, 0, 3),
    })
    nc = bacc.Bacc("TRN2", target_bir_lowering=False, num_devices=1)
    arrays, ins = {}, {}
    for name, v in a.items():
        v = np.ascontiguousarray(v)
        arrays["in_" + name] = v
        ins[name] = nc.dram_tensor("in_" + name, v.shape, mybir.dt.from_np(v.dtype), kind="ExternalInput").ap()
    out = nc.dram_tensor("out_0", (NSEQ * S, D), F32, kind="ExternalOutput").ap()
    build(nc, ins, out)
    r = run(nc, [arrays], core_ids=[0])
    return r.results[0]["out_0"].reshape(NSEQ, S, D)
```

```python
from contextlib import ExitStack

import numpy as np

import concourse.bass as bass
from concourse import mybir

F32 = mybir.dt.float32
BF16 = mybir.dt.bfloat16
ALU = mybir.AluOpType
ACT = mybir.ActivationFunctionType
X = mybir.AxisListType.X

P = 128
NSEQ, S, D = 8, 512, 128
T = S // P
H = 16
HD0, HD1 = D // H, 64
G0 = 4
NLAT, LH, LHD, LD = 64, 4, 8, 32
CHUNK = S // NLAT
FF = 512
NE, FE = 8, 512
FC = FF // P
NEG = -1.0e9
NEG1 = -1.0e30
CLAMP = 1.0e8
LN_EPS, RMS_EPS, Q_EPS = 1e-5, 1e-6, 1e-5
SCALE0 = float(1.0 / np.sqrt(HD0))
SCALEL = float(1.0 / np.sqrt(LHD))
SCALE1 = float(HD1 ** -0.5)
W0 = (256, 256, 256, 128)
OFF0 = (0, 256, 512, 768)
OFF1 = (0, 512, 1024, 896)
VEC_STEPS = 81


class Sig:

    def __init__(self, ctx, nc, name, per_turn):
        self.sem = ctx.enter_context(nc.semaphore(name))
        self.n = per_turn

    def at(self, b, k):
        return b * self.n + k


def build(nc, ins, out):
    ctx = ExitStack()
    with ctx:
        def sb(name, shape, dt=F32):
            return ctx.enter_context(nc.sbuf_tensor(name, shape, dt))

        def sig(name, n):
            return Sig(ctx, nc, name, n)

        loaded = {}
        order = ["ident_f", "wqrep", "wkrep", "bqk", "wv", "bv", "rq_w", "rq_b", "rkv_w", "rk_b", "rv_b",
                 "small", "lmask", "rout_w", "rout_b", "out_w", "out_b", "glr",
                 "w1", "b1", "w2", "b2", "wqkv1", "wo1", "gate_w", "tri", "down", "masks", "sel", "cs", "qkn", "gu"]
        for name in order[:-5]:
            loaded[name] = sb("c_" + name, list(ins[name].shape))
        c = loaded
        ident_f = c["ident_f"][:, :]
        ident_b_t = sb("ident_b", [P, P], BF16)
        masks_b = sb("masks_b", [P, 768], BF16)
        sel_b = sb("sel_b", [H, H, P], BF16)
        ident_b = ident_b_t[:, :]
        hmask = c["small"][:, 0:4]
        lhmask = c["small"][0:LD, 4:8]
        bdmask = c["small"][:, 8:8 + 2 * LD].rearrange("p (c d) -> p c d", c=2)
        mhalf = c["small"][:, 72:88]
        onesf = sb("onesf", [P, P])
        mask_rows, mask_cols = masks_b[:, 0:256], masks_b[:, 256:512]
        cmask_rows, cmask_cols = masks_b[:, 512:640], masks_b[:, 640:768]

        gu_b = sb("gu_b", [P, 2, NE, 2 * FE], BF16)
        xh = sb("xh", [P, 2, S], BF16)
        x_in = sb("x_in", [P, T, D])
        x = sb("x", [P, T, D])
        x_out = sb("x_out", [P, T, D])
        norm = sb("norm", [P, 3 * T * D])
        xn = norm[:, 0:512].rearrange("p (t d) -> p t d", t=T)
        y = norm[:, 512:1024].rearrange("p (t d) -> p t d", t=T)
        xnT = norm[:, 1024:1536]
        bst = sb("bst", [P, T, 6])
        mv = sb("mv", [P, T, 2])
        ve = sb("ve", [P, T])
        rstd = sb("rstd", [P, T])

        region = sb("region", [P, 12 * 1024])
        region2 = sb("region2", [P, 7 * 1024])
        rb = region[:, :].bitcast(BF16)
        c["masks"], c["sel"] = region[:, 1024:1792], region[0:H, 2048:4096]
        c["gu"] = region[:, 0:8192].rearrange("p (e n) -> p e n", e=NE)
        c["cs"] = region[:, 4096:4608].rearrange("p (k t d) -> p k t d", k=2, t=T)
        c["qkn"] = region[:, 4608:4736].rearrange("p (k d) -> p k d", k=2)
        km = rb[:, 0:H * S].rearrange("p (h s) -> p h s", h=H)
        pT0 = region[:, 4096:4096 + 3 * 896].rearrange("p (r s) -> p r s", r=3)
        lp = region[:, 7168:7168 + 1024].rearrange("p (t h l) -> p t h l", t=T, h=LH)
        lpT = region[:, 8192:8192 + 1024].rearrange("p (c s) -> p c s", c=2)
        qs = region[:, 9216:9216 + 1024].bitcast(BF16).rearrange("p (g s) -> p g s", g=H // G0)
        ks = region[:, 10240:10240 + 1024].bitcast(BF16).rearrange("p (g s) -> p g s", g=H // G0)
        mixT = region[:, 11264:11264 + 512]
        remote = region2[:, 0:512].rearrange("p (t d) -> p t d", t=T)
        local = region2[:, 512:1024].rearrange("p (t d) -> p t d", t=T)
        gtmp = region2[:, 1024:1536].rearrange("p (t d) -> p t d", t=T)
        oT = region2[:, 4096:6144].rearrange("p (g s) -> p g s", g=H // G0)
        rqT = region2[0:LD, 1536:2048]
        latT = region2[0:LD, 2048:2560]
        rkM = region2[0:LD, 2560:2816].rearrange("p (h l) -> p h l", h=LH)
        pooled2 = region2[:, 2816:2944].rearrange("p (r l) -> p r l", r=2)
        psumf = region2[:, 2944:3008]
        rvb = region2[:, 3008:3040]
        rvM = region2[:, 3072:3136].rearrange("p (c d) -> p c d", c=2)
        mx0 = sb("mx0", [P, T, H])
        nm = sb("nm", [P, T, H])
        nmT = sb("nmT", [H, S], BF16)
        lmx = sb("lmx", [P, T, LH])
        lsum = sb("lsum", [P, T, LH])
        v0 = sb("v0", [P, T, H, 32])
        rden = sb("rden", [P, T, H])
        gz = sb("gz", [P, T, H])
        gz2 = sb("gz2", [P, T, H])
        h0T = region[:, 0:4 * S].rearrange("p (f s) -> p f s", f=FC)
        qst = rb[:, 0:8192].rearrange("p (h s) -> p h s", h=H)
        kst = rb[:, 8192:16384].rearrange("p (h s) -> p h s", h=H)
        kst2 = rb[:, 16384:24576].rearrange("p (h s) -> p h s", h=H)
        rot1 = region2[:, 0:3072].rearrange("p (r h d) -> p r h d", r=3, h=H)
        rot2 = region2[:, 3072:5120].rearrange("p (r h d) -> p r h d", r=2, h=H)
        sq = region2[:, 5120:7168].rearrange("p (r h d) -> p r h d", r=2, h=H)
        hilo = region[:, 8192:11264].bitcast(BF16).rearrange("p (r h k d) -> p r h k d", r=3, h=H, k=2)
        ao = region2[:, 0:4096].rearrange("p (t n) -> p t n", t=T)
        aoT = region[:, 0:4096].rearrange("p (r k s) -> p r k s", r=4, k=8)
        p1 = region2[:, 4096:5376]
        p1_parts = [a.bitcast(BF16).rearrange("p (k s) -> p k s", k=2)
                    for a in (region2[:, 5376:6656], norm[:, 0:1280])]
        v1 = sb("v1", [P, T, H, 2, HD1 + 1], BF16)
        ve1 = sb("ve1", [P, 2, H])
        rinv = sb("rinv", [P, 2, H])
        r1 = sb("r1", [P, 2, T])
        csq = sb("csq", [P, 2, 2, T, HD1])
        hT = region[:, 0:4096].rearrange("p (r f s) -> p r f s", r=2, f=FC)
        gact = region[:, 4096:4096 + 1536].rearrange("p (r s) -> p r s", r=3)
        acc = y
        pr = region[:, 6144:6176].rearrange("p (t e) -> p t e", t=T)
        comb = region[:, 6176:6208].rearrange("p (t e) -> p t e", t=T)
        cmp1 = region[:, 5632:5888].rearrange("p (t a e) -> p t a e", t=T, a=NE)
        cmp2 = region[:, 5888:6144].rearrange("p (t a e) -> p t a e", t=T, a=NE)
        r4 = sb("r4", [P, T])
        thr = region[:, 5000:5004]
        gam = region[:, 5004:5006]
        qtmp = region[:, 0:512]
        qtmp2 = region[:, 512:1024]

        ps = ctx.enter_context(nc.psum_tensor("ps", [P, 8, 512], F32))

        def bank(i, n=1):
            return ps[:, i, :] if n == 1 else ps[:, i:i + n, :].rearrange("p b n -> p (b n)")

        wload = {k: sig("w_" + k, 16) for k in ("qkv", "lat", "gate", "mlp", "attn1", "exp", "gu")}
        group_of = {}
        for k in order:
            group_of[k] = ("qkv" if k in ("ident_f", "wqrep", "wkrep", "bqk", "wv", "bv") else
                           "lat" if k in ("rq_w", "rq_b", "rkv_w", "rk_b", "rv_b", "small", "lmask", "rout_w",
                                          "rout_b") else
                           "gate" if k in ("out_w", "out_b", "glr", "masks", "sel") else
                           "mlp" if k in ("w1", "b1", "w2", "b2") else
                           "gu" if k == "gu" else "attn1" if k in ("cs", "qkn", "wqkv1", "wo1") else "exp")
        gcount = {g: 16 * sum(1 for k in order if group_of[k] == g) for g in wload}

        set_ones = sig("set_ones", 0)
        abs_sums = sig("abs_sums", 0)
        gam_ready = sig("gam_ready", 0)
        quant_done = sig("quant_done", 0)
        gu_hi = sig("gu_hi", 0)
        gu_lo = sig("gu_lo", 0)
        setup_step = sig("setup_step", 0)

        x_loaded = sig("x_loaded", 16)
        x_taken = sig("x_taken", 1)
        x_final = sig("x_final", 1)
        x_out_free = sig("x_out_free", 16)
        vec = sig("vec_step", VEC_STEPS)
        var_ready = sig("var_ready", 16)
        rstd_ready = sig("rstd_ready", 16)
        xn_ready = sig("xn_ready", 4)
        xnT_ps = sig("xnT_ps", 4)
        xnT_ready = sig("xnT_ready", 4)

        q0_ps = sig("q0_ps", 8)
        q0_hi = sig("q0_hi", 8)
        q0_lo = sig("q0_lo", 8)
        km_ready = sig("km_ready", H)
        va_ps = sig("va_ps", 1)
        va_ready = sig("va_ready", 1)
        rq_ps = sig("rq_ps", 1)
        rq_ready = sig("rq_ready", 1)
        pool_ready = sig("pool_ready", 1)
        rkv_ps = sig("rkv_ps", 1)
        rkv_ready = sig("rkv_ready", 1)
        ls_ps = sig("ls_ps", 1)
        ls_free = sig("ls_free", 1)
        ls_ready = sig("ls_ready", 1)
        lexp = sig("lexp", 1)
        lp_ready = sig("lp_ready", 1)
        lpT_ps = sig("lpT_ps", 1)
        lpT_ready = sig("lpT_ready", 1)
        lat_ps = sig("lat_ps", 1)
        lat_ready = sig("lat_ready", 1)
        rem_ps = sig("rem_ps", 1)
        rem_ready = sig("rem_ready", 1)
        sr0 = sig("sr0", 16)
        mx0_done = sig("mx0_done", 16)
        nm_ready = sig("nm_ready", 2)
        nmT_ps = sig("nmT_ps", 2)
        nmT_ready = sig("nmT_ready", 2)
        sc0 = sig("sc0", H)
        e0 = sig("e0", H)
        pv0 = sig("pv0", H)
        o_ev = sig("o_ev", H // G0)
        o_rows = sig("o_rows", 1)
        gz_ready = sig("gz_ready", 1)
        gexp = sig("gexp", 1)
        mix_ready = sig("mix_ready", 1)
        mixT_ps = sig("mixT_ps", 1)
        mixT_ready = sig("mixT_ready", 1)
        y_ps = sig("y_ps", 3)
        y_read = sig("y_read", 3)
        h_ps = sig("h_ps", FC)
        h_ready = sig("h_ready", FC)

        pj = sig("pj", 8)
        pv_ps = sig("pv_ps", T)
        b_sq = sig("b_sq", 8)
        b_rot = sig("b_rot", 8)
        b_vh = sig("b_vh", T)
        b_v = sig("b_v", T)
        b_sum = sig("b_sum", 8)
        b_qn = sig("b_qn", 8)
        b_hi = sig("b_hi", 8)
        b_lo = sig("b_lo", 8)
        b_tr = sig("b_tr", 8)
        b_ev = sig("b_ev", 8)
        k_swapped = sig("k_swapped", 32)
        sr1 = sig("sr1", H)
        mx1_done = sig("mx1_done", H)
        sc1 = sig("sc1", H)
        e1 = sig("e1", 2 * H)
        p1_lo = sig("p1_lo", H)
        pv1 = sig("pv1", H)
        ao_done = sig("ao_done", H)
        aoT_ps = sig("aoT_ps", T)
        aoT_ready = sig("aoT_ready", T)

        xh_hi = sig("xh_hi", 1)
        xh_lo = sig("xh_lo", 1)
        lg_ps = sig("lg_ps", 1)
        lg_max = sig("lg_max", 1)
        lg_exp = sig("lg_exp", 1)
        gu_ps = sig("gu_ps", NE * FC)
        gelu_done = sig("gelu_done", NE * FC)
        hact = sig("hact", NE * FC)
        dn_ps = sig("dn_ps", NE)
        dn_read = sig("dn_read", NE)

        block = ctx.enter_context(nc.Block())
        x_dram = ins["x"].rearrange("(b t p) d -> b p t d", t=T, p=P)
        out_dram = out.rearrange("(b t p) d -> b p t d", t=T, p=P)

        @block.sync
        def _(sp):
            sp.dma_start(x_in[:, :, :], x_dram[0]).then_inc(x_loaded.sem, 16)
            for name in order:
                dst = c[name]
                full = tuple(slice(None) for _ in dst.shape)
                if name == "gu":
                    sp.wait_ge(quant_done.sem, 2)
                sp.dma_start(dst[full], ins[name]).then_inc(wload[group_of[name]].sem, 16)
            with sp.Fori(0, NSEQ) as b:
                sp.wait_ge(b_ev.sem, b_ev.at(b, 8))
                sp.dma_start(kst2[64:128, :, :], kst[0:64, :, :]).then_inc(k_swapped.sem, 16)
                sp.dma_start(kst2[0:64, :, :], kst[64:128, :, :]).then_inc(k_swapped.sem, 16)
                sp.wait_ge(x_taken.sem, x_taken.at(b, 1))
                sp.dma_start(x_in[:, :, :], x_dram[(b + 1) % NSEQ]).then_inc(x_loaded.sem, 16)
                sp.wait_ge(x_final.sem, x_final.at(b, 1))
                sp.dma_start(out_dram[b], x_out[:, :, :]).then_inc(x_out_free.sem, 16)
            sp.wait_ge(x_loaded.sem, 16 * (NSEQ + 1))
            sp.wait_ge(x_out_free.sem, 16 * NSEQ + 1)

        @block.gpsimd
        def _(pool):
            with pool.Fori(0, NSEQ) as b:
                done = [0]

                def power(dst, src):
                    done[0] += 1
                    pool.wait_ge(var_ready.sem, var_ready.at(b, done[0]))
                    pool.tensor_tensor(dst, src, mhalf[:, 0:src.shape[1]], ALU.pow).then_inc(rstd_ready.sem, 1)

                for n in range(5):
                    power(rstd[:, :], ve[:, :])
                for i in range(8):
                    pool.wait_ge(b_rot.sem, b_rot.at(b, i + 1))
                    pool.tensor_tensor(rot1[:, i % 3], rot1[:, i % 3], rot2[:, i % 2], ALU.add)\
                        .then_inc(b_sum.sem, 1)
                    power(rinv[:, i % 2, :], ve1[:, i % 2, :])
                for n in range(3):
                    power(rstd[:, :], ve[:, :])

        @block.scalar
        def _(act):
            act.wait_ge(wload["mlp"].sem, gcount["mlp"])
            act.activation(qtmp, c["w1"][:, :], ACT.Abs, accum_out=gam[:, 0:1]).then_inc(abs_sums.sem, 1)
            act.activation(qtmp2, c["w2"][:, :], ACT.Abs, accum_out=gam[:, 1:2]).then_inc(abs_sums.sem, 1)
            act.wait_ge(wload["gu"].sem, gcount["gu"])
            for e in range(NE):
                act.copy(gu_b[:, 0, e, :], c["gu"][:, e, :]).then_inc(gu_hi.sem, 1)
            with act.Fori(0, NSEQ) as b:
                def copy_xnT(n):
                    act.wait_ge(xnT_ps.sem, xnT_ps.at(b, n + 1))
                    act.copy(xnT[:, :], bank(0)).then_inc(xnT_ready.sem, 1)

                copy_xnT(0)
                for g in range(H // G0):
                    for kk, dst in enumerate((qs, ks)):
                        i = 2 * g + kk
                        act.wait_ge(q0_ps.sem, q0_ps.at(b, i + 1))
                        act.activation(dst[:, g, :], bank(i), ACT.Identity, bias=c["bqk"][:, i:i + 1])\
                            .then_inc(q0_hi.sem, 1)
                act.wait_ge(rq_ps.sem, rq_ps.at(b, 1))
                act.activation(rqT, ps[0:LD, 1, :], ACT.Identity, bias=c["rq_b"][:, 0:1])\
                    .then_inc(rq_ready.sem, 1)
                act.wait_ge(ls_ready.sem, ls_ready.at(b, 1))
                act.activation(lp, lp, ACT.Exp, scale=SCALEL).then_inc(lexp.sem, 1)
                act.wait_ge(lpT_ps.sem, lpT_ps.at(b, 1))
                act.copy(lpT.rearrange("p c s -> p (c s)"), bank(4, 2)).then_inc(lpT_ready.sem, 1)
                act.wait_ge(lat_ps.sem, lat_ps.at(b, 1))
                act.copy(latT, ps[0:LD, 6, :]).then_inc(lat_ready.sem, 1)
                act.wait_ge(nmT_ps.sem, nmT_ps.at(b, 1))
                act.copy(nmT[:, :], ps[0:H, 6, :]).then_inc(nmT_ready.sem, 1)
                for h in range(H):
                    act.wait_ge(sc0.sem, sc0.at(b, h + 1))
                    if h >= 3:
                        act.wait_ge(pv0.sem, pv0.at(b, h - 2))
                    act.activation(pT0[:, h % 3, :], bank(2 * (h % 3), 2)[:, 0:896], ACT.Exp, scale=SCALE0)\
                        .then_inc(e0.sem, 1)
                act.wait_ge(gz_ready.sem, gz_ready.at(b, 1))
                act.activation(gz2[:, :, :], gz[:, :, :], ACT.Exp, scale=-1.0).then_inc(gexp.sem, 1)
                act.wait_ge(mixT_ps.sem, mixT_ps.at(b, 1))
                act.copy(mixT, bank(0)).then_inc(mixT_ready.sem, 1)

                copy_xnT(1)
                for f in range(FC):
                    act.wait_ge(h_ps.sem, h_ps.at(b, f + 1))
                    act.activation(h0T[:, f, :], bank(1 + f), ACT.Relu, bias=c["b1"][:, f:f + 1])\
                        .then_inc(h_ready.sem, 1)

                copy_xnT(2)

                def square(i):
                    act.wait_ge(pj.sem, pj.at(b, i + 1))
                    if i >= 2:
                        act.wait_ge(var_ready.sem, var_ready.at(b, 5 + i - 1))
                    act.activation(sq[:, i % 2].rearrange("p h d -> p (h d)"), bank(2 * (i % 3), 2), ACT.Square)\
                        .then_inc(b_sq.sem, 1)

                def take_v(t):
                    act.wait_ge(pv_ps.sem, pv_ps.at(b, t + 1))
                    act.copy(v1[:, t, :, 0, 0:HD1],
                             bank(4 + 2 * (t % 2), 2).rearrange("p (h d) -> p h d", h=H)).then_inc(b_vh.sem, 1)

                def hi(i):
                    act.wait_ge(b_qn.sem, b_qn.at(b, i + 1))
                    act.copy(hilo[:, i % 3, :, 0, :], rot1[:, i % 3]).then_inc(b_hi.sem, 1)

                def evac(i):
                    act.wait_ge(b_tr.sem, b_tr.at(b, i + 1))
                    dst = (qst, kst)[i % 2]
                    t = i // 2
                    act.copy(dst[:, :, t * P:(t + 1) * P],
                             bank(6, 2).bitcast(BF16).rearrange("p (h s) -> p h s", h=H)).then_inc(b_ev.sem, 1)

                square(0)
                square(1)
                for t in range(T):
                    take_v(t)
                for i in range(10):
                    if 1 <= i < 7:
                        square(i + 1)
                    if 1 <= i < 9:
                        hi(i - 1)
                    if i >= 3:
                        evac(i - 3)
                evac(7)
                act.wait_ge(nmT_ps.sem, nmT_ps.at(b, 2))
                act.copy(nmT[:, :], ps[0:H, 6, :]).then_inc(nmT_ready.sem, 1)
                for h in range(H):
                    act.wait_ge(sc1.sem, sc1.at(b, h + 1))
                    if h >= 2:
                        act.wait_ge(pv1.sem, pv1.at(b, h - 1))
                    src = bank(3 * (h % 2), 3)[:, 0:1280]
                    act.activation(p1_parts[h % 2][:, 0, :], src, ACT.Exp, scale=SCALE1).then_inc(e1.sem, 1)
                    if h >= 1:
                        act.wait_ge(p1_lo.sem, p1_lo.at(b, h))
                    act.activation(p1, src, ACT.Exp, scale=SCALE1).then_inc(e1.sem, 1)
                for t in range(T):
                    act.wait_ge(aoT_ps.sem, aoT_ps.at(b, t + 1))
                    act.copy(aoT[:, t].rearrange("p k s -> p (k s)"), bank(2 * (t % 2), 2))\
                        .then_inc(aoT_ready.sem, 1)

                copy_xnT(3)
                act.copy(xh[:, 0, :], bank(0)).then_inc(xh_hi.sem, 1)
                act.wait_ge(lg_max.sem, lg_max.at(b, 1))
                act.activation(pr[:, :, :], pr[:, :, :], ACT.Exp).then_inc(lg_exp.sem, 1)
                for n in range(NE * FC):
                    act.wait_ge(gu_ps.sem, gu_ps.at(b, n + 1))
                    if n >= 3:
                        act.wait_ge(hact.sem, hact.at(b, n - 2))
                    act.activation(gact[:, n % 3, :], bank(2 * (n % 3)), ACT.Gelu).then_inc(gelu_done.sem, 1)

        @block.tensor
        def _(pe):
            pe.wait_ge(abs_sums.sem, 2)
            pe.wait_ge(set_ones.sem, 1)
            pe.matmul(ps[:, 7, 0:2], onesf[:, :], gam[:, :], start=True, stop=True).then_inc(gam_ready.sem, 1)
            for g in wload:
                pe.wait_ge(wload[g].sem, gcount[g])
            pe.wait_ge(gu_lo.sem, NE)
            pe.wait_ge(quant_done.sem, 2)
            with pe.Fori(0, NSEQ) as b:
                def mm(o, l, r, start=True, stop=True):
                    return pe.matmul(o, l, r, start=start, stop=stop, skip_group_check=True)

                def turn_rows(n):
                    pe.wait_ge(xn_ready.sem, xn_ready.at(b, n + 1))
                    for t in range(T):
                        last = pe.transpose(ps[:, 0, t * P:(t + 1) * P], xn[:, t, :], ident_f)
                    last.then_inc(xnT_ps.sem, 1)
                    pe.wait_ge(xnT_ready.sem, xnT_ready.at(b, n + 1))

                turn_rows(0)
                for g in range(H // G0):
                    for kk, w in enumerate(("wqrep", "wkrep")):
                        mm(bank(2 * g + kk), c[w][:, g * P:(g + 1) * P], xnT[:, :]).then_inc(q0_ps.sem, 1)
                pe.wait_ge(q0_lo.sem, q0_lo.at(b, 1))
                for t in range(T):
                    last = mm(ps[:, 0, t * P:(t + 1) * P], xnT[:, t * P:(t + 1) * P], c["wv"][:, :])
                last.then_inc(va_ps.sem, 1)
                pe.wait_ge(q0_lo.sem, q0_lo.at(b, 2))
                mm(ps[0:LD, 1, :], c["rq_w"][:, :], xnT[:, :]).then_inc(rq_ps.sem, 1)
                pe.wait_ge(q0_lo.sem, q0_lo.at(b, 3))
                pe.wait_ge(pool_ready.sem, pool_ready.at(b, 1))
                mm(ps[0:LD, 2, 0:NLAT], c["rkv_w"][:, 0:LD], pooled2[:, 0, :])
                mm(ps[:, 2, NLAT:NLAT + LD], pooled2.rearrange("p r l -> p (r l)"), c["rkv_w"][:, LD:2 * LD])\
                    .then_inc(rkv_ps.sem, 1)
                pe.wait_ge(rq_ready.sem, rq_ready.at(b, 1))
                pe.wait_ge(rkv_ready.sem, rkv_ready.at(b, 1))
                pe.wait_ge(q0_lo.sem, q0_lo.at(b, 8))
                for t in range(T):
                    last = mm(bank(6, 2)[:, t * 256:(t + 1) * 256], rqT[:, t * P:(t + 1) * P],
                              rkM.rearrange("p h l -> p (h l)"))
                last.then_inc(ls_ps.sem, 1)

                pe.wait_ge(va_ready.sem, va_ready.at(b, 1))

                def rows0(i):
                    g, qb = divmod(i, T)
                    s = i % 3
                    if i >= 3:
                        pe.wait_ge(mx0_done.sem, mx0_done.at(b, i - 2))
                    if i % T == 0:
                        pe.wait_ge(km_ready.sem, km_ready.at(b, G0 * (g + 1)))
                    w, k0 = (P, 0) if qb == 0 else (2 * P, (qb - 1) * P)
                    for half in range(1 if qb == 0 else 2):
                        nh = 512 // w
                        o = ps[:, 2 * s + half, :]
                        mm(o.rearrange("p (h n) -> p h n", h=nh), ident_b,
                           mask_rows[:, 256 - w:256].unsqueeze(1).to_broadcast([P, nh, w]), stop=False)
                        for hh in range(nh):
                            h = G0 * g + nh * half + hh
                            last = mm(o[:, hh * w:(hh + 1) * w], qs[:, g, qb * P:(qb + 1) * P],
                                      km[:, h, k0:k0 + w], start=False)
                    last.then_inc(sr0.sem, 1)

                for i in range(6):
                    rows0(i)
                pe.wait_ge(mx0_done.sem, mx0_done.at(b, 6))
                pe.wait_ge(lp_ready.sem, lp_ready.at(b, 1))
                for cc in range(2):
                    for t in range(T):
                        last = pe.transpose(ps[:, 4 + cc, t * P:(t + 1) * P],
                                            lp[:, t, 2 * cc:2 * cc + 2, :].rearrange("p h l -> p (h l)"), ident_f)
                last.then_inc(lpT_ps.sem, 1)
                pe.wait_ge(lpT_ready.sem, lpT_ready.at(b, 1))
                for cc in range(2):
                    last = mm(ps[0:LD, 6, :], rvM[:, cc, :], lpT[:, cc, :], start=cc == 0, stop=cc == 1)
                last.then_inc(lat_ps.sem, 1)
                pe.wait_ge(lat_ready.sem, lat_ready.at(b, 1))
                for t in range(T):
                    last = mm(ps[:, 7, t * P:(t + 1) * P], latT[:, t * P:(t + 1) * P], c["rout_w"][:, :])
                last.then_inc(rem_ps.sem, 1)
                for i in range(6, 16):
                    rows0(i)

                def turn_max(n):
                    pe.wait_ge(nm_ready.sem, nm_ready.at(b, n + 1))
                    for t in range(T):
                        last = pe.transpose(ps[0:H, 6, t * P:(t + 1) * P], nm[:, t, :], ident_f)
                    last.then_inc(nmT_ps.sem, 1)
                    pe.wait_ge(nmT_ready.sem, nmT_ready.at(b, n + 1))

                turn_max(0)
                pe.wait_ge(rem_ready.sem, rem_ready.at(b, 1))

                def cols0(h):
                    g, s = h // G0, 2 * (h % 3)
                    if h >= 3:
                        pe.wait_ge(e0.sem, e0.at(b, h - 2))
                    o = ps[:, s, :]
                    mm(o.rearrange("p (j n) -> p j n", j=2), ident_b,
                       mask_cols.unsqueeze(1).to_broadcast([P, 2, 256]), stop=False)
                    o = ps[:, s + 1, :]
                    mm(o[:, 0:256], ident_b, mask_cols, stop=False)
                    mm(o[:, 256:384], ident_b, mask_cols[:, 0:P], start=False, stop=False)
                    for j in range(T):
                        o = ps[:, s + j // 2, (j % 2) * 256:(j % 2) * 256 + W0[j]]
                        q = slice(j * P, j * P + W0[j])
                        mm(o, sel_b[:, h, :], nmT[:, q], start=False, stop=False)
                        last = mm(o, km[:, h, j * P:(j + 1) * P], qs[:, g, q], start=False)
                    last.then_inc(sc0.sem, 1)

                def values0(h):
                    g, r = h // G0, 32 * (h % G0)
                    pe.wait_ge(e0.sem, e0.at(b, h + 1))
                    if h % G0 == 0 and g >= 2:
                        pe.wait_ge(o_ev.sem, o_ev.at(b, g - 1))
                    for j in range(T):
                        last = mm(ps[r:r + 32, 6 + g % 2, j * P:j * P + W0[j]], v0[:, j, h, :],
                                  pT0[:, h % 3, OFF0[j]:OFF0[j] + W0[j]], start=j == 0)
                    last.then_inc(pv0.sem, 1)

                for h in range(H):
                    cols0(h)
                    if h >= 1:
                        values0(h - 1)
                values0(H - 1)
                pe.wait_ge(o_ev.sem, o_ev.at(b, H // G0))
                pe.wait_ge(e0.sem, e0.at(b, H))
                for t in range(T):
                    for g in range(H // G0):
                        last = pe.transpose(ps[:, t, g * P:(g + 1) * P], oT[:, g, t * P:(t + 1) * P], ident_f)
                last.then_inc(o_rows.sem, 1)
                pe.wait_ge(mix_ready.sem, mix_ready.at(b, 1))
                for t in range(T):
                    last = pe.transpose(ps[:, 0, t * P:(t + 1) * P], xn[:, t, :], ident_f)
                last.then_inc(mixT_ps.sem, 1)
                pe.wait_ge(mixT_ready.sem, mixT_ready.at(b, 1))
                for t in range(T):
                    last = mm(ps[:, 1, t * P:(t + 1) * P], mixT[:, t * P:(t + 1) * P], c["out_w"][:, :])
                last.then_inc(y_ps.sem, 1)

                turn_rows(1)
                for f in range(FC):
                    mm(bank(1 + f), c["w1"][:, f * P:(f + 1) * P], xnT[:, :]).then_inc(h_ps.sem, 1)
                pe.wait_ge(h_ready.sem, h_ready.at(b, FC))
                for t in range(T):
                    for f in range(FC):
                        last = mm(ps[:, 5, t * P:(t + 1) * P], h0T[:, f, t * P:(t + 1) * P],
                                  c["w2"][:, f * P:(f + 1) * P], start=f == 0, stop=f == FC - 1)
                last.then_inc(y_ps.sem, 1)

                turn_rows(2)

                def turn_parts(i):
                    pe.wait_ge(b_lo.sem, b_lo.at(b, i + 1))
                    if i >= 1:
                        pe.wait_ge(b_ev.sem, b_ev.at(b, i))
                    dst = bank(6, 2).bitcast(BF16)
                    for h in range(H):
                        last = pe.transpose(dst[:, h * P:(h + 1) * P],
                                            hilo[:, i % 3, h].rearrange("p k d -> p (k d)"), ident_b)
                    last.then_inc(b_tr.sem, 1)

                def project(t, kind, first_bank):
                    for n in range(2):
                        col = kind * 1024 + n * 512
                        last = mm(bank(first_bank + n), xnT[:, t * P:(t + 1) * P], c["wqkv1"][:, col:col + 512])
                    return last

                for i in range(2):
                    project(0, i, 2 * i).then_inc(pj.sem, 1)
                for t in range(T):
                    if t >= 2:
                        pe.wait_ge(b_v.sem, b_v.at(b, t - 1))
                    project(t, 2, 4 + 2 * (t % 2)).then_inc(pv_ps.sem, 1)
                for i in range(2, 8):
                    if i >= 3:
                        pe.wait_ge(b_rot.sem, b_rot.at(b, i - 2))
                    else:
                        pe.wait_ge(b_v.sem, b_v.at(b, 3))
                    project(i // 2, i % 2, 2 * (i % 3)).then_inc(pj.sem, 1)
                    if i >= 3:
                        if i == 3:
                            pe.wait_ge(b_v.sem, b_v.at(b, T))
                        turn_parts(i - 3)
                for i in range(5, 8):
                    turn_parts(i)
                pe.wait_ge(b_ev.sem, b_ev.at(b, 8))
                pe.wait_ge(b_rot.sem, b_rot.at(b, 8))

                def rows1(h):
                    s = 3 * (h % 2)
                    if h >= 2:
                        pe.wait_ge(mx1_done.sem, mx1_done.at(b, h - 1))
                    for qb in (3, 2, 1, 0):
                        w = (qb + 1) * P
                        o = ps[:, s + (0, 1, 2, 2)[3 - qb], (256 if qb == 0 else 0):(256 if qb == 0 else 0) + w]
                        mm(o, qst[:, h, qb * P:(qb + 1) * P], kst[:, h, 0:w], stop=False)
                        last = mm(o[:, w - P:w], ident_b, cmask_rows, start=False)
                    last.then_inc(sr1.sem, 1)

                for h in range(H):
                    rows1(h)
                turn_max(1)
                pe.wait_ge(k_swapped.sem, k_swapped.at(b, 32))

                def cols1(h):
                    s = 3 * (h % 2)
                    if h >= 2:
                        pe.wait_ge(e1.sem, e1.at(b, 2 * (h - 1)))
                    for j in range(T):
                        w = S - j * P
                        o = bank(s, 3)[:, OFF1[j]:OFF1[j] + w]
                        k = slice(j * P, (j + 1) * P)
                        q = slice(j * P, S)
                        mm(o, kst[:, h, k], qst[:, h, q], stop=False)
                        mm(o, kst2[:, h, k], qst[:, h, q], start=False, stop=False)
                        mm(o, sel_b[:, h, :], nmT[:, q], start=False, stop=False)
                        last = mm(o[:, 0:P], ident_b, cmask_cols, start=False)
                    last.then_inc(sc1.sem, 1)

                def values1(h):
                    pe.wait_ge(p1_lo.sem, p1_lo.at(b, h + 1))
                    if h >= 2:
                        pe.wait_ge(ao_done.sem, ao_done.at(b, h - 1))
                    part = p1_parts[h % 2]
                    for qb in range(T):
                        o = ps[:, 6 + h % 2, 65 * qb:65 * qb + 65]
                        for j in range(qb + 1):
                            a = OFF1[j] + (qb - j) * P
                            mm(o, part[:, 0, a:a + P], v1[:, j, h, 0, :], start=j == 0, stop=False)
                            mm(o, part[:, 0, a:a + P], v1[:, j, h, 1, :], start=False, stop=False)
                            last = mm(o, part[:, 1, a:a + P], v1[:, j, h, 0, :], start=False, stop=j == qb)
                    last.then_inc(pv1.sem, 1)

                for h in range(H):
                    cols1(h)
                    if h >= 1:
                        values1(h - 1)
                values1(H - 1)
                pe.wait_ge(ao_done.sem, ao_done.at(b, H))
                for t in range(T + 1):
                    if t < T:
                        if t >= 2:
                            pe.wait_ge(aoT_ready.sem, aoT_ready.at(b, t - 1))
                        for k in range(8):
                            last = pe.transpose(bank(2 * (t % 2), 2)[:, k * P:(k + 1) * P],
                                                ao[:, t, k * P:(k + 1) * P], ident_f)
                        last.then_inc(aoT_ps.sem, 1)
                    if t >= 1:
                        pe.wait_ge(aoT_ready.sem, aoT_ready.at(b, t))
                        for k in range(8):
                            last = mm(ps[:, 4, (t - 1) * P:t * P], aoT[:, t - 1, k, :],
                                      c["wo1"][:, k * P:(k + 1) * P], start=k == 0, stop=k == 7)
                last.then_inc(y_ps.sem, 1)

                turn_rows(3)
                for t in range(T):
                    last = mm(ps[:, 7, t * NE:(t + 1) * NE], xnT[:, t * P:(t + 1) * P], c["gate_w"][:, :])
                last.then_inc(lg_ps.sem, 1)
                pe.wait_ge(xh_lo.sem, xh_lo.at(b, 1))

                def down(e):
                    pe.wait_ge(hact.sem, hact.at(b, FC * (e + 1)))
                    if e >= 2:
                        pe.wait_ge(dn_read.sem, dn_read.at(b, e - 1))
                    if e == 1:
                        pe.wait_ge(lg_max.sem, lg_max.at(b, 1))
                    for t in range(T):
                        for f in range(FC):
                            last = mm(ps[:, 6 + e % 2, t * P:(t + 1) * P], hT[:, e % 2, f, t * P:(t + 1) * P],
                                      c["down"][:, e, f, :], start=f == 0, stop=f == FC - 1)
                    last.then_inc(dn_ps.sem, 1)

                for e in range(NE):
                    for f in range(FC):
                        n = e * FC + f
                        if n >= 3:
                            pe.wait_ge(hact.sem, hact.at(b, n - 2))
                        for k in range(2):
                            w = slice(k * FE + f * P, k * FE + (f + 1) * P)
                            o = bank(2 * (n % 3) + k)
                            mm(o, gu_b[:, 0, e, w], xh[:, 0, :], stop=False)
                            mm(o, gu_b[:, 1, e, w], xh[:, 0, :], start=False, stop=False)
                            last = mm(o, gu_b[:, 0, e, w], xh[:, 1, :], start=False)
                        last.then_inc(gu_ps.sem, 1)
                    if e >= 1:
                        down(e - 1)
                down(NE - 1)

        @block.vector
        def _(dve):
            n = [0]

            def s_step(i):
                n[0] += 1
                i.then_inc(setup_step.sem, 1)
                dve.wait_ge(setup_step.sem, n[0])

            dve.memset(x_out[:, 0, 0:1], 0.0).then_inc(x_out_free.sem, 1)
            dve.memset(v0[:, :, :, HD0:HD0 + 1], 1.0)
            dve.memset(v0[:, :, :, HD0 + 1:], 0.0)
            dve.memset(v1[:, :, :, 0, HD1:HD1 + 1], 1.0)
            dve.memset(v1[:, :, :, 1, HD1:HD1 + 1], 0.0)
            dve.memset(onesf[:, :], 1.0).then_inc(set_ones.sem, 1)
            dve.wait_ge(gam_ready.sem, 1)
            s_step(dve.tensor_scalar(thr[:, 2:4], ps[:, 7, 0:2], 1.0 / (D * FF), Q_EPS, ALU.mult, ALU.add))
            s_step(dve.tensor_scalar(thr[:, 0:2], thr[:, 2:4], 0.5, None, ALU.mult))
            s_step(dve.tensor_scalar(thr[:, 2:4], thr[:, 0:2], -1.0, None, ALU.mult))
            for k, w in enumerate(("w1", "w2")):
                s_step(dve.tensor_scalar(qtmp, c[w][:, :], thr[:, 2 + k:3 + k], None, ALU.is_lt))
                s_step(dve.scalar_tensor_tensor(out=c[w][:, :], in0=c[w][:, :], scalar=thr[:, k:k + 1],
                                                in1=qtmp, op0=ALU.is_gt, op1=ALU.subtract))
            dve.wait_ge(wload["attn1"].sem, gcount["attn1"])
            half = HD1 // 2
            for k in range(2):
                w = c["qkn"][:, k, :]
                for t in range(T):
                    dve.tensor_tensor(csq[:, k, 0, t, :], c["cs"][:, 0, t, :], w, ALU.mult)
                    dve.tensor_tensor(csq[:, k, 1, t, 0:half], c["cs"][:, 1, t, 0:half], w[:, half:HD1], ALU.mult)
                    last = dve.tensor_tensor(csq[:, k, 1, t, half:HD1], c["cs"][:, 1, t, half:HD1],
                                             w[:, 0:half], ALU.mult)
            last.then_inc(quant_done.sem, 1)
            for g in ("qkv", "lat", "gate", "exp"):
                dve.wait_ge(wload[g].sem, gcount[g])
            dve.tensor_copy(ident_b_t[:, :], ident_f)
            dve.tensor_copy(masks_b[:, :], c["masks"])
            dve.tensor_copy(sel_b[:, :, :].rearrange("r h p -> r (h p)"), c["sel"]).then_inc(quant_done.sem, 1)
            dve.wait_ge(quant_done.sem, 2)
            for e in range(NE):
                dve.wait_ge(gu_hi.sem, e + 1)
                dve.tensor_tensor(gu_b[:, 1, e, :], c["gu"][:, e, :], gu_b[:, 0, e, :], ALU.subtract)\
                    .then_inc(gu_lo.sem, 1)
            dve.wait_ge(gu_lo.sem, NE)

            with dve.Fori(0, NSEQ) as b:
                step_no, norm_no = [0], [0]

                def step(i):
                    step_no[0] += 1
                    i.then_inc(vec.sem, 1)
                    dve.wait_ge(vec.sem, vec.at(b, step_no[0]))

                def stats(src):
                    for t in range(T):
                        last = dve.bn_stats(bst[:, t, :], src[:, t, :])
                    step(last)
                    dve.memset(ve[:, :], 0.0)
                    for t in range(T):
                        last = dve.bn_aggr(mv[:, t, :], bst[:, t, :])
                    step(last)
                    dve.tensor_scalar(ve[:, :], mv[:, :, 1], LN_EPS, None, ALU.add).then_inc(var_ready.sem, 1)
                    norm_no[0] += 1
                    dve.wait_ge(rstd_ready.sem, rstd_ready.at(b, norm_no[0]))

                def norm_in():
                    stats(x)
                    for t in range(T):
                        last = dve.tensor_scalar(xn[:, t, :], x[:, t, :], mv[:, t, 0:1], rstd[:, t:t + 1],
                                                 ALU.subtract, ALU.mult)
                    last.then_inc(xn_ready.sem, 1)

                def norm_out(dst):
                    stats(y)
                    for t in range(T):
                        last = dve.tensor_scalar(xn[:, t, :], y[:, t, :], mv[:, t, 0:1], rstd[:, t:t + 1],
                                                 ALU.subtract, ALU.mult)
                    step(last)
                    return dve.tensor_tensor(dst[:, :, :], x[:, :, :], xn[:, :, :], ALU.add)

                def rows(bk):
                    return bank(bk).rearrange("p (t d) -> p t d", t=T)

                def over_tiles(w):
                    return w.unsqueeze(1).to_broadcast([P, T, D])

                dve.wait_ge(x_loaded.sem, x_loaded.at(b, 16))
                dve.tensor_copy(x[:, :, :], x_in[:, :, :]).then_inc(x_taken.sem, 1)
                dve.wait_ge(x_taken.sem, x_taken.at(b, 1))

                norm_in()
                dve.wait_ge(xnT_ready.sem, xnT_ready.at(b, 1))
                step(dve.tensor_reduce(psumf, xnT[:, :].rearrange("p (l c) -> p l c", c=CHUNK), X, ALU.add))
                dve.tensor_scalar(pooled2[:, 0, :], psumf, 1.0 / CHUNK, None, ALU.mult)
                dve.tensor_scalar(pooled2[:, 1, :], psumf, 1.0 / CHUNK, None, ALU.mult).then_inc(pool_ready.sem, 1)
                for g in range(H // G0):
                    for kk, dst in enumerate((qs, ks)):
                        i = 2 * g + kk
                        dve.wait_ge(q0_hi.sem, q0_hi.at(b, i + 1))
                        for r0, r1_ in (((64, 128),) if kk == 0 else ((32, 64), (64, 96))):
                            last = dve.scalar_tensor_tensor(
                                out=dst[r0:r1_, g, :], in0=ps[r0:r1_, i, :], scalar=c["bqk"][r0:r1_, i:i + 1],
                                in1=dst[r0:r1_, g, :], op0=ALU.add, op1=ALU.subtract)
                        last.then_inc(q0_lo.sem, 1)
                    dve.wait_ge(q0_lo.sem, q0_lo.at(b, 2 * g + 2))
                    for hh in range(G0):
                        dve.tensor_scalar(km[:, G0 * g + hh, :], ks[:, g, :], hmask[:, hh:hh + 1], None, ALU.mult)\
                            .then_inc(km_ready.sem, 1)
                dve.wait_ge(rkv_ps.sem, rkv_ps.at(b, 1))
                for hh in range(LH):
                    dve.tensor_scalar(rkM[:, hh, :], ps[0:LD, 2, 0:NLAT], c["rk_b"][:, 0:1], lhmask[:, hh:hh + 1],
                                      ALU.add, ALU.mult)
                step(dve.tensor_tensor(rvb, ps[:, 2, NLAT:NLAT + LD], c["rv_b"][:, :], ALU.add))
                dve.tensor_tensor(rvM, rvb.unsqueeze(1).to_broadcast([P, 2, LD]), bdmask, ALU.mult)\
                    .then_inc(rkv_ready.sem, 1)
                dve.wait_ge(va_ps.sem, va_ps.at(b, 1))
                for t in range(T):
                    last = dve.tensor_tensor(v0[:, t, :, 0:HD0],
                                             ps[:, 0, t * P:(t + 1) * P].rearrange("p (h d) -> p h d", h=H),
                                             c["bv"][:, :].rearrange("p (h d) -> p h d", h=H), ALU.add)
                last.then_inc(va_ready.sem, 1)
                dve.wait_ge(ls_ps.sem, ls_ps.at(b, 1))
                lsc = bank(6, 2).rearrange("p (t h l) -> p t h l", t=T, h=LH)
                for t in range(T):
                    last = dve.tensor_tensor(lp[:, t], lsc[:, t],
                                             c["lmask"][:, t, :].unsqueeze(1).to_broadcast([P, LH, NLAT]), ALU.add)
                step(last)
                step(dve.tensor_reduce(lmx[:, :, :], lp, X, ALU.max))
                step(dve.tensor_scalar(lmx[:, :, :], lmx[:, :, :], -CLAMP, None, ALU.max))
                lpf = lp.rearrange("p t h l -> p (t h) l")

                def lat_bc(a):
                    return a[:, :, :].rearrange("p t h -> p (t h)").unsqueeze(2).to_broadcast([P, T * LH, NLAT])

                dve.tensor_tensor(lpf, lpf, lat_bc(lmx), ALU.subtract).then_inc(ls_ready.sem, 1)

                def max0(i):
                    g, qb = divmod(i, T)
                    s = 2 * (i % 3)
                    dve.wait_ge(sr0.sem, sr0.at(b, i + 1))
                    w = P if qb == 0 else 2 * P
                    src = bank(s, 2)[:, 0:G0 * w].rearrange("p (h n) -> p h n", h=G0)
                    dve.tensor_reduce(mx0[:, qb, G0 * g:G0 * g + G0], src, X, ALU.max).then_inc(mx0_done.sem, 1)

                for i in range(3):
                    max0(i)
                dve.wait_ge(lexp.sem, lexp.at(b, 1))
                step(dve.tensor_reduce(lsum[:, :, :], lp, X, ALU.add))
                step(dve.tensor_scalar(lsum[:, :, :], lsum[:, :, :], 1e-30, None, ALU.max))
                step(dve.reciprocal(lsum[:, :, :], lsum[:, :, :]))
                dve.tensor_tensor(lpf, lpf, lat_bc(lsum), ALU.mult).then_inc(lp_ready.sem, 1)
                for i in range(3, 6):
                    max0(i)
                dve.wait_ge(rem_ps.sem, rem_ps.at(b, 1))
                dve.tensor_tensor(remote, rows(7), over_tiles(c["rout_b"][:, :]), ALU.add)\
                    .then_inc(rem_ready.sem, 1)
                for i in range(6, 16):
                    max0(i)
                dve.wait_ge(mx0_done.sem, mx0_done.at(b, 16))
                dve.tensor_scalar(nm[:, :, :], mx0[:, :, :], -1.0, CLAMP, ALU.mult, ALU.min)\
                    .then_inc(nm_ready.sem, 1)

                def heads(a):
                    return a.rearrange("p t (h d) -> p (t h) d", h=H)

                def head_bc(a):
                    return a.rearrange("p t h -> p (t h)").unsqueeze(2).to_broadcast([P, T * H, HD0])

                dve.wait_ge(rem_ready.sem, rem_ready.at(b, 1))
                step(dve.tensor_tensor(heads(gtmp), heads(remote),
                                       c["glr"][:, 1, :].unsqueeze(1).to_broadcast([P, T * H, HD0]), ALU.mult))
                step(dve.tensor_reduce(gz2[:, :, :].rearrange("p t h -> p (t h)"), heads(gtmp), X, ALU.add))
                for g in range(H // G0):
                    dve.wait_ge(pv0.sem, pv0.at(b, G0 * (g + 1)))
                    dve.tensor_copy(oT[:, g, :], bank(6 + g % 2)).then_inc(o_ev.sem, 1)
                dve.wait_ge(o_rows.sem, o_rows.at(b, 1))
                orow = bank(0, 4).rearrange("p (k d) -> p k d", d=32)
                rd = rden[:, :, :].rearrange("p t h -> p (t h)")
                step(dve.tensor_scalar(rd, orow[:, :, HD0], 1e-30, None, ALU.max))
                step(dve.reciprocal(rd, rd))
                last = dve.tensor_tensor(heads(local), orow[:, :, 0:HD0], head_bc(rden[:, :, :]), ALU.mult)
                step(last)
                step(dve.tensor_tensor(heads(gtmp), heads(local),
                                       c["glr"][:, 0, :].unsqueeze(1).to_broadcast([P, T * H, HD0]), ALU.mult))
                step(dve.tensor_reduce(gz[:, :, :].rearrange("p t h -> p (t h)"), heads(gtmp), X, ALU.add))
                dve.tensor_tensor(gz[:, :, :], gz[:, :, :], gz2[:, :, :], ALU.add).then_inc(gz_ready.sem, 1)
                step(dve.tensor_tensor(local, local, remote, ALU.subtract))
                dve.wait_ge(gexp.sem, gexp.at(b, 1))
                step(dve.tensor_scalar(gz2[:, :, :], gz2[:, :, :], 1.0, None, ALU.add))
                step(dve.reciprocal(gz2[:, :, :], gz2[:, :, :]))
                step(dve.tensor_tensor(heads(local), heads(local), head_bc(gz2[:, :, :]), ALU.mult))
                dve.tensor_tensor(xn[:, :, :], local, remote, ALU.add).then_inc(mix_ready.sem, 1)

                def finish(n, bk, bias, dst):
                    dve.wait_ge(y_ps.sem, y_ps.at(b, n + 1))
                    if bias is None:
                        i = dve.tensor_copy(y[:, :, :], rows(bk))
                    else:
                        i = dve.tensor_tensor(y[:, :, :], rows(bk), over_tiles(bias), ALU.add)
                    step(i)
                    step(norm_out(dst))

                finish(0, 1, c["out_b"][:, :], x)
                norm_in()
                finish(1, 5, c["b2"][:, :], x)
                norm_in()

                def rotate(i):
                    t, kk = divmod(i, 2)
                    if i >= 3:
                        dve.wait_ge(b_lo.sem, b_lo.at(b, i - 2))
                    dve.wait_ge(b_sq.sem, b_sq.at(b, i + 1))
                    src = bank(2 * (i % 3), 2).rearrange("p (h d) -> p h d", h=H)

                    def tab(k, lo, hi_):
                        return csq[:, kk, k, t, lo:hi_].unsqueeze(1).to_broadcast([P, H, hi_ - lo])

                    dve.tensor_tensor(rot1[:, i % 3], src, tab(0, 0, HD1), ALU.mult)
                    dve.tensor_tensor(rot2[:, i % 2, :, 0:half], src[:, :, half:HD1], tab(1, 0, half), ALU.mult)
                    dve.tensor_tensor(rot2[:, i % 2, :, half:HD1], src[:, :, 0:half], tab(1, half, HD1), ALU.mult)\
                        .then_inc(b_rot.sem, 1)
                    step(dve.tensor_reduce(ve1[:, i % 2, :], sq[:, i % 2], X, ALU.add))
                    dve.tensor_scalar(ve1[:, i % 2, :], ve1[:, i % 2, :], 1.0 / HD1, RMS_EPS, ALU.mult, ALU.add)\
                        .then_inc(var_ready.sem, 1)

                def scale(i):
                    dve.wait_ge(b_sum.sem, b_sum.at(b, i + 1))
                    dve.wait_ge(rstd_ready.sem, rstd_ready.at(b, 5 + i + 1))
                    dve.tensor_tensor(rot1[:, i % 3], rot1[:, i % 3],
                                      rinv[:, i % 2, :].unsqueeze(2).to_broadcast([P, H, HD1]), ALU.mult)\
                        .then_inc(b_qn.sem, 1)

                def low_part(i):
                    dve.wait_ge(b_hi.sem, b_hi.at(b, i + 1))
                    dve.tensor_tensor(hilo[:, i % 3, :, 1, :], rot1[:, i % 3], hilo[:, i % 3, :, 0, :], ALU.subtract)\
                        .then_inc(b_lo.sem, 1)

                def v_low(t):
                    dve.wait_ge(b_vh.sem, b_vh.at(b, t + 1))
                    dve.tensor_tensor(v1[:, t, :, 1, 0:HD1],
                                      bank(4 + 2 * (t % 2), 2).rearrange("p (h d) -> p h d", h=H),
                                      v1[:, t, :, 0, 0:HD1], ALU.subtract).then_inc(b_v.sem, 1)

                for i in range(10):
                    if i < 8:
                        rotate(i)
                    if i == 0:
                        for t in range(T):
                            v_low(t)
                    if i >= 2:
                        low_part(i - 2)
                    if 1 <= i < 9:
                        scale(i - 1)
                norm_no[0] += 8
                for h in range(H):
                    s = 3 * (h % 2)
                    dve.wait_ge(sr1.sem, sr1.at(b, h + 1))
                    for qb in (3, 2, 1, 0):
                        w = (qb + 1) * P
                        a = 256 if qb == 0 else 0
                        last = dve.tensor_reduce(mx0[:, qb, h:h + 1], ps[:, s + (0, 1, 2, 2)[3 - qb], a:a + w],
                                                 X, ALU.max)
                    last.then_inc(mx1_done.sem, 1)
                dve.wait_ge(mx1_done.sem, mx1_done.at(b, H))
                dve.tensor_scalar(nm[:, :, :], mx0[:, :, :], -1.0, None, ALU.mult).then_inc(nm_ready.sem, 1)
                for h in range(H + 1):
                    if h < H:
                        dve.wait_ge(e1.sem, e1.at(b, 2 * h + 2))
                        dve.tensor_tensor(p1_parts[h % 2][:, 1, :], p1, p1_parts[h % 2][:, 0, :], ALU.subtract)\
                            .then_inc(p1_lo.sem, 1)
                    if h >= 1:
                        k = h - 1
                        dve.wait_ge(pv1.sem, pv1.at(b, k + 1))
                        src = ps[:, 6 + k % 2, 0:260].rearrange("p (t d) -> p t d", t=T)
                        step(dve.reciprocal(r1[:, k % 2, :], src[:, :, HD1]))
                        dve.tensor_tensor(ao[:, :, k * HD1:(k + 1) * HD1], src[:, :, 0:HD1],
                                          r1[:, k % 2, :].unsqueeze(2).to_broadcast([P, T, HD1]), ALU.mult)\
                            .then_inc(ao_done.sem, 1)
                finish(2, 4, None, x)

                norm_in()
                dve.wait_ge(xh_hi.sem, xh_hi.at(b, 1))
                dve.tensor_tensor(xh[:, 1, :], xnT[:, :], xh[:, 0, :], ALU.subtract).then_inc(xh_lo.sem, 1)
                dve.wait_ge(lg_ps.sem, lg_ps.at(b, 1))
                lg = ps[:, 7, 0:T * NE].rearrange("p (t e) -> p t e", t=T)

                def tok_bc(a):
                    return a.unsqueeze(2).to_broadcast([P, T, NE])

                step(dve.tensor_reduce(r4[:, :], lg, X, ALU.max))
                dve.tensor_tensor(pr[:, :, :], lg, tok_bc(r4[:, :]), ALU.subtract).then_inc(lg_max.sem, 1)
                dve.wait_ge(lg_exp.sem, lg_exp.at(b, 1))
                step(dve.tensor_reduce(r4[:, :], pr[:, :, :], X, ALU.add))
                step(dve.reciprocal(r4[:, :], r4[:, :]))
                step(dve.tensor_tensor(pr[:, :, :], pr[:, :, :], tok_bc(r4[:, :]), ALU.mult))
                for t in range(T):
                    other = pr[:, t, :].unsqueeze(1).to_broadcast([P, NE, NE])
                    mine = pr[:, t, :].unsqueeze(2).to_broadcast([P, NE, NE])
                    dve.tensor_tensor(cmp1[:, t], other, mine, ALU.is_gt)
                    last = dve.tensor_tensor(cmp2[:, t], other, mine, ALU.is_equal)
                step(last)
                tri = c["tri"][:, :].unsqueeze(1).to_broadcast([P, T, NE * NE])
                step(dve.tensor_tensor(cmp2[:, :, :, :].rearrange("p t a e -> p t (a e)"),
                                       cmp2[:, :, :, :].rearrange("p t a e -> p t (a e)"), tri, ALU.mult))
                step(dve.tensor_tensor(cmp1[:, :, :, :], cmp1[:, :, :, :], cmp2[:, :, :, :], ALU.add))
                step(dve.tensor_reduce(comb[:, :, :], cmp1[:, :, :, :], X, ALU.add))
                step(dve.scalar_tensor_tensor(out=comb[:, :, :], in0=comb[:, :, :], scalar=2.0, in1=pr[:, :, :],
                                              op0=ALU.is_lt, op1=ALU.mult))
                step(dve.tensor_reduce(r4[:, :], comb[:, :, :], X, ALU.add))
                step(dve.reciprocal(r4[:, :], r4[:, :]))
                step(dve.tensor_tensor(comb[:, :, :], comb[:, :, :], tok_bc(r4[:, :]), ALU.mult))

                def combine(e):
                    dve.wait_ge(dn_ps.sem, dn_ps.at(b, e + 1))
                    if e:
                        dve.wait_ge(dn_read.sem, dn_read.at(b, e))
                    for t in range(T):
                        o = ps[:, 6 + e % 2, t * P:(t + 1) * P]
                        if e == 0:
                            last = dve.tensor_scalar(acc[:, t, :], o, comb[:, t, e:e + 1], None, ALU.mult)
                        else:
                            last = dve.scalar_tensor_tensor(out=acc[:, t, :], in0=o, scalar=comb[:, t, e:e + 1],
                                                            in1=acc[:, t, :], op0=ALU.mult, op1=ALU.add)
                    last.then_inc(dn_read.sem, 1)

                for e in range(NE):
                    for f in range(FC):
                        k = e * FC + f
                        dve.wait_ge(gelu_done.sem, gelu_done.at(b, k + 1))
                        if e >= 2 and f == 0:
                            dve.wait_ge(dn_ps.sem, dn_ps.at(b, e - 1))
                        dve.tensor_tensor(hT[:, e % 2, f, :], gact[:, k % 3, :], bank(2 * (k % 3) + 1), ALU.mult)\
                            .then_inc(hact.sem, 1)
                    if e >= 1:
                        combine(e - 1)
                combine(NE - 1)
                dve.wait_ge(dn_read.sem, dn_read.at(b, NE))
                dve.wait_ge(x_out_free.sem, x_out_free.at(b, 1))
                norm_out(x_out).then_inc(x_final.sem, 1)
                dve.wait_ge(x_final.sem, x_final.at(b, 1))
                assert step_no[0] == VEC_STEPS, step_no[0]


_CONST = {}


def constants():
    i = np.arange(P)
    small = np.zeros((P, 88), np.float32)
    small[:, 0:4] = (i[:, None] % 32) // 8 == np.arange(4)
    small[:LD, 4:8] = i[:LD, None] // 8 == np.arange(4)
    col = np.arange(2 * LD)
    small[:, 8:72] = (col[None, :] % LD) // LHD == 2 * (col[None, :] // LD) + i[:, None] // 64
    small[:, 72:] = -0.5
    a, k = i[:, None], i[None, :]
    masks = np.zeros((P, 768), np.float32)
    masks[:, 0:128] = np.where(k >= a, 0, NEG)
    masks[:, 128:256] = np.where(k < a, 0, NEG)
    masks[:, 256:384] = np.where(k > a, 0, NEG)
    masks[:, 384:512] = np.where(k <= a, 0, NEG)
    masks[:, 512:640] = np.where(k <= a, 0, NEG1)
    masks[:, 640:768] = np.where(k >= a, 0, NEG1)
    sel = np.zeros((H, H, P), np.float32)
    sel[np.arange(H), np.arange(H), :] = 1
    tok = (np.arange(T)[None, :] * P + i[:, None])
    lmask = np.where(np.arange(NLAT)[None, None, :] < (tok // CHUNK)[:, :, None], 0, NEG).astype(np.float32)
    inv = (1.0 / np.float32(10000.0) ** (np.arange(0, HD1, 2, dtype=np.float32) / np.float32(HD1))).astype(np.float32)
    fr = (np.arange(S, dtype=np.float32)[:, None] * inv).astype(np.float32)
    cos, sin = np.cos(fr), np.sin(fr)
    cs = np.stack([np.concatenate([cos, cos], 1), np.concatenate([-sin, sin], 1)])
    cs = cs.reshape(2, T, P, HD1).transpose(2, 0, 1, 3)
    e = np.arange(NE)
    tri = np.broadcast_to((e[None, :] < e[:, None]).reshape(1, -1), (P, NE * NE))
    return {"ident_f": np.eye(P, dtype=np.float32), "small": small,
            "masks": masks, "sel": sel.reshape(H, H * P), "lmask": lmask, "cs": cs.astype(np.float32),
            "tri": tri.astype(np.float32)}


def kernel(**inputs):
    import concourse.bacc as bacc
    from concourse.bass_utils import run_bass_kernel_spmd as run

    w = {k: np.asarray(v) for k, v in inputs.items()}

    def rows(v):
        return np.broadcast_to(v.reshape(1, -1), (P, v.size))

    def slots(m):
        return np.concatenate([np.tile(m[..., 32 * g:32 * g + 32], 4) for g in range(4)], -1)

    qkv, qb = w["L0_attn_qkv_w"], w["L0_attn_qkv_b"]
    bq, bk = slots(qb[0:D]).reshape(4, P), slots(qb[D:2 * D]).reshape(4, P)
    a = dict(constants())
    a.update({
        "x": w["L0_attn_x"].reshape(NSEQ * S, D),
        "wqrep": slots(qkv[:, 0:D]), "wkrep": slots(qkv[:, D:2 * D]), "wv": qkv[:, 2 * D:],
        "bqk": np.stack([bq, bk], 1).reshape(8, P).T, "bv": rows(qb[2 * D:]),
        "rq_w": w["L0_attn_rq_w"], "rq_b": w["L0_attn_rq_b"].reshape(LD, 1),
        "rkv_w": w["L0_attn_rkv_w"], "rk_b": w["L0_attn_rkv_b"][:LD].reshape(LD, 1),
        "rv_b": rows(w["L0_attn_rkv_b"][LD:]),
        "rout_w": w["L0_attn_rout_w"], "rout_b": rows(w["L0_attn_rout_b"]),
        "out_w": w["L0_attn_out_w"], "out_b": rows(w["L0_attn_out_b"]),
        "glr": np.broadcast_to(np.stack([w["L0_attn_gl_w"].ravel(), w["L0_attn_gr_w"].ravel()])[None],
                               (P, 2, HD0)),
        "w1": w["L0_ffn_W1"].T, "b1": w["L0_ffn_b1"].reshape(FC, P).T,
        "w2": w["L0_ffn_W2"].T.reshape(FC, P, D).transpose(1, 0, 2).reshape(P, FC * D),
        "b2": rows(w["L0_ffn_b2"]),
        "qkn": np.broadcast_to(np.stack([w["L1_attn_q_norm_w"], w["L1_attn_k_norm_w"]])[None], (P, 2, HD1)),
        "wqkv1": w["L1_attn_wqkv"].T,
        "wo1": w["L1_attn_wo"].T.reshape(8, P, D).transpose(1, 0, 2).reshape(P, 8 * D),
        "gate_w": w["L1_ffn_gate_w"].T,
        "gu": w["L1_ffn_gate_up_w"].transpose(2, 0, 1),
        "down": w["L1_ffn_down_w"].transpose(2, 0, 1).reshape(FC, P, NE, D).transpose(1, 2, 0, 3),
    })
    nc = bacc.Bacc("TRN2", target_bir_lowering=False, num_devices=1)
    arrays, ins = {}, {}
    for name, v in a.items():
        v = np.ascontiguousarray(v)
        arrays["in_" + name] = v
        ins[name] = nc.dram_tensor("in_" + name, v.shape, mybir.dt.from_np(v.dtype), kind="ExternalInput").ap()
    out = nc.dram_tensor("out_0", (NSEQ * S, D), F32, kind="ExternalOutput").ap()
    build(nc, ins, out)
    r = run(nc, [arrays], core_ids=[0])
    return r.results[0]["out_0"].reshape(NSEQ, S, D)
```

```python
from contextlib import ExitStack

import numpy as np

import concourse.bass as bass
from concourse import mybir

F32 = mybir.dt.float32
BF16 = mybir.dt.bfloat16
ALU = mybir.AluOpType
ACT = mybir.ActivationFunctionType
X = mybir.AxisListType.X

P = 128
NSEQ, S, D = 8, 512, 128
T = S // P
H = 16
HD0, HD1 = D // H, 64
G0 = 4
NLAT, LH, LHD, LD = 64, 4, 8, 32
CHUNK = S // NLAT
FF = 512
NE, FE = 8, 512
FC = FF // P
NEG = -1.0e9
NEG1 = -1.0e30
CLAMP = 1.0e8
LN_EPS, RMS_EPS, Q_EPS = 1e-5, 1e-6, 1e-5
SCALE0 = float(1.0 / np.sqrt(HD0))
SCALEL = float(1.0 / np.sqrt(LHD))
SCALE1 = float(HD1 ** -0.5)
W0 = (256, 256, 256, 128)
OFF0 = (0, 256, 512, 768)
OFF1 = (0, 512, 1024, 896)
ROW_UNITS = (((0, 3, 0),), ((0, 2, 0), (0, 0, 384)), ((1, 3, 0),), ((1, 2, 0), (1, 0, 384)), ((0, 1, 0), (1, 1, 256)))
AO_HEAD = (8, 9, 10, 11, 12, 14)
AO_BANK = (5, 7, 5, 7, 5, 7, 5, 5)
ROWS_HALF = 5 * H // 4
VEC_STEPS = 64
MVEC_STEPS = 17
PLAN = {"start": [1], "turned": [0], "heads": [0, 1, 1, 1], "latent": [3], "maxima": [0, 1, 0, 1, 1, 0, 1, 1, 1, 0, 1, 1, 0, 1, 1, 0],
        "shift": [2], "banded": [0] * 16, "gate": [1, 1, 2], "norms": [2] * 8, "mlp": [1, 1, 1], "causal": [1],
        "values": [1] * 4, "parts": [1, 0] + [1, 1] * 9, "rows": [2, 2, 1, 1], "end": [99]}
HALVES = 2 * NE * FC
ROUTER = (4, 5, 6, 8)
PIECES = 4 + HALVES + 2 + 2


class Sig:

    def __init__(self, ctx, nc, name, per_turn, before=0):
        self.sem = ctx.enter_context(nc.semaphore(name))
        self.n = per_turn
        self.before = before

    def at(self, b, k):
        return b * self.n + (k + self.before)


def build(nc, ins, out):
    ctx = ExitStack()
    with ctx:
        def sb(name, shape, dt=F32):
            return ctx.enter_context(nc.sbuf_tensor(name, shape, dt))

        def sig(name, n, before=0):
            return Sig(ctx, nc, name, n, before)

        loaded = {}
        order = ["ident_f", "wqrep", "wkrep", "bqk", "wv", "bv", "rq_w", "rq_b", "rkv_w", "rk_b", "rv_b",
                 "small", "lmask", "rout_w", "rout_b", "out_w", "out_b", "glr",
                 "w1", "b1", "w2", "b2", "wqkv1", "wo1", "gate_w", "tri", "down", "masks", "cs", "qkn", "gu"]
        for name in order[:-4]:
            loaded[name] = sb("c_" + name, list(ins[name].shape))
        c = loaded
        ident_f = c["ident_f"][:, :]
        ident_b_t = sb("ident_b", [P, P], BF16)
        masks_b = sb("masks_b", [P, 768], BF16)
        ident_b = ident_b_t[:, :]
        hmask = c["small"][:, 0:4]
        lhmask = c["small"][0:LD, 4:8]
        bdmask = c["small"][:, 8:8 + 2 * LD].rearrange("p (c d) -> p c d", c=2)
        mhalf = c["small"][:, 72:88]
        onesf = sb("onesf", [P, P])
        mask_rows, mask_cols = masks_b[:, 0:256], masks_b[:, 256:512]
        cmask_rows, cmask_cols = masks_b[:, 512:640], masks_b[:, 640:768]

        gu_b = sb("gu_b", [P, 2, NE, 2 * FE], BF16)
        xh = sb("xh", [P, 2, S], BF16)
        x_in = sb("x_in", [P, T, D])
        x = sb("x", [P, T, D])
        norm = sb("norm", [P, 3 * T * D])
        xn = norm[:, 0:512].rearrange("p (t d) -> p t d", t=T)
        y = norm[:, 512:1024].rearrange("p (t d) -> p t d", t=T)
        xnT = norm[:, 1024:1536]
        bst = sb("bst", [P, T, 6])
        mv = sb("mv", [P, T, 2])
        ve = sb("ve", [P, T])
        rstd = sb("rstd", [P, T])

        region = sb("region", [P, 12 * 1024])
        region2 = sb("region2", [P, 7 * 1024])
        rb = region[:, :].bitcast(BF16)
        c["masks"] = region2[:, 1024:1792]
        c["gu"] = region[:, 0:8192].rearrange("p (e n) -> p e n", e=NE)
        c["cs"] = region2[:, 4096:4608].rearrange("p (k t d) -> p k t d", k=2, t=T)
        c["qkn"] = region2[:, 4608:4736].rearrange("p (k d) -> p k d", k=2)
        km = rb[:, 0:H * S].rearrange("p (h s) -> p h s", h=H)
        pT0 = region[:, 4096:4096 + 3 * 896].rearrange("p (r s) -> p r s", r=3)
        lp = region[:, 7168:7168 + 1024].rearrange("p (t h l) -> p t h l", t=T, h=LH)
        lpT = region[:, 8192:8192 + 1024].rearrange("p (c s) -> p c s", c=2)
        qs = region[:, 9216:9216 + 1024].bitcast(BF16).rearrange("p (g s) -> p g s", g=H // G0)
        ks = region[:, 10240:10240 + 1024].bitcast(BF16).rearrange("p (g s) -> p g s", g=H // G0)
        mixT = region[:, 11264:11264 + 512]
        remote = region2[:, 0:512].rearrange("p (t d) -> p t d", t=T)
        local = region2[:, 512:1024].rearrange("p (t d) -> p t d", t=T)
        gtmp = region2[:, 1024:1536].rearrange("p (t d) -> p t d", t=T)
        oT = region2[:, 4096:6144].rearrange("p (g s) -> p g s", g=H // G0)
        rqT = region2[0:LD, 1536:2048]
        latT = region2[0:LD, 2048:2560]
        rkM = region2[0:LD, 2560:2816].rearrange("p (h l) -> p h l", h=LH)
        pooled2 = region2[:, 2816:2944].rearrange("p (r l) -> p r l", r=2)
        psumf = region2[:, 2944:3008]
        rvb = region2[:, 3008:3040]
        rvM = region2[:, 3072:3136].rearrange("p (c d) -> p c d", c=2)
        mx0 = sb("mx0", [P, T, H])
        nm = sb("nm", [P, T, H])
        nmT = sb("nmT", [H, S], BF16)
        lmx = sb("lmx", [P, T, LH])
        lsum = sb("lsum", [P, T, LH])
        rden = sb("rden", [P, T, H])
        gz = sb("gz", [P, T, H])
        gz2 = sb("gz2", [P, T, H])
        h0T = region[:, 0:4 * S].rearrange("p (f s) -> p f s", f=FC)
        qst = rb[:, 0:8192].rearrange("p (h s) -> p h s", h=H)
        kst = rb[:, 8192:16384].rearrange("p (h s) -> p h s", h=H)
        kst2 = rb[:, 16384:24576].rearrange("p (h s) -> p h s", h=H)
        rot1 = region2[:, 0:3072].rearrange("p (r h d) -> p r h d", r=3, h=H)
        rot2 = region2[:, 3072:5120].rearrange("p (r h d) -> p r h d", r=2, h=H)
        sq = region2[:, 5120:7168].rearrange("p (r h d) -> p r h d", r=2, h=H)
        hilo = region[:, 8192:11264].bitcast(BF16).rearrange("p (r h k d) -> p r h k d", r=3, h=H, k=2)
        ao = region2[:, 0:4096].rearrange("p (t n) -> p t n", t=T)
        aoT = [region[:, a:a + 512] for a in (*range(0, 2048, 512), *range(4096, 6144, 512))]
        p1 = region2[:, 4096:5376]
        hT1 = sb("hT1", [P, FC, S])
        p1_parts = [a.bitcast(BF16).rearrange("p (k s) -> p k s", k=2)
                    for a in (region2[:, 5376:6656], norm[:, 0:1280],
                              hT1[:, 0:3, :].rearrange("p f s -> p (f s)")[:, 0:1280])]
        vmem = sb("vmem", [P, T * H * (HD1 + 1)])
        v1 = vmem[:, :].bitcast(BF16).rearrange("p (t h k d) -> p t h k d", t=T, h=H, k=2)
        v0 = vmem[:, 0:T * H * 32].rearrange("p (t h d) -> p t h d", t=T, h=H)
        ve1 = sb("ve1", [P, 2, H])
        rinv = sb("rinv", [P, 2, H])
        r1 = sb("r1", [P, 2, T])
        csq = sb("csq", [P, 2, 2, T, HD1])
        nmT1 = (nmT[0:8, :], norm[0:8, 1280:1536].bitcast(BF16))
        xm = sb("xm", [P, T, D])
        em = sb("em", [P, T, D])
        gact1 = sb("gact1", [P, S])
        xmT = gact1[:, :]
        gact_alone = region[:, 0:6 * 256].rearrange("p (r s) -> p r s", r=6)
        bstm = sb("bstm", [P, T, 6])
        mvm = sb("mvm", [P, T, 2])
        vem = sb("vem", [P, T])
        rstdm = sb("rstdm", [P, T])
        pr = sb("pr", [P, T, NE])
        comb = sb("comb", [P, T, NE])
        cmp1 = norm[:, 512:768].rearrange("p (t a e) -> p t a e", t=T, a=NE)
        cmp2 = norm[:, 768:1024].rearrange("p (t a e) -> p t a e", t=T, a=NE)
        r4 = sb("r4", [P, T])
        thr = region2[:, 5000:5004]
        gam = region2[:, 5004:5006]
        qtmp = region2[:, 0:512]
        qtmp2 = region2[:, 512:1024]

        ps = ctx.enter_context(nc.psum_tensor("ps", [P, 8, 512], F32))

        def bank(i, n=1):
            return ps[:, i, :] if n == 1 else ps[:, i:i + n, :].rearrange("p b n -> p (b n)")

        wload = {k: sig("w_" + k, 16) for k in ("qkv", "lat", "gate", "mlp", "attn1", "exp", "gu")}
        group_of = {}
        for k in order:
            group_of[k] = ("qkv" if k in ("ident_f", "wqrep", "wkrep", "bqk", "wv", "bv") else
                           "lat" if k in ("rq_w", "rq_b", "rkv_w", "rk_b", "rv_b", "small", "lmask", "rout_w",
                                          "rout_b") else
                           "gate" if k in ("out_w", "out_b", "glr", "masks") else
                           "mlp" if k in ("w1", "b1", "w2", "b2") else
                           "gu" if k == "gu" else "attn1" if k in ("cs", "qkn", "wqkv1", "wo1") else "exp")
        gcount = {g: 16 * sum(1 for k in order if group_of[k] == g) for g in wload}

        set_ones = sig("set_ones", 0)
        abs_sums = sig("abs_sums", 0)
        gam_ready = sig("gam_ready", 0)
        quant_done = sig("quant_done", 0)
        gu_hi = sig("gu_hi", 0)
        gu_lo = sig("gu_lo", 0)
        setup_step = sig("setup_step", 0)

        x_loaded = sig("x_loaded", 16)
        x_taken = sig("x_taken", 1)
        x_final = sig("x_final", 1)
        x_out_free = sig("x_out_free", 16)
        vec = sig("vec_step", VEC_STEPS, 2)
        var_ready = sig("var_ready", 14, 1)
        rstd_ready = sig("rstd_ready", 14, 1)
        xn_ready = sig("xn_ready", 3, 1)
        xnT_ps = sig("xnT_ps", 3)
        xnT_ready = sig("xnT_ready", 3)

        q0_ps = sig("q0_ps", 8)
        q0_hi = sig("q0_hi", 8)
        q0_lo = sig("q0_lo", 8)
        km_ready = sig("km_ready", H)
        va_ps = sig("va_ps", 1)
        va_ready = sig("va_ready", 1)
        rq_ps = sig("rq_ps", 1)
        rq_ready = sig("rq_ready", 1)
        pool_ready = sig("pool_ready", 1)
        rkv_ps = sig("rkv_ps", 1)
        rkv_ready = sig("rkv_ready", 1)
        ls_ps = sig("ls_ps", 1)
        ls_free = sig("ls_free", 1)
        ls_ready = sig("ls_ready", 1)
        lexp = sig("lexp", 1)
        lp_ready = sig("lp_ready", 1)
        lpT_ps = sig("lpT_ps", 2)
        lpT_ready = sig("lpT_ready", 2)
        lat_ps = sig("lat_ps", 1)
        lat_ready = sig("lat_ready", 1)
        rem_ps = sig("rem_ps", 1)
        rem_ready = sig("rem_ready", 1)
        sr0 = sig("sr0", 16)
        mx0_done = sig("mx0_done", 16)
        nm_ready = sig("nm_ready", 3)
        nmT_ps = sig("nmT_ps", 3)
        nmT_ready = sig("nmT_ready", 3)
        sc0 = sig("sc0", H)
        e0 = sig("e0", H)
        pv0 = sig("pv0", H)
        o_ev = sig("o_ev", H // G0)
        o_rows = sig("o_rows", 1)
        gz_ready = sig("gz_ready", 1)
        gexp = sig("gexp", 1)
        mix_ready = sig("mix_ready", 1)
        mixT_ps = sig("mixT_ps", 1)
        mixT_ready = sig("mixT_ready", 1)
        y_ps = sig("y_ps", 3)
        v0_set = sig("v0_set", 1)
        v1_set = sig("v1_set", 1)
        h_ps = sig("h_ps", FC)
        h_ready = sig("h_ready", FC)

        pj = sig("pj", 8)
        pv_ps = sig("pv_ps", T)
        b_sq = sig("b_sq", 8)
        b_rot = sig("b_rot", 8)
        b_vh = sig("b_vh", T)
        b_v = sig("b_v", T)
        b_sum = sig("b_sum", 8)
        b_qn = sig("b_qn", 8)
        b_hi = sig("b_hi", 8)
        b_lo = sig("b_lo", 8)
        b_tr = sig("b_tr", 16)
        b_ev = sig("b_ev", 16)
        k_swapped = sig("k_swapped", 32)
        sr1 = sig("sr1", 5 * H // 2)
        mx1_done = sig("mx1_done", 5 * H // 2)
        sc1 = sig("sc1", H)
        e1 = sig("e1", 4 * H)
        p1_lo = sig("p1_lo", H)
        pv1 = sig("pv1", H)
        ao_done = sig("ao_done", H)
        aoT_ps = sig("aoT_ps", 8)
        aoT_ready = sig("aoT_ready", 8)

        mvar_ready = sig("mvar_ready", 2)
        mrstd_ready = sig("mrstd_ready", 2)
        mvec = sig("mvec_step", MVEC_STEPS)
        em_ready = sig("em_ready", 1)
        xmT_ps = sig("xmT_ps", 1)
        xh_hi = sig("xh_hi", 1)
        xh_lo = sig("xh_lo", 1)
        lg_ps = sig("lg_ps", 1)
        lg_max = sig("lg_max", 1)
        lg_exp = sig("lg_exp", 1)
        gu_ps = sig("gu_ps", HALVES)
        gelu_done = sig("gelu_done", HALVES)
        hact = sig("hact", HALVES)
        dn_ps = sig("dn_ps", NE * FC)
        dn_read = sig("dn_read", NE)

        block = ctx.enter_context(nc.Block())
        x_dram = ins["x"].rearrange("(b t p) d -> b p t d", t=T, p=P)
        out_dram = out.rearrange("(b t p) d -> b p t d", t=T, p=P)

        def drive(eng, layers, experts):
            for _ in layers(0, True):
                pass
            with eng.Fori(0, NSEQ - 1) as b:
                pieces, met, left = experts(b), {}, PIECES
                for place in layers(b + 1, False):
                    k = met.get(place, 0)
                    met[place] = k + 1
                    for _ in range(min(PLAN[place][k], left)):
                        next(pieces)
                        left -= 1
                assert left == 0, left
                for _ in pieces:
                    assert False
            for _ in experts(NSEQ - 1):
                pass

        def units_beside(h):
            return range(ROWS_HALF + 3 * h, min(ROWS_HALF + 3 * h + 3, 2 * ROWS_HALF))

        def beside(b):
            if isinstance(b, int):
                return 6, 0, gact_alone
            return 2, 5, gact1[:, :].rearrange("p (r s) -> p r s", r=2)

        @block.sync
        def _(sp):
            sp.dma_start(x_in[:, :, :], x_dram[0]).then_inc(x_loaded.sem, 16)
            for name in order:
                dst = c[name]
                full = tuple(slice(None) for _ in dst.shape)
                sp.dma_start(dst[full], ins[name]).then_inc(wload[group_of[name]].sem, 16)
            def swap_k(b):
                sp.wait_ge(b_ev.sem, b_ev.at(b, 16))
                sp.dma_start(kst2[64:128, :, :], kst[0:64, :, :]).then_inc(k_swapped.sem, 16)
                sp.dma_start(kst2[0:64, :, :], kst[64:128, :, :]).then_inc(k_swapped.sem, 16)

            def load(b, taken):
                sp.wait_ge(x_taken.sem, taken)
                sp.dma_start(x_in[:, :, :], x_dram[b]).then_inc(x_loaded.sem, 16)

            def store(b):
                sp.wait_ge(x_final.sem, x_final.at(b, 1))
                sp.dma_start(out_dram[b], em[:, :, :]).then_inc(x_out_free.sem, 16)

            load(1, 1)
            swap_k(0)
            with sp.Fori(0, NSEQ - 1) as b:
                load((b + 2) % NSEQ, b + 2)
                swap_k(b + 1)
                store(b)
            store(NSEQ - 1)
            sp.wait_ge(x_loaded.sem, 16 * (NSEQ + 1))
            sp.wait_ge(x_out_free.sem, 16 * NSEQ + 1)

        @block.gpsimd
        def _(pool):
            pool.wait_ge(set_ones.sem, 1)
            ones = onesf[:, 0:T * H].rearrange("p (t h) -> p t h", t=T)

            pool.wait_ge(var_ready.sem, 1)
            pool.tensor_tensor(rstd[:, :], ve[:, :], mhalf[:, 0:T], ALU.pow).then_inc(rstd_ready.sem, 1)

            def set_one(dst):
                pool.tensor_tensor(dst, ones, ones, ALU.mult)

            def layers(b, first):
                done = [0]

                def power(dst, src):
                    done[0] += 1
                    pool.wait_ge(var_ready.sem, var_ready.at(b, done[0]))
                    pool.tensor_tensor(dst, src, mhalf[:, 0:src.shape[1]], ALU.pow).then_inc(rstd_ready.sem, 1)

                def between():
                    for k in range(2):
                        power(rstd[:, :], ve[:, :])
                        yield "norms"
                        yield "norms"

                if not first:
                    pool.wait_ge(pv1.sem, pv1.at(b, 0))
                set_one(v0[:, :, :, HD0])
                pool.memset(v0[:, :, :, HD0 + 1:], 0.0).then_inc(v0_set.sem, 1)
                yield "start"
                yield "turned"
                for g in range(H // G0):
                    pool.wait_ge(q0_lo.sem, q0_lo.at(b, 2 * g + 2))
                    for hh in range(G0):
                        pool.tensor_tensor(km[:, G0 * g + hh, :], ks[:, g, :],
                                           hmask[:, hh:hh + 1].to_broadcast([P, S]), ALU.mult)\
                            .then_inc(km_ready.sem, 1)
                    yield "heads"
                yield "latent"
                for i in range(16):
                    yield "maxima"
                yield "shift"
                for h in range(H):
                    yield "banded"
                pool.wait_ge(pv0.sem, pv0.at(b, H))
                set_one(v1[:, :, :, 0, HD1])
                pool.memset(v1[:, :, :, 1, HD1:HD1 + 1], 0.0).then_inc(v1_set.sem, 1)
                for k in range(3):
                    yield "gate"
                yield from between()
                for k in range(3):
                    yield "mlp"
                yield from between()
                yield "causal"
                for t in range(T):
                    yield "values"
                for i in range(10):
                    if i < 8:
                        pool.wait_ge(b_rot.sem, b_rot.at(b, i + 1))
                        pool.tensor_tensor(rot1[:, i % 3], rot1[:, i % 3], rot2[:, i % 2], ALU.add)\
                            .then_inc(b_sum.sem, 1)
                    yield "parts"
                    if i < 8:
                        power(rinv[:, i % 2, :], ve1[:, i % 2, :])
                    yield "parts"
                for pair in range(H // 4):
                    yield "rows"
                yield "end"
                power(rstd[:, :], ve[:, :])
                power(rstd[:, :], ve[:, :])

            def experts(b):
                for n in range(PIECES):
                    if n in (0, PIECES - 2):
                        pool.wait_ge(mvar_ready.sem, mvar_ready.at(b, 1 if n == 0 else 2))
                        pool.tensor_tensor(rstdm[:, :], vem[:, :], mhalf[:, 0:T], ALU.pow)\
                            .then_inc(mrstd_ready.sem, 1)
                    yield

            drive(pool, layers, experts)

        @block.scalar
        def _(act):
            act.wait_ge(wload["mlp"].sem, gcount["mlp"])
            act.activation(qtmp, c["w1"][:, :], ACT.Abs, accum_out=gam[:, 0:1]).then_inc(abs_sums.sem, 1)
            act.activation(qtmp2, c["w2"][:, :], ACT.Abs, accum_out=gam[:, 1:2]).then_inc(abs_sums.sem, 1)
            act.wait_ge(wload["gu"].sem, gcount["gu"])
            for e in range(NE):
                act.copy(gu_b[:, 0, e, :], c["gu"][:, e, :]).then_inc(gu_hi.sem, 1)
            def layers(b, first):
                def take_chunk(k):
                    act.wait_ge(aoT_ps.sem, aoT_ps.at(b, k + 1))
                    act.copy(aoT[k], bank(AO_BANK[k])).then_inc(aoT_ready.sem, 1)

                def copy_xnT(n):
                    act.wait_ge(xnT_ps.sem, xnT_ps.at(b, n + 1))
                    act.copy(xnT[:, :], bank(0)).then_inc(xnT_ready.sem, 1)

                yield "start"
                copy_xnT(0)
                yield "turned"
                for g in range(H // G0):
                    for kk, dst in enumerate((qs, ks)):
                        i = 2 * g + kk
                        act.wait_ge(q0_ps.sem, q0_ps.at(b, i + 1))
                        act.activation(dst[:, g, :], bank(i % 4), ACT.Identity, bias=c["bqk"][:, i:i + 1])\
                            .then_inc(q0_hi.sem, 1)
                    yield "heads"
                act.wait_ge(rq_ps.sem, rq_ps.at(b, 1))
                act.activation(rqT, ps[0:LD, 0, :], ACT.Identity, bias=c["rq_b"][:, 0:1])\
                    .then_inc(rq_ready.sem, 1)
                yield "latent"
                act.wait_ge(ls_ready.sem, ls_ready.at(b, 1))
                act.activation(lp, lp, ACT.Exp, scale=SCALEL).then_inc(lexp.sem, 1)
                for i in range(16):
                    if i in (3, 5):
                        k = i // 2 - 1
                        act.wait_ge(lpT_ps.sem, lpT_ps.at(b, k + 1))
                        act.copy(lpT[:, k, :], bank(4)).then_inc(lpT_ready.sem, 1)
                    if i == 7:
                        act.wait_ge(lat_ps.sem, lat_ps.at(b, 1))
                        act.copy(latT, ps[0:LD, 4, :]).then_inc(lat_ready.sem, 1)
                    yield "maxima"
                act.wait_ge(nmT_ps.sem, nmT_ps.at(b, 1))
                act.copy(nmT[:, :], ps[0:H, 4, :]).then_inc(nmT_ready.sem, 1)
                yield "shift"
                for h in range(H):
                    act.wait_ge(sc0.sem, sc0.at(b, h + 1))
                    if h >= 3:
                        act.wait_ge(pv0.sem, pv0.at(b, h - 2))
                    act.activation(pT0[:, h % 3, :], bank(2 * (h % 2), 2)[:, 0:896], ACT.Exp, scale=SCALE0)\
                        .then_inc(e0.sem, 1)
                    yield "banded"
                yield "gate"
                act.wait_ge(gz_ready.sem, gz_ready.at(b, 1))
                act.activation(gz2[:, :, :], gz[:, :, :], ACT.Exp, scale=-1.0).then_inc(gexp.sem, 1)
                yield "gate"
                act.wait_ge(mixT_ps.sem, mixT_ps.at(b, 1))
                act.copy(mixT, bank(4)).then_inc(mixT_ready.sem, 1)
                yield "gate"

                for k in range(4):
                    yield "norms"
                copy_xnT(1)
                for f in range(FC):
                    act.wait_ge(h_ps.sem, h_ps.at(b, f + 1))
                    act.activation(h0T[:, f, :], bank(1 + f), ACT.Relu, bias=c["b1"][:, f:f + 1])\
                        .then_inc(h_ready.sem, 1)
                    if f % 2:
                        yield "mlp"
                yield "mlp"

                for k in range(4):
                    yield "norms"
                copy_xnT(2)
                yield "causal"

                def square(i):
                    act.wait_ge(pj.sem, pj.at(b, i + 1))
                    if i >= 2:
                        act.wait_ge(var_ready.sem, var_ready.at(b, 4 + i - 1))
                    act.activation(sq[:, i % 2].rearrange("p h d -> p (h d)"), bank(2 * (i % 2), 2), ACT.Square)\
                        .then_inc(b_sq.sem, 1)

                def take_v(t):
                    act.wait_ge(pv_ps.sem, pv_ps.at(b, t + 1))
                    act.copy(v1[:, t, :, 0, 0:HD1],
                             bank(2 * (t % 2), 2).rearrange("p (h d) -> p h d", h=H)).then_inc(b_vh.sem, 1)

                def hi(i):
                    act.wait_ge(b_qn.sem, b_qn.at(b, i + 1))
                    act.copy(hilo[:, i % 3, :, 0, :], rot1[:, i % 3]).then_inc(b_hi.sem, 1)

                def evac(i, k):
                    t = i // 2
                    act.wait_ge(b_tr.sem, b_tr.at(b, 2 * i + k + 1))
                    act.copy((qst, kst)[i % 2][:, 8 * k:8 * k + 8, t * P:(t + 1) * P],
                             bank(4).bitcast(BF16).rearrange("p (h s) -> p h s", h=8)).then_inc(b_ev.sem, 1)

                for t in range(T):
                    take_v(t)
                    yield "values"
                square(0)
                square(1)
                for i in range(10):
                    if i >= 3:
                        evac(i - 3, 0)
                    yield "parts"
                    if i >= 3:
                        evac(i - 3, 1)
                    if 1 <= i < 7:
                        square(i + 1)
                    if 1 <= i < 9:
                        hi(i - 1)
                    yield "parts"
                evac(7, 0)
                evac(7, 1)
                for pair in range(H // 4):
                    yield "rows"
                yield "end"
                act.wait_ge(nmT_ps.sem, nmT_ps.at(b, 2))
                act.copy(nmT1[0], ps[0:8, 6, :]).then_inc(nmT_ready.sem, 1)
                for h in range(H):
                    act.wait_ge(sc1.sem, sc1.at(b, h + 1))
                    if h >= 3:
                        act.wait_ge(pv1.sem, pv1.at(b, h - 2))
                    sides = ((ps[:, 2, 0:256], slice(1024, 1280)), (bank(3 * (h % 2), 2), slice(0, 1024)))
                    for src, q in sides:
                        act.activation(p1_parts[h % 3][:, 0, q], src, ACT.Exp, scale=SCALE1).then_inc(e1.sem, 1)
                    if h >= 1:
                        act.wait_ge(p1_lo.sem, p1_lo.at(b, h))
                    for src, q in sides:
                        act.activation(p1[:, q], src, ACT.Exp, scale=SCALE1).then_inc(e1.sem, 1)
                    if h == 7:
                        act.wait_ge(nmT_ps.sem, nmT_ps.at(b, 3))
                        act.copy(nmT1[1], ps[0:8, 5, :]).then_inc(nmT_ready.sem, 1)
                    if h in AO_HEAD:
                        take_chunk(AO_HEAD.index(h))
                take_chunk(6)
                take_chunk(7)

            def experts(b):
                ring, first_bank, gact = beside(b)
                yield
                act.wait_ge(xmT_ps.sem, xmT_ps.at(b, 1))
                act.copy(xmT, bank(7))
                act.copy(xh[:, 0, :], bank(7)).then_inc(xh_hi.sem, 1)
                yield
                act.wait_ge(lg_max.sem, lg_max.at(b, 1))
                act.activation(pr[:, :, :], pr[:, :, :], ACT.Exp).then_inc(lg_exp.sem, 1)
                yield
                yield
                for k in range(HALVES):
                    act.wait_ge(gu_ps.sem, gu_ps.at(b, k + 1))
                    if k >= ring:
                        act.wait_ge(hact.sem, hact.at(b, k - ring + 1))
                    act.activation(gact[:, k % ring, :], ps[:, first_bank + k % ring, 0:256], ACT.Gelu)\
                        .then_inc(gelu_done.sem, 1)
                    yield
                for _ in range(4):
                    yield

            drive(act, layers, experts)

        @block.tensor
        def _(pe):
            pe.wait_ge(abs_sums.sem, 2)
            pe.wait_ge(set_ones.sem, 1)
            pe.matmul(ps[:, 7, 0:2], onesf[:, :], gam[:, :], start=True, stop=True).then_inc(gam_ready.sem, 1)
            for g in wload:
                pe.wait_ge(wload[g].sem, gcount[g])
            pe.wait_ge(gu_lo.sem, NE)
            pe.wait_ge(quant_done.sem, 2)
            def mm(o, l, r, start=True, stop=True):
                return pe.matmul(o, l, r, start=start, stop=stop, skip_group_check=True)

            def pick(h, n):
                return ident_b[0:n, h:h + 1].to_broadcast([n, P])

            def layers(b, first):
                def turn_rows(n):
                    pe.wait_ge(xn_ready.sem, xn_ready.at(b, n))
                    for t in range(T):
                        last = pe.transpose(ps[:, 0, t * P:(t + 1) * P], xn[:, t, :], ident_f)
                    last.then_inc(xnT_ps.sem, 1)
                    pe.wait_ge(xnT_ready.sem, xnT_ready.at(b, n + 1))

                yield "start"
                turn_rows(0)
                yield "turned"
                for g in range(H // G0):
                    for kk, w in enumerate(("wqrep", "wkrep")):
                        i = 2 * g + kk
                        if i >= 4:
                            pe.wait_ge(q0_lo.sem, q0_lo.at(b, i - 3))
                        mm(bank(i % 4), c[w][:, g * P:(g + 1) * P], xnT).then_inc(q0_ps.sem, 1)
                    yield "heads"
                for t in range(T):
                    last = mm(ps[:, 4, t * P:(t + 1) * P], xnT[:, t * P:(t + 1) * P], c["wv"][:, :])
                last.then_inc(va_ps.sem, 1)
                pe.wait_ge(q0_lo.sem, q0_lo.at(b, 5))
                mm(ps[0:LD, 0, :], c["rq_w"][:, :], xnT).then_inc(rq_ps.sem, 1)
                pe.wait_ge(q0_lo.sem, q0_lo.at(b, 6))
                pe.wait_ge(pool_ready.sem, pool_ready.at(b, 1))
                mm(ps[0:LD, 1, 0:NLAT], c["rkv_w"][:, 0:LD], pooled2[:, 0, :])
                mm(ps[:, 1, NLAT:NLAT + LD], pooled2.rearrange("p r l -> p (r l)"), c["rkv_w"][:, LD:2 * LD])\
                    .then_inc(rkv_ps.sem, 1)
                yield "latent"
                pe.wait_ge(rq_ready.sem, rq_ready.at(b, 1))
                pe.wait_ge(rkv_ready.sem, rkv_ready.at(b, 1))
                pe.wait_ge(q0_lo.sem, q0_lo.at(b, 8))
                for t in range(T):
                    last = mm(bank(2, 2)[:, t * 256:(t + 1) * 256], rqT[:, t * P:(t + 1) * P],
                              rkM.rearrange("p h l -> p (h l)"))
                last.then_inc(ls_ps.sem, 1)

                pe.wait_ge(va_ready.sem, va_ready.at(b, 1))

                def rows0(i):
                    g, qb = divmod(i, T)
                    s = i % 2
                    if i >= 2:
                        pe.wait_ge(mx0_done.sem, mx0_done.at(b, i - 1))
                    if i == 1:
                        pe.wait_ge(ls_free.sem, ls_free.at(b, 1))
                    if i % T == 0:
                        pe.wait_ge(km_ready.sem, km_ready.at(b, G0 * (g + 1)))
                    w, k0 = (P, 0) if qb == 0 else (2 * P, (qb - 1) * P)
                    for half in range(1 if qb == 0 else 2):
                        nh = 512 // w
                        o = ps[:, 2 * s + half, :]
                        mm(o.rearrange("p (h n) -> p h n", h=nh), ident_b,
                           mask_rows[:, 256 - w:256].unsqueeze(1).to_broadcast([P, nh, w]), stop=False)
                        for hh in range(nh):
                            h = G0 * g + nh * half + hh
                            last = mm(o[:, hh * w:(hh + 1) * w], qs[:, g, qb * P:(qb + 1) * P],
                                      km[:, h, k0:k0 + w], start=False)
                    last.then_inc(sr0.sem, 1)

                for i in range(16):
                    rows0(i)
                    if i in (2, 4):
                        k = i // 2 - 1
                        pe.wait_ge(lp_ready.sem, lp_ready.at(b, 1))
                        if k:
                            pe.wait_ge(lpT_ready.sem, lpT_ready.at(b, 1))
                        for t in range(T):
                            last = pe.transpose(ps[:, 4, t * P:(t + 1) * P],
                                                lp[:, t, 2 * k:2 * k + 2, :].rearrange("p h l -> p (h l)"), ident_f)
                        last.then_inc(lpT_ps.sem, 1)
                    if i == 6:
                        pe.wait_ge(lpT_ready.sem, lpT_ready.at(b, 2))
                        for k in range(2):
                            last = mm(ps[0:LD, 4, :], rvM[:, k, :], lpT[:, k, :], start=k == 0, stop=k == 1)
                        last.then_inc(lat_ps.sem, 1)
                    if i == 8:
                        pe.wait_ge(lat_ready.sem, lat_ready.at(b, 1))
                        for t in range(T):
                            last = mm(ps[:, 4, t * P:(t + 1) * P], latT[:, t * P:(t + 1) * P], c["rout_w"][:, :])
                        last.then_inc(rem_ps.sem, 1)
                    yield "maxima"

                def turn_max(n, bk):
                    pe.wait_ge(nm_ready.sem, nm_ready.at(b, n + 1))
                    for t in range(T):
                        last = pe.transpose(ps[0:H, bk, t * P:(t + 1) * P], nm[:, t, :], ident_f)
                    last.then_inc(nmT_ps.sem, 1)
                    pe.wait_ge(nmT_ready.sem, nmT_ready.at(b, n + 1))

                pe.wait_ge(rem_ready.sem, rem_ready.at(b, 1))
                turn_max(0, 4)
                yield "shift"

                def cols0(h):
                    g, s = h // G0, 2 * (h % 2)
                    if h >= 2:
                        pe.wait_ge(e0.sem, e0.at(b, h - 1))
                    o = ps[:, s, :]
                    mm(o.rearrange("p (j n) -> p j n", j=2), ident_b,
                       mask_cols.unsqueeze(1).to_broadcast([P, 2, 256]), stop=False)
                    o = ps[:, s + 1, :]
                    mm(o[:, 0:256], ident_b, mask_cols, stop=False)
                    mm(o[:, 256:384], ident_b, mask_cols[:, 0:P], start=False, stop=False)
                    for j in range(T):
                        o = ps[:, s + j // 2, (j % 2) * 256:(j % 2) * 256 + W0[j]]
                        q = slice(j * P, j * P + W0[j])
                        mm(o, pick(h, H), nmT[:, q], start=False, stop=False)
                        last = mm(o, km[:, h, j * P:(j + 1) * P], qs[:, g, q], start=False)
                    last.then_inc(sc0.sem, 1)

                def values0(h):
                    g, r = h // G0, 32 * (h % G0)
                    pe.wait_ge(e0.sem, e0.at(b, h + 1))
                    if h == 0:
                        pe.wait_ge(v0_set.sem, v0_set.at(b, 1))
                    if h % G0 == 0 and g >= 1:
                        pe.wait_ge(o_ev.sem, o_ev.at(b, g))
                    for j in range(T):
                        last = mm(ps[r:r + 32, 4, j * P:j * P + W0[j]], v0[:, j, h, :],
                                  pT0[:, h % 3, OFF0[j]:OFF0[j] + W0[j]], start=j == 0)
                    last.then_inc(pv0.sem, 1)

                for h in range(H):
                    cols0(h)
                    if h >= 1:
                        values0(h - 1)
                    yield "banded"
                values0(H - 1)
                pe.wait_ge(o_ev.sem, o_ev.at(b, H // G0))
                pe.wait_ge(e0.sem, e0.at(b, H))
                for t in range(T):
                    for g in range(H // G0):
                        last = pe.transpose(ps[:, t, g * P:(g + 1) * P], oT[:, g, t * P:(t + 1) * P], ident_f)
                last.then_inc(o_rows.sem, 1)
                yield "gate"
                yield "gate"
                pe.wait_ge(mix_ready.sem, mix_ready.at(b, 1))
                for t in range(T):
                    last = pe.transpose(ps[:, 4, t * P:(t + 1) * P], xn[:, t, :], ident_f)
                last.then_inc(mixT_ps.sem, 1)
                pe.wait_ge(mixT_ready.sem, mixT_ready.at(b, 1))
                for t in range(T):
                    last = mm(ps[:, 1, t * P:(t + 1) * P], mixT[:, t * P:(t + 1) * P], c["out_w"][:, :])
                last.then_inc(y_ps.sem, 1)
                yield "gate"

                for k in range(4):
                    yield "norms"
                turn_rows(1)
                for f in range(FC):
                    mm(bank(1 + f), c["w1"][:, f * P:(f + 1) * P], xnT).then_inc(h_ps.sem, 1)
                    if f % 2:
                        yield "mlp"
                pe.wait_ge(h_ready.sem, h_ready.at(b, FC))
                for t in range(T):
                    for f in range(FC):
                        last = mm(ps[:, 0, t * P:(t + 1) * P], h0T[:, f, t * P:(t + 1) * P],
                                  c["w2"][:, f * P:(f + 1) * P], start=f == 0, stop=f == FC - 1)
                last.then_inc(y_ps.sem, 1)
                yield "mlp"

                for k in range(4):
                    yield "norms"
                turn_rows(2)
                yield "causal"

                def turn_parts(i, k):
                    if k == 0:
                        pe.wait_ge(b_lo.sem, b_lo.at(b, i + 1))
                    dst = bank(4).bitcast(BF16)
                    if i or k:
                        pe.wait_ge(b_ev.sem, b_ev.at(b, 2 * i + k))
                    for h in range(8):
                        last = pe.transpose(dst[:, h * P:(h + 1) * P],
                                            hilo[:, i % 3, 8 * k + h].rearrange("p k d -> p (k d)"), ident_b)
                    last.then_inc(b_tr.sem, 1)

                def project(t, kind, first_bank):
                    for n in range(2):
                        col = kind * 1024 + n * 512
                        last = mm(bank(first_bank + n), xnT[:, t * P:(t + 1) * P], c["wqkv1"][:, col:col + 512])
                    return last

                for t in range(T):
                    if t >= 2:
                        pe.wait_ge(b_v.sem, b_v.at(b, t - 1))
                    project(t, 2, 2 * (t % 2)).then_inc(pv_ps.sem, 1)
                    yield "values"
                for i in range(2):
                    pe.wait_ge(b_v.sem, b_v.at(b, 3 + i))
                    project(0, i, 2 * i).then_inc(pj.sem, 1)
                for i in range(10):
                    if i >= 3:
                        turn_parts(i - 3, 0)
                    yield "parts"
                    if i >= 3:
                        turn_parts(i - 3, 1)
                    if 1 <= i < 7:
                        pe.wait_ge(b_rot.sem, b_rot.at(b, i))
                        project((i + 1) // 2, (i + 1) % 2, 2 * ((i + 1) % 2)).then_inc(pj.sem, 1)
                    yield "parts"
                turn_parts(7, 0)
                turn_parts(7, 1)
                pe.wait_ge(b_ev.sem, b_ev.at(b, 16))
                pe.wait_ge(b_rot.sem, b_rot.at(b, 8))

                def row_unit(n):
                    pair, u = divmod(n, 5)
                    if n < ROWS_HALF:
                        bk, free = u, n - 5
                    else:
                        bk, free = 5 + 2 * (n % 2), (n - 2 if n >= ROWS_HALF + 2 else -1)
                    if free >= 0:
                        pe.wait_ge(mx1_done.sem, mx1_done.at(b, free + 1))
                    for hh, qb, col in ROW_UNITS[u]:
                        h, w = 2 * pair + hh, (qb + 1) * P
                        o = ps[:, bk, col:col + w]
                        mm(o, qst[:, h, qb * P:(qb + 1) * P], kst[:, h, 0:w], stop=False)
                        last = mm(o[:, w - P:w], ident_b, cmask_rows, start=False)
                    last.then_inc(sr1.sem, 1)

                def turn_max1(part, bk):
                    pe.wait_ge(nm_ready.sem, nm_ready.at(b, part + 2))
                    for t in range(T):
                        last = pe.transpose(ps[0:8, bk, t * P:(t + 1) * P], nm[:, t, 8 * part:8 * part + 8], ident_f)
                    last.then_inc(nmT_ps.sem, 1)

                for pair in range(H // 4):
                    for u in range(5):
                        row_unit(5 * pair + u)
                    yield "rows"
                yield "end"
                if not first:
                    pe.wait_ge(dn_read.sem, dn_read.at(b, 0))
                turn_max1(0, 6)
                pe.wait_ge(nmT_ready.sem, nmT_ready.at(b, 2))
                pe.wait_ge(v1_set.sem, v1_set.at(b, 1))
                pe.wait_ge(k_swapped.sem, k_swapped.at(b, 32))

                def cols1(h):
                    s = 3 * (h % 2)
                    if h >= 2:
                        pe.wait_ge(e1.sem, e1.at(b, 4 * (h - 1)))
                    for j in (0, 1, 3, 2):
                        w = S - j * P
                        if j == 2:
                            if h:
                                pe.wait_ge(e1.sem, e1.at(b, 4 * h - 1))
                            o = ps[:, 2, 0:w]
                        else:
                            o = bank(s, 2)[:, OFF1[j]:OFF1[j] + w]
                        k = slice(j * P, (j + 1) * P)
                        q = slice(j * P, S)
                        mm(o, kst[:, h, k], qst[:, h, q], stop=False)
                        mm(o, kst2[:, h, k], qst[:, h, q], start=False, stop=False)
                        mm(o, pick(h % 8, 8), nmT1[h // 8][:, q], start=False, stop=False)
                        last = mm(o[:, 0:P], ident_b, cmask_cols, start=False)
                    last.then_inc(sc1.sem, 1)

                def values1(h):
                    pe.wait_ge(p1_lo.sem, p1_lo.at(b, h + 1))
                    if h >= 1:
                        pe.wait_ge(ao_done.sem, ao_done.at(b, h))
                    part = p1_parts[h % 3]
                    for qb in range(T):
                        o = ps[:, 6, 65 * qb:65 * qb + 65]
                        for j in range(qb + 1):
                            a = OFF1[j] + (qb - j) * P
                            mm(o, part[:, 0, a:a + P], v1[:, j, h, 0, :], start=j == 0, stop=False)
                            mm(o, part[:, 0, a:a + P], v1[:, j, h, 1, :], start=False, stop=False)
                            last = mm(o, part[:, 1, a:a + P], v1[:, j, h, 0, :], start=False, stop=j == qb)
                    last.then_inc(pv1.sem, 1)

                def turn_chunk(k):
                    pe.wait_ge(ao_done.sem, ao_done.at(b, 2 * k + 2))
                    if k >= 2:
                        pe.wait_ge(aoT_ready.sem, aoT_ready.at(b, k if k == 7 else k - 1))
                    for t in range(T):
                        last = pe.transpose(ps[:, AO_BANK[k], t * P:(t + 1) * P], ao[:, t, k * P:(k + 1) * P],
                                            ident_f)
                    last.then_inc(aoT_ps.sem, 1)

                def output(k):
                    pe.wait_ge(aoT_ready.sem, aoT_ready.at(b, max(k + 1, 6)))
                    for t in range(T):
                        last = mm(ps[:, 7, t * P:(t + 1) * P], aoT[k][:, t * P:(t + 1) * P],
                                  c["wo1"][:, k * P:(k + 1) * P], start=k == 0 and t == 0, stop=k == 7)
                    return last

                for h in range(H):
                    if h == 8:
                        pe.wait_ge(nmT_ready.sem, nmT_ready.at(b, 3))
                    cols1(h)
                    for n in units_beside(h)[0:2]:
                        row_unit(n)
                    if h == 7:
                        turn_max1(1, 5)
                    if h >= 2:
                        values1(h - 2)
                    for n in units_beside(h)[2:]:
                        row_unit(n)
                    if h in AO_HEAD:
                        turn_chunk(AO_HEAD.index(h))
                values1(H - 2)
                turn_chunk(6)
                for k in range(6):
                    output(k)
                values1(H - 1)
                output(6)
                turn_chunk(7)
                output(7).then_inc(y_ps.sem, 1)

            def experts(b):
                ring, first_bank, _ = beside(b)
                yield
                pe.wait_ge(em_ready.sem, em_ready.at(b, 1))
                for t in range(T):
                    last = pe.transpose(ps[:, 7, t * P:(t + 1) * P], em[:, t, :], ident_f)
                last.then_inc(xmT_ps.sem, 1)
                yield
                pe.wait_ge(xh_hi.sem, xh_hi.at(b, 1))
                for t in range(T):
                    last = mm(ps[:, 6, t * NE:(t + 1) * NE], xmT[:, t * P:(t + 1) * P], c["gate_w"][:, :])
                last.then_inc(lg_ps.sem, 1)
                yield
                pe.wait_ge(xh_lo.sem, xh_lo.at(b, 1))
                pe.wait_ge(lg_max.sem, lg_max.at(b, 1))
                yield

                def up(k):
                    n, half = divmod(k, 2)
                    e, f = divmod(n, FC)
                    if k >= ring:
                        pe.wait_ge(hact.sem, hact.at(b, k - ring + 1))
                    q = slice(256 * half, 256 * half + 256)
                    for kk in range(2):
                        w = slice(kk * FE + f * P, kk * FE + (f + 1) * P)
                        o = ps[:, first_bank + k % ring, 256 * kk:256 * kk + 256]
                        mm(o, gu_b[:, 0, e, w], xh[:, 0, q], stop=False)
                        mm(o, gu_b[:, 1, e, w], xh[:, 0, q], start=False, stop=False)
                        last = mm(o, gu_b[:, 0, e, w], xh[:, 1, q], start=False)
                    last.then_inc(gu_ps.sem, 1)

                def down(n):
                    e, f = divmod(n, FC)
                    pe.wait_ge(hact.sem, hact.at(b, 2 * n + 2))
                    if e and f == 0:
                        pe.wait_ge(dn_read.sem, dn_read.at(b, e))
                    for t in range(T):
                        last = mm(ps[:, 7, t * P:(t + 1) * P], hT1[:, f, t * P:(t + 1) * P], c["down"][:, e, f, :],
                                  start=f == 0 and t == 0, stop=f == FC - 1)
                    last.then_inc(dn_ps.sem, 1)

                for k in range(HALVES + 2):
                    if k < HALVES:
                        up(k)
                    if k >= 3 and k % 2:
                        down((k - 3) // 2)
                    yield
                yield
                yield

            drive(pe, layers, experts)

        @block.vector
        def _(dve):
            n = [0]

            def s_step(i):
                n[0] += 1
                i.then_inc(setup_step.sem, 1)
                dve.wait_ge(setup_step.sem, n[0])

            dve.memset(em[:, 0, 0:1], 0.0).then_inc(x_out_free.sem, 1)
            dve.memset(onesf[:, :], 1.0).then_inc(set_ones.sem, 1)
            dve.wait_ge(gam_ready.sem, 1)
            s_step(dve.tensor_scalar(thr[:, 2:4], ps[:, 7, 0:2], 1.0 / (D * FF), Q_EPS, ALU.mult, ALU.add))
            s_step(dve.tensor_scalar(thr[:, 0:2], thr[:, 2:4], 0.5, None, ALU.mult))
            s_step(dve.tensor_scalar(thr[:, 2:4], thr[:, 0:2], -1.0, None, ALU.mult))
            for k, w in enumerate(("w1", "w2")):
                s_step(dve.tensor_scalar(qtmp, c[w][:, :], thr[:, 2 + k:3 + k], None, ALU.is_lt))
                s_step(dve.scalar_tensor_tensor(out=c[w][:, :], in0=c[w][:, :], scalar=thr[:, k:k + 1],
                                                in1=qtmp, op0=ALU.is_gt, op1=ALU.subtract))
            dve.wait_ge(wload["attn1"].sem, gcount["attn1"])
            half = HD1 // 2
            for k in range(2):
                w = c["qkn"][:, k, :]
                for t in range(T):
                    dve.tensor_tensor(csq[:, k, 0, t, :], c["cs"][:, 0, t, :], w, ALU.mult)
                    dve.tensor_tensor(csq[:, k, 1, t, 0:half], c["cs"][:, 1, t, 0:half], w[:, half:HD1], ALU.mult)
                    last = dve.tensor_tensor(csq[:, k, 1, t, half:HD1], c["cs"][:, 1, t, half:HD1],
                                             w[:, 0:half], ALU.mult)
            last.then_inc(quant_done.sem, 1)
            for g in ("qkv", "lat", "gate", "exp"):
                dve.wait_ge(wload[g].sem, gcount[g])
            dve.tensor_copy(ident_b_t[:, :], ident_f)
            dve.tensor_copy(masks_b[:, :], c["masks"]).then_inc(quant_done.sem, 1)
            dve.wait_ge(quant_done.sem, 2)
            for e in range(NE):
                dve.wait_ge(gu_hi.sem, e + 1)
                dve.tensor_tensor(gu_b[:, 1, e, :], c["gu"][:, e, :], gu_b[:, 0, e, :], ALU.subtract)\
                    .then_inc(gu_lo.sem, 1)
            dve.wait_ge(gu_lo.sem, NE)

            def row_stats(src, part, mean_var, eps_var, step):
                for t in range(T):
                    last = dve.bn_stats(part[:, t, :], src[:, t, :])
                step(last)
                dve.memset(eps_var[:, :], 0.0)
                for t in range(T):
                    last = dve.bn_aggr(mean_var[:, t, :], part[:, t, :])
                step(last)
                return dve.tensor_scalar(eps_var[:, :], mean_var[:, :, 1], LN_EPS, None, ALU.add)

            def normalise(dst, src, mean_var, inv):
                for t in range(T):
                    last = dve.tensor_scalar(dst[:, t, :], src[:, t, :], mean_var[:, t, 0:1], inv[:, t:t + 1],
                                             ALU.subtract, ALU.mult)
                return last

            def first_step(i):
                n[0] += 1
                i.then_inc(vec.sem, 1)
                dve.wait_ge(vec.sem, n[0])

            dve.wait_ge(x_loaded.sem, 16)
            dve.tensor_copy(x[:, :, :], x_in[:, :, :]).then_inc(x_taken.sem, 1)
            dve.wait_ge(x_taken.sem, 1)
            n = [0]
            row_stats(x, bst, mv, ve, first_step).then_inc(var_ready.sem, 1)
            dve.wait_ge(rstd_ready.sem, 1)
            normalise(xn, x, mv, rstd).then_inc(xn_ready.sem, 1)

            def layers(b, first):
                step_no, norm_no = [0], [0]

                def step(i):
                    step_no[0] += 1
                    i.then_inc(vec.sem, 1)
                    dve.wait_ge(vec.sem, vec.at(b, step_no[0]))

                def variance(src):
                    row_stats(src, bst, mv, ve, step).then_inc(var_ready.sem, 1)
                    norm_no[0] += 1

                def wait_rstd():
                    dve.wait_ge(rstd_ready.sem, rstd_ready.at(b, norm_no[0]))

                def take_x():
                    dve.wait_ge(x_loaded.sem, x_loaded.at(b, 32))
                    dve.tensor_copy(x[:, :, :], x_in[:, :, :]).then_inc(x_taken.sem, 1)
                    dve.wait_ge(x_taken.sem, x_taken.at(b, 2))
                    variance(x)
                    wait_rstd()
                    normalise(xn, x, mv, rstd).then_inc(xn_ready.sem, 1)

                def rows(bk):
                    return bank(bk).rearrange("p (t d) -> p t d", t=T)

                def over_tiles(w):
                    return w.unsqueeze(1).to_broadcast([P, T, D])

                yield "start"
                yield "turned"
                dve.wait_ge(xnT_ready.sem, xnT_ready.at(b, 1))
                step(dve.tensor_reduce(psumf, xnT[:, :].rearrange("p (l c) -> p l c", c=CHUNK), X, ALU.add))
                dve.tensor_scalar(pooled2[:, 0, :], psumf, 1.0 / CHUNK, None, ALU.mult)
                dve.tensor_scalar(pooled2[:, 1, :], psumf, 1.0 / CHUNK, None, ALU.mult).then_inc(pool_ready.sem, 1)
                for g in range(H // G0):
                    for kk, dst in enumerate((qs, ks)):
                        i = 2 * g + kk
                        dve.wait_ge(q0_hi.sem, q0_hi.at(b, i + 1))
                        for r0, r1_ in (((64, 128),) if kk == 0 else ((32, 64), (64, 96))):
                            last = dve.scalar_tensor_tensor(
                                out=dst[r0:r1_, g, :], in0=ps[r0:r1_, i % 4, :], scalar=c["bqk"][r0:r1_, i:i + 1],
                                in1=dst[r0:r1_, g, :], op0=ALU.add, op1=ALU.subtract)
                        last.then_inc(q0_lo.sem, 1)
                    yield "heads"
                dve.wait_ge(rkv_ps.sem, rkv_ps.at(b, 1))
                for hh in range(LH):
                    dve.tensor_scalar(rkM[:, hh, :], ps[0:LD, 1, 0:NLAT], c["rk_b"][:, 0:1], lhmask[:, hh:hh + 1],
                                      ALU.add, ALU.mult)
                step(dve.tensor_tensor(rvb, ps[:, 1, NLAT:NLAT + LD], c["rv_b"][:, :], ALU.add))
                dve.tensor_tensor(rvM, rvb.unsqueeze(1).to_broadcast([P, 2, LD]), bdmask, ALU.mult)\
                    .then_inc(rkv_ready.sem, 1)
                dve.wait_ge(va_ps.sem, va_ps.at(b, 1))
                if not first:
                    dve.wait_ge(pv1.sem, pv1.at(b, 0))
                for t in range(T):
                    last = dve.tensor_tensor(v0[:, t, :, 0:HD0],
                                             ps[:, 4, t * P:(t + 1) * P].rearrange("p (h d) -> p h d", h=H),
                                             c["bv"][:, :].rearrange("p (h d) -> p h d", h=H), ALU.add)
                last.then_inc(va_ready.sem, 1)
                yield "latent"
                dve.wait_ge(ls_ps.sem, ls_ps.at(b, 1))
                lsc = bank(2, 2).rearrange("p (t h l) -> p t h l", t=T, h=LH)
                for t in range(T):
                    last = dve.tensor_tensor(lp[:, t], lsc[:, t],
                                             c["lmask"][:, t, :].unsqueeze(1).to_broadcast([P, LH, NLAT]), ALU.add)
                last.then_inc(ls_free.sem, 1)
                dve.wait_ge(ls_free.sem, ls_free.at(b, 1))
                step(dve.tensor_reduce(lmx[:, :, :], lp, X, ALU.max))
                step(dve.tensor_scalar(lmx[:, :, :], lmx[:, :, :], -CLAMP, None, ALU.max))
                lpf = lp.rearrange("p t h l -> p (t h) l")

                def lat_bc(a):
                    return a[:, :, :].rearrange("p t h -> p (t h)").unsqueeze(2).to_broadcast([P, T * LH, NLAT])

                dve.tensor_tensor(lpf, lpf, lat_bc(lmx), ALU.subtract).then_inc(ls_ready.sem, 1)

                def max0(i):
                    g, qb = divmod(i, T)
                    s = 2 * (i % 2)
                    dve.wait_ge(sr0.sem, sr0.at(b, i + 1))
                    w = P if qb == 0 else 2 * P
                    src = bank(s, 2)[:, 0:G0 * w].rearrange("p (h n) -> p h n", h=G0)
                    dve.tensor_reduce(mx0[:, qb, G0 * g:G0 * g + G0], src, X, ALU.max).then_inc(mx0_done.sem, 1)

                for i in range(16):
                    max0(i)
                    if i == 1:
                        dve.wait_ge(lexp.sem, lexp.at(b, 1))
                        step(dve.tensor_reduce(lsum[:, :, :], lp, X, ALU.add))
                        step(dve.tensor_scalar(lsum[:, :, :], lsum[:, :, :], 1e-30, None, ALU.max))
                        step(dve.reciprocal(lsum[:, :, :], lsum[:, :, :]))
                        dve.tensor_tensor(lpf, lpf, lat_bc(lsum), ALU.mult).then_inc(lp_ready.sem, 1)
                    if i == 9:
                        dve.wait_ge(rem_ps.sem, rem_ps.at(b, 1))
                        dve.tensor_tensor(remote, rows(4), over_tiles(c["rout_b"][:, :]), ALU.add)\
                            .then_inc(rem_ready.sem, 1)
                    yield "maxima"
                dve.wait_ge(mx0_done.sem, mx0_done.at(b, 16))
                dve.tensor_scalar(nm[:, :, :], mx0[:, :, :], -1.0, CLAMP, ALU.mult, ALU.min)\
                    .then_inc(nm_ready.sem, 1)
                yield "shift"

                def heads(a):
                    return a.rearrange("p t (h d) -> p (t h) d", h=H)

                def head_bc(a):
                    return a.rearrange("p t h -> p (t h)").unsqueeze(2).to_broadcast([P, T * H, HD0])

                dve.wait_ge(rem_ready.sem, rem_ready.at(b, 1))
                step(dve.tensor_tensor(heads(gtmp), heads(remote),
                                       c["glr"][:, 1, :].unsqueeze(1).to_broadcast([P, T * H, HD0]), ALU.mult))
                step(dve.tensor_reduce(gz2[:, :, :].rearrange("p t h -> p (t h)"), heads(gtmp), X, ALU.add))
                for h in range(H):
                    if h and h % G0 == 0:
                        dve.wait_ge(pv0.sem, pv0.at(b, h))
                        dve.tensor_copy(oT[:, h // G0 - 1, :], bank(4)).then_inc(o_ev.sem, 1)
                    yield "banded"
                dve.wait_ge(pv0.sem, pv0.at(b, H))
                dve.tensor_copy(oT[:, H // G0 - 1, :], bank(4)).then_inc(o_ev.sem, 1)
                yield "gate"
                dve.wait_ge(o_rows.sem, o_rows.at(b, 1))
                orow = bank(0, 4).rearrange("p (k d) -> p k d", d=32)
                rd = rden[:, :, :].rearrange("p t h -> p (t h)")
                step(dve.tensor_scalar(rd, orow[:, :, HD0], 1e-30, None, ALU.max))
                step(dve.reciprocal(rd, rd))
                last = dve.tensor_tensor(heads(local), orow[:, :, 0:HD0], head_bc(rden[:, :, :]), ALU.mult)
                step(last)
                step(dve.tensor_tensor(heads(gtmp), heads(local),
                                       c["glr"][:, 0, :].unsqueeze(1).to_broadcast([P, T * H, HD0]), ALU.mult))
                step(dve.tensor_reduce(gz[:, :, :].rearrange("p t h -> p (t h)"), heads(gtmp), X, ALU.add))
                dve.tensor_tensor(gz[:, :, :], gz[:, :, :], gz2[:, :, :], ALU.add).then_inc(gz_ready.sem, 1)
                step(dve.tensor_tensor(local, local, remote, ALU.subtract))
                yield "gate"
                dve.wait_ge(gexp.sem, gexp.at(b, 1))
                step(dve.tensor_scalar(gz2[:, :, :], gz2[:, :, :], 1.0, None, ALU.add))
                step(dve.reciprocal(gz2[:, :, :], gz2[:, :, :]))
                step(dve.tensor_tensor(heads(local), heads(local), head_bc(gz2[:, :, :]), ALU.mult))
                dve.tensor_tensor(xn[:, :, :], local, remote, ALU.add).then_inc(mix_ready.sem, 1)
                yield "gate"

                def between(n, bk, bias):
                    dve.wait_ge(y_ps.sem, y_ps.at(b, n + 1))
                    step(dve.tensor_tensor(y[:, :, :], rows(bk), over_tiles(bias), ALU.add))
                    variance(y)
                    yield "norms"
                    wait_rstd()
                    step(normalise(xn, y, mv, rstd))
                    step(dve.tensor_tensor(x[:, :, :], x[:, :, :], xn[:, :, :], ALU.add))
                    yield "norms"
                    variance(x)
                    yield "norms"
                    wait_rstd()
                    normalise(xn, x, mv, rstd).then_inc(xn_ready.sem, 1)
                    yield "norms"

                yield from between(0, 1, c["out_b"][:, :])
                for k in range(3):
                    yield "mlp"
                yield from between(1, 0, c["b2"][:, :])
                yield "causal"

                def rotate(i):
                    t, kk = divmod(i, 2)
                    if i >= 3:
                        dve.wait_ge(b_lo.sem, b_lo.at(b, i - 2))
                    dve.wait_ge(b_sq.sem, b_sq.at(b, i + 1))
                    src = bank(2 * (i % 2), 2).rearrange("p (h d) -> p h d", h=H)

                    def tab(k, lo, hi_):
                        return csq[:, kk, k, t, lo:hi_].unsqueeze(1).to_broadcast([P, H, hi_ - lo])

                    dve.tensor_tensor(rot1[:, i % 3], src, tab(0, 0, HD1), ALU.mult)
                    dve.tensor_tensor(rot2[:, i % 2, :, 0:half], src[:, :, half:HD1], tab(1, 0, half), ALU.mult)
                    dve.tensor_tensor(rot2[:, i % 2, :, half:HD1], src[:, :, 0:half], tab(1, half, HD1), ALU.mult)\
                        .then_inc(b_rot.sem, 1)
                    step(dve.tensor_reduce(ve1[:, i % 2, :], sq[:, i % 2], X, ALU.add))
                    dve.tensor_scalar(ve1[:, i % 2, :], ve1[:, i % 2, :], 1.0 / HD1, RMS_EPS, ALU.mult, ALU.add)\
                        .then_inc(var_ready.sem, 1)

                def scale(i):
                    dve.wait_ge(b_sum.sem, b_sum.at(b, i + 1))
                    dve.wait_ge(rstd_ready.sem, rstd_ready.at(b, 4 + i + 1))
                    dve.tensor_tensor(rot1[:, i % 3], rot1[:, i % 3],
                                      rinv[:, i % 2, :].unsqueeze(2).to_broadcast([P, H, HD1]), ALU.mult)\
                        .then_inc(b_qn.sem, 1)

                def low_part(i):
                    dve.wait_ge(b_hi.sem, b_hi.at(b, i + 1))
                    dve.tensor_tensor(hilo[:, i % 3, :, 1, :], rot1[:, i % 3], hilo[:, i % 3, :, 0, :], ALU.subtract)\
                        .then_inc(b_lo.sem, 1)

                def v_low(t):
                    dve.wait_ge(b_vh.sem, b_vh.at(b, t + 1))
                    dve.tensor_tensor(v1[:, t, :, 1, 0:HD1],
                                      bank(2 * (t % 2), 2).rearrange("p (h d) -> p h d", h=H),
                                      v1[:, t, :, 0, 0:HD1], ALU.subtract).then_inc(b_v.sem, 1)

                for t in range(T):
                    v_low(t)
                    yield "values"
                for i in range(10):
                    if i < 8:
                        rotate(i)
                    yield "parts"
                    if i >= 2:
                        low_part(i - 2)
                    if 1 <= i < 9:
                        scale(i - 1)
                    yield "parts"
                norm_no[0] += 8
                def unit_max(n):
                    pair, u = divmod(n, 5)
                    bk = u if n < ROWS_HALF else 5 + 2 * (n % 2)
                    dve.wait_ge(sr1.sem, sr1.at(b, n + 1))
                    if u == 4:
                        last = dve.tensor_reduce(mx0[:, 1, 2 * pair:2 * pair + 2],
                                                 bank(bk).rearrange("p (h n) -> p h n", h=2), X, ALU.max)
                    else:
                        for hh, qb, col in ROW_UNITS[u]:
                            h = 2 * pair + hh
                            last = dve.tensor_reduce(mx0[:, qb, h:h + 1], ps[:, bk, col:col + (qb + 1) * P],
                                                     X, ALU.max)
                    last.then_inc(mx1_done.sem, 1)

                def negate(part):
                    dve.wait_ge(mx1_done.sem, mx1_done.at(b, ROWS_HALF * (part + 1)))
                    q = slice(8 * part, 8 * part + 8)
                    dve.tensor_scalar(nm[:, :, q], mx0[:, :, q], -1.0, None, ALU.mult).then_inc(nm_ready.sem, 1)

                for pair in range(H // 4):
                    for u in range(5):
                        unit_max(5 * pair + u)
                    yield "rows"
                negate(0)
                yield "end"
                step(dve.tensor_copy(xm[:, :, :], x[:, :, :]))
                for h in range(H + 2):
                    if h == H + 1:
                        take_x()
                    for n in units_beside(h)[0:2]:
                        unit_max(n)
                    if h >= 2:
                        k = h - 2
                        dve.wait_ge(pv1.sem, pv1.at(b, k + 1))
                        src = ps[:, 6, 0:260].rearrange("p (t d) -> p t d", t=T)
                        step(dve.reciprocal(r1[:, k % 2, :], src[:, :, HD1]))
                        dve.tensor_tensor(ao[:, :, k * HD1:(k + 1) * HD1], src[:, :, 0:HD1],
                                          r1[:, k % 2, :].unsqueeze(2).to_broadcast([P, T, HD1]), ALU.mult)\
                            .then_inc(ao_done.sem, 1)
                    for n in units_beside(h)[2:]:
                        unit_max(n)
                    if h == 6:
                        negate(1)
                    if h < H:
                        dve.wait_ge(e1.sem, e1.at(b, 4 * h + 4))
                        dve.tensor_tensor(p1_parts[h % 3][:, 1, :], p1, p1_parts[h % 3][:, 0, :], ALU.subtract)\
                            .then_inc(p1_lo.sem, 1)
                dve.wait_ge(y_ps.sem, y_ps.at(b, 3))
                step(dve.tensor_copy(y[:, :, :], rows(7)))
                variance(y)
                wait_rstd()
                step(normalise(y, y, mv, rstd))
                step(dve.tensor_tensor(xm[:, :, :], xm[:, :, :], y[:, :, :], ALU.add))
                assert step_no[0] == VEC_STEPS, step_no[0]

            def experts(b):
                ring, first_bank, gact = beside(b)
                step_no = [0]

                def step(i):
                    step_no[0] += 1
                    i.then_inc(mvec.sem, 1)
                    dve.wait_ge(mvec.sem, mvec.at(b, step_no[0]))

                def tok_bc(a):
                    return a.unsqueeze(2).to_broadcast([P, T, NE])

                row_stats(xm, bstm, mvm, vem, step).then_inc(mvar_ready.sem, 1)
                dve.wait_ge(mrstd_ready.sem, mrstd_ready.at(b, 1))
                dve.wait_ge(x_out_free.sem, x_out_free.at(b, 1))
                normalise(em, xm, mvm, rstdm).then_inc(em_ready.sem, 1)
                yield
                yield
                dve.wait_ge(xh_hi.sem, xh_hi.at(b, 1))
                dve.tensor_tensor(xh[:, 1, :], xmT, xh[:, 0, :], ALU.subtract).then_inc(xh_lo.sem, 1)
                dve.wait_ge(lg_ps.sem, lg_ps.at(b, 1))
                lg = ps[:, 6, 0:T * NE].rearrange("p (t e) -> p t e", t=T)
                step(dve.tensor_reduce(r4[:, :], lg, X, ALU.max))
                dve.tensor_tensor(pr[:, :, :], lg, tok_bc(r4[:, :]), ALU.subtract).then_inc(lg_max.sem, 1)
                yield
                yield

                def probabilities():
                    dve.wait_ge(lg_exp.sem, lg_exp.at(b, 1))
                    step(dve.tensor_reduce(r4[:, :], pr[:, :, :], X, ALU.add))
                    step(dve.reciprocal(r4[:, :], r4[:, :]))
                    step(dve.tensor_tensor(pr[:, :, :], pr[:, :, :], tok_bc(r4[:, :]), ALU.mult))

                def compare():
                    for t in range(T):
                        other = pr[:, t, :].unsqueeze(1).to_broadcast([P, NE, NE])
                        mine = pr[:, t, :].unsqueeze(2).to_broadcast([P, NE, NE])
                        dve.tensor_tensor(cmp1[:, t], other, mine, ALU.is_gt)
                        last = dve.tensor_tensor(cmp2[:, t], other, mine, ALU.is_equal)
                    step(last)

                def ranks():
                    tri = c["tri"][:, :].unsqueeze(1).to_broadcast([P, T, NE * NE])
                    step(dve.tensor_tensor(cmp2[:, :, :, :].rearrange("p t a e -> p t (a e)"),
                                           cmp2[:, :, :, :].rearrange("p t a e -> p t (a e)"), tri, ALU.mult))
                    step(dve.tensor_tensor(cmp1[:, :, :, :], cmp1[:, :, :, :], cmp2[:, :, :, :], ALU.add))

                def weights():
                    step(dve.tensor_reduce(comb[:, :, :], cmp1[:, :, :, :], X, ALU.add))
                    step(dve.scalar_tensor_tensor(out=comb[:, :, :], in0=comb[:, :, :], scalar=2.0, in1=pr[:, :, :],
                                                  op0=ALU.is_lt, op1=ALU.mult))
                    step(dve.tensor_reduce(r4[:, :], comb[:, :, :], X, ALU.add))
                    step(dve.reciprocal(r4[:, :], r4[:, :]))
                    step(dve.tensor_tensor(comb[:, :, :], comb[:, :, :], tok_bc(r4[:, :]), ALU.mult))

                def product(k):
                    n, half = divmod(k, 2)
                    if n >= FC and half == 0:
                        dve.wait_ge(dn_ps.sem, dn_ps.at(b, n - FC + 1))
                    dve.wait_ge(gelu_done.sem, gelu_done.at(b, k + 1))
                    dve.tensor_tensor(hT1[:, n % FC, 256 * half:256 * half + 256], gact[:, k % ring, :],
                                      ps[:, first_bank + k % ring, 256:512], ALU.mult).then_inc(hact.sem, 1)

                def combine(e):
                    dve.wait_ge(dn_ps.sem, dn_ps.at(b, FC * (e + 1)))
                    if e:
                        dve.wait_ge(dn_read.sem, dn_read.at(b, e))
                    for t in range(T):
                        o = ps[:, 7, t * P:(t + 1) * P]
                        if e == 0:
                            last = dve.tensor_scalar(em[:, t, :], o, comb[:, t, e:e + 1], None, ALU.mult)
                        else:
                            last = dve.scalar_tensor_tensor(out=em[:, t, :], in0=o, scalar=comb[:, t, e:e + 1],
                                                            in1=em[:, t, :], op0=ALU.mult, op1=ALU.add)
                    last.then_inc(dn_read.sem, 1)

                for k in range(HALVES + 2):
                    if 1 <= k <= HALVES:
                        product(k - 1)
                    if k in ROUTER:
                        (probabilities, compare, ranks, weights)[ROUTER.index(k)]()
                    if k >= 10 and (k - 10) % 8 == 0:
                        combine((k - 10) // 8)
                    yield
                combine(NE - 1)
                dve.wait_ge(dn_read.sem, dn_read.at(b, NE))
                row_stats(em, bstm, mvm, vem, step).then_inc(mvar_ready.sem, 1)
                yield
                dve.wait_ge(mrstd_ready.sem, mrstd_ready.at(b, 2))
                step(normalise(em, em, mvm, rstdm))
                dve.tensor_tensor(em[:, :, :], xm[:, :, :], em[:, :, :], ALU.add).then_inc(x_final.sem, 1)
                dve.wait_ge(x_final.sem, x_final.at(b, 1))
                assert step_no[0] == MVEC_STEPS, step_no[0]
                yield

            drive(dve, layers, experts)


def constants():
    i = np.arange(P)
    small = np.zeros((P, 88), np.float32)
    small[:, 0:4] = (i[:, None] % 32) // 8 == np.arange(4)
    small[:LD, 4:8] = i[:LD, None] // 8 == np.arange(4)
    col = np.arange(2 * LD)
    small[:, 8:72] = (col[None, :] % LD) // LHD == 2 * (col[None, :] // LD) + i[:, None] // 64
    small[:, 72:] = -0.5
    a, k = i[:, None], i[None, :]
    masks = np.zeros((P, 768), np.float32)
    masks[:, 0:128] = np.where(k >= a, 0, NEG)
    masks[:, 128:256] = np.where(k < a, 0, NEG)
    masks[:, 256:384] = np.where(k > a, 0, NEG)
    masks[:, 384:512] = np.where(k <= a, 0, NEG)
    masks[:, 512:640] = np.where(k <= a, 0, NEG1)
    masks[:, 640:768] = np.where(k >= a, 0, NEG1)
    tok = (np.arange(T)[None, :] * P + i[:, None])
    lmask = np.where(np.arange(NLAT)[None, None, :] < (tok // CHUNK)[:, :, None], 0, NEG).astype(np.float32)
    inv = (1.0 / np.float32(10000.0) ** (np.arange(0, HD1, 2, dtype=np.float32) / np.float32(HD1))).astype(np.float32)
    fr = (np.arange(S, dtype=np.float32)[:, None] * inv).astype(np.float32)
    cos, sin = np.cos(fr), np.sin(fr)
    cs = np.stack([np.concatenate([cos, cos], 1), np.concatenate([-sin, sin], 1)])
    cs = cs.reshape(2, T, P, HD1).transpose(2, 0, 1, 3)
    e = np.arange(NE)
    tri = np.broadcast_to((e[None, :] < e[:, None]).reshape(1, -1), (P, NE * NE))
    return {"ident_f": np.eye(P, dtype=np.float32), "small": small,
            "masks": masks, "lmask": lmask, "cs": cs.astype(np.float32),
            "tri": tri.astype(np.float32)}


def kernel(**inputs):
    import concourse.bacc as bacc
    from concourse.bass_utils import run_bass_kernel_spmd as run

    w = {k: np.asarray(v) for k, v in inputs.items()}

    def rows(v):
        return np.broadcast_to(v.reshape(1, -1), (P, v.size))

    def slots(m):
        return np.concatenate([np.tile(m[..., 32 * g:32 * g + 32], 4) for g in range(4)], -1)

    qkv, qb = w["L0_attn_qkv_w"], w["L0_attn_qkv_b"]
    bq, bk = slots(qb[0:D]).reshape(4, P), slots(qb[D:2 * D]).reshape(4, P)
    a = dict(constants())
    a.update({
        "x": w["L0_attn_x"].reshape(NSEQ * S, D),
        "wqrep": slots(qkv[:, 0:D]), "wkrep": slots(qkv[:, D:2 * D]), "wv": qkv[:, 2 * D:],
        "bqk": np.stack([bq, bk], 1).reshape(8, P).T, "bv": rows(qb[2 * D:]),
        "rq_w": w["L0_attn_rq_w"], "rq_b": w["L0_attn_rq_b"].reshape(LD, 1),
        "rkv_w": w["L0_attn_rkv_w"], "rk_b": w["L0_attn_rkv_b"][:LD].reshape(LD, 1),
        "rv_b": rows(w["L0_attn_rkv_b"][LD:]),
        "rout_w": w["L0_attn_rout_w"], "rout_b": rows(w["L0_attn_rout_b"]),
        "out_w": w["L0_attn_out_w"], "out_b": rows(w["L0_attn_out_b"]),
        "glr": np.broadcast_to(np.stack([w["L0_attn_gl_w"].ravel(), w["L0_attn_gr_w"].ravel()])[None],
                               (P, 2, HD0)),
        "w1": w["L0_ffn_W1"].T, "b1": w["L0_ffn_b1"].reshape(FC, P).T,
        "w2": w["L0_ffn_W2"].T.reshape(FC, P, D).transpose(1, 0, 2).reshape(P, FC * D),
        "b2": rows(w["L0_ffn_b2"]),
        "qkn": np.broadcast_to(np.stack([w["L1_attn_q_norm_w"], w["L1_attn_k_norm_w"]])[None], (P, 2, HD1)),
        "wqkv1": w["L1_attn_wqkv"].T,
        "wo1": w["L1_attn_wo"].T.reshape(8, P, D).transpose(1, 0, 2).reshape(P, 8 * D),
        "gate_w": w["L1_ffn_gate_w"].T,
        "gu": w["L1_ffn_gate_up_w"].transpose(2, 0, 1),
        "down": w["L1_ffn_down_w"].transpose(2, 0, 1).reshape(FC, P, NE, D).transpose(1, 2, 0, 3),
    })
    nc = bacc.Bacc("TRN2", target_bir_lowering=False, num_devices=1)
    arrays, ins = {}, {}
    for name, v in a.items():
        v = np.ascontiguousarray(v)
        arrays["in_" + name] = v
        ins[name] = nc.dram_tensor("in_" + name, v.shape, mybir.dt.from_np(v.dtype), kind="ExternalInput").ap()
    out = nc.dram_tensor("out_0", (NSEQ * S, D), F32, kind="ExternalOutput").ap()
    build(nc, ins, out)
    r = run(nc, [arrays], core_ids=[0])
    return r.results[0]["out_0"].reshape(NSEQ, S, D)
```
